# Optimizing a Trainium2 kernel written in Bass

```python
import numpy as np
import jax
import jax.numpy as jnp

def _softmax(x, axis=-1):
    return jax.nn.softmax(x, axis=axis)

def _gelu(x):
    return jax.nn.gelu(x, approximate=True)

def _silu(x):
    return jax.nn.silu(x)

def _sigmoid(x):
    return jax.nn.sigmoid(x)

def _layernorm(x, axis=-1, eps=1e-05):
    m = jnp.mean(x, axis=axis, keepdims=True)
    v = jnp.var(x, axis=axis, keepdims=True)
    return (x - m) / jnp.sqrt(v + eps)

def _scatter_add(tgt, idx, src, axis=0):
    return tgt.at[idx].add(src)

def _segment_sum(src, seg, n):
    return jax.ops.segment_sum(src, seg, n)
kernel_name = 'mk_gnn_ffn_d1_gnn_r8_116ae7'

def setup_inputs(seed: int=0):
    np.random.seed(seed)
    _w = jnp.asarray

    def _rec_inputs():
        import jax
        import jax.numpy as jnp
        _gk = jax.random.key(seed)
        x = -0.0003713 + 1 * jax.random.normal(jax.random.fold_in(_gk, 1), (6250, 256), jnp.float32)
        src = jax.random.randint(jax.random.fold_in(_gk, 2), (100000,), 0, 6250, jnp.int32)
        dst = jnp.minimum((6250 * jax.random.uniform(jax.random.fold_in(_gk, 3), (100000,)) ** 2.0).astype(jnp.int32), 49999)
        _o = jnp.argsort(dst, stable=True)
        src = src[_o]
        dst = dst[_o]
        edge_attr_3 = -1.09012e-05 + 0.99985 * jax.random.normal(jax.random.fold_in(_gk, 11), (100000, 3), jnp.float32)
        return (x, src, dst, edge_attr_3)
    x, src, dst, edge_attr_3 = _rec_inputs()

    def _L0_gnn_setup():
        import jax, jax.numpy as jnp
        import numpy as np
        N = 6250
        E = 50000
        IN = 256
        H = 8
        D = 32
        EF = 3
        key = jax.random.key(seed)
        ks = jax.random.split(key, 8)
        x = jax.random.normal(ks[0], (N, IN), dtype=jnp.float32)
        edge_index = jax.random.randint(ks[1], (2, E), 0, N, dtype=jnp.int64)
        edge_attr = jax.random.normal(ks[2], (E, EF), dtype=jnp.float32)
        W = jax.random.normal(ks[3], (H * D, IN), dtype=jnp.float32) * np.float32(np.sqrt(2.0 / (IN + H * D)))
        a_src = jax.random.normal(ks[4], (H, D), dtype=jnp.float32) * np.float32(np.sqrt(2.0 / (H + D)))
        a_dst = jax.random.normal(ks[5], (H, D), dtype=jnp.float32) * np.float32(np.sqrt(2.0 / (H + D)))
        edge_W = jax.random.normal(ks[6], (H * D, EF), dtype=jnp.float32) * np.float32(np.sqrt(2.0 / (EF + H * D)))
        edge_b = jnp.zeros((H * D,), dtype=jnp.float32)
        bias = jnp.zeros((H * D,), dtype=jnp.float32)
        return {'x': x, 'W': W, 'a_src': a_src, 'a_dst': a_dst, 'edge_W': edge_W, 'edge_b': edge_b, 'bias': bias, 'edge_attr': edge_attr, 'edge_index': edge_index}
    _L0_gnn_all = _L0_gnn_setup()
    _L0_gnn_in = {k: v for k, v in _L0_gnn_all.items() if k in ('W', 'a_src', 'a_dst', 'edge_W', 'edge_b', 'bias')}
    del _L0_gnn_all

    def _L0_ffn_setup():
        import jax, jax.numpy as jnp
        import numpy as np
        TOP_K = 2
        LN_EPS = 1e-05
        key = jax.random.key(seed)
        ks = jax.random.split(key, 8)
        B, S, D, E, H = (16, 1024, 256, 8, 1024)
        x = jax.random.normal(ks[0], (B, S, D), dtype=jnp.float32)
        Wr = jax.random.normal(ks[1], (D, E), dtype=jnp.float32) * 0.1
        br = jnp.zeros((E,), dtype=jnp.float32)
        ln_g = jnp.ones((E, D), dtype=jnp.float32)
        ln_b = jnp.zeros((E, D), dtype=jnp.float32)
        W1 = jax.random.normal(ks[2], (E, D, H), dtype=jnp.float32) * (1.0 / np.sqrt(D))
        b1 = jnp.zeros((E, H), dtype=jnp.float32)
        W2 = jax.random.normal(ks[3], (E, H, D), dtype=jnp.float32) * (1.0 / np.sqrt(H))
        b2 = jnp.zeros((E, D), dtype=jnp.float32)
        return {'x': x, 'Wr': Wr, 'br': br, 'ln_g': ln_g, 'ln_b': ln_b, 'W1': W1, 'b1': b1, 'W2': W2, 'b2': b2}
    _L0_ffn_all = _L0_ffn_setup()
    _L0_ffn_in = {k: v for k, v in _L0_ffn_all.items() if k in ('Wr', 'br', 'ln_g', 'ln_b', 'W1', 'b1', 'W2', 'b2')}
    del _L0_ffn_all
    return {'x': x, 'src': src, 'dst': dst, 'edge_attr_3': edge_attr_3, 'L0_gnn_W': _L0_gnn_in['W'], 'L0_gnn_a_src': _L0_gnn_in['a_src'], 'L0_gnn_a_dst': _L0_gnn_in['a_dst'], 'L0_gnn_edge_W': _L0_gnn_in['edge_W'], 'L0_gnn_edge_b': _L0_gnn_in['edge_b'], 'L0_gnn_bias': _L0_gnn_in['bias'], 'L0_ffn_Wr': _L0_ffn_in['Wr'], 'L0_ffn_br': _L0_ffn_in['br'], 'L0_ffn_ln_g': _L0_ffn_in['ln_g'], 'L0_ffn_ln_b': _L0_ffn_in['ln_b'], 'L0_ffn_W1': _L0_ffn_in['W1'], 'L0_ffn_b1': _L0_ffn_in['b1'], 'L0_ffn_W2': _L0_ffn_in['W2'], 'L0_ffn_b2': _L0_ffn_in['b2']}

def reference(x, src, dst, edge_attr_3, L0_gnn_W, L0_gnn_a_src, L0_gnn_a_dst, L0_gnn_edge_W, L0_gnn_edge_b, L0_gnn_bias, L0_ffn_Wr, L0_ffn_br, L0_ffn_ln_g, L0_ffn_ln_b, L0_ffn_W1, L0_ffn_b1, L0_ffn_W2, L0_ffn_b2):
    import jax
    import jax.numpy as jnp

    def _L0_gnn_ref(x, W, a_src, a_dst, edge_W, edge_b, bias, edge_attr, edge_index):
        import jax, jax.numpy as jnp
        import numpy as np
        N = 6250
        E = 50000
        IN = 256
        H = 8
        D = 32
        EF = 3
        n = x.shape[0]
        h = (x @ W.T).reshape(n, H, D)
        src, dst = (edge_index[0], edge_index[1])
        h_src = h[src]
        h_dst = h[dst]
        alpha = jnp.einsum('ehd,hd->eh', h_src, a_src) + jnp.einsum('ehd,hd->eh', h_dst, a_dst)
        enc = jax.nn.relu(edge_attr @ edge_W.T + edge_b).reshape(-1, H, D)
        alpha = alpha + jnp.sum(enc * h_dst, axis=-1)
        alpha = jnp.where(alpha >= 0, alpha, 0.2 * alpha)
        amax = jax.ops.segment_max(alpha, dst, num_segments=n)
        ex = jnp.exp(alpha - amax[dst])
        denom = jax.ops.segment_sum(ex, dst, num_segments=n)
        attn = ex / jnp.maximum(denom[dst], 1e-10)
        out = jax.ops.segment_sum(h_src * attn[..., None], dst, num_segments=n)
        return out.reshape(n, H * D) + bias

    def _L0_ffn_ref(x, Wr, br, ln_g, ln_b, W1, b1, W2, b2):
        import jax, jax.numpy as jnp
        import numpy as np
        TOP_K = 2
        LN_EPS = 1e-05
        B, S, D = x.shape
        N = B * S
        xt = x.reshape(N, D)
        logits = xt @ Wr + br
        probs = jax.nn.softmax(logits, axis=-1)
        top_p, top_idx = jax.lax.top_k(probs, TOP_K)
        weights = top_p / top_p.sum(axis=-1, keepdims=True)
        mu = xt.mean(axis=-1, keepdims=True)
        var = ((xt - mu) ** 2).mean(axis=-1, keepdims=True)
        xn = (xt - mu) * jax.lax.rsqrt(var + LN_EPS)
        xe = xn[None, :, :] * ln_g[:, None, :] + ln_b[:, None, :]
        h = jax.nn.gelu(jnp.einsum('end,edh->enh', xe, W1) + b1[:, None, :], approximate=False)
        y = jnp.einsum('enh,ehd->end', h, W2) + b2[:, None, :]
        y_tok = jnp.transpose(y, (1, 0, 2))
        sel = jnp.take_along_axis(y_tok, top_idx[:, :, None], axis=1)
        out = (weights[:, :, None] * sel).sum(axis=1)
        return out.reshape(B, S, D)
    edge_index = jnp.stack([src, dst])
    x = x + _L0_gnn_ref(_layernorm(x, axis=-1), L0_gnn_W, L0_gnn_a_src, L0_gnn_a_dst, L0_gnn_edge_W, L0_gnn_edge_b, L0_gnn_bias, edge_attr_3, edge_index)
    x = x + _L0_ffn_ref(_layernorm(x, axis=-1)[None], L0_ffn_Wr, L0_ffn_br, L0_ffn_ln_g, L0_ffn_ln_b, L0_ffn_W1, L0_ffn_b1, L0_ffn_W2, L0_ffn_b2)[0]
    return x

_drawn_inputs = setup_inputs


def setup_inputs(seed=0):
    import zlib

    import numpy as np

    out = dict(_drawn_inputs(seed))
    spreads = {'L0_gnn_edge_b': (0.0, 0.1),
     'L0_gnn_bias': (0.0, 0.1),
     'L0_ffn_br': (0.0, 0.1),
     'L0_ffn_ln_g': (1.0, 0.2),
     'L0_ffn_ln_b': (0.0, 0.1),
     'L0_ffn_b1': (0.0, 0.1),
     'L0_ffn_b2': (0.0, 0.1)}
    factors = {}
    for name, (base, spread) in spreads.items():
        noise = np.random.default_rng([zlib.crc32(name.encode()), seed]).standard_normal(out[name].shape)
        drawn = base * np.exp(spread * noise) if base else spread * noise
        out[name] = jnp.asarray(drawn.astype(out[name].dtype))
    for name, factor in factors.items():
        out[name] = (out[name] * factor).astype(out[name].dtype)
    return out
```

```python
from contextlib import ExitStack

import concourse.bass as bass
from concourse import mybir

F32 = mybir.dt.float32
I32 = mybir.dt.int32
ALU = mybir.AluOpType
ACT = mybir.ActivationFunctionType
AX = mybir.AxisListType
ds = bass.ds

P = 128
N, IN, H, D, EF, E = 6250, 256, 8, 32, 3, 100000
X, HID, TOPK = 8, 1024, 2
HD = H * D
KH = IN // P
HW = H * (D + 1)
HS = HW + H
J = -(-N // P)
NP = J * P
GT = 7
GROUPS = J // GT
CT = 16
SLOTS = -(-(-(-E // P) + J - 1) // CT) * CT
T = SLOTS - J + 1
CH = SLOTS // CT
EP = T * P
R = 8
TURNS = SLOTS // R
SG = -(-SLOTS // P)
MOE_TILES = (TOPK * NP + X * (P - 1)) // P
MOE_TILES += MOE_TILES % 2
XS_TILES = MOE_TILES + 2
LN_EPS = 1e-5
BIG = 1.5e38
FLAT = CH * P
CHAIN = SLOTS * 2
assert GROUPS * GT == J and TURNS * R == SLOTS and XS_TILES % 4 == 0

W1_AT = 0
W1_WORDS = KH * X * HID
W2_AT = W1_AT + W1_WORDS
W2_WORDS = HID // P * X * IN
B1_AT = W2_AT + W2_WORDS
B1_WORDS = X * HID
EX_AT = B1_AT + B1_WORDS
EX_WORDS = SLOTS * H
ARENA = EX_AT + EX_WORDS
LOGITS_AT = W2_AT + J * HW


class Chip:
    pass


def semaphores(nc, ctx, *names):
    return [ctx.enter_context(nc.semaphore(n)) for n in names]


def merge_stats(nc, dve, st, mv, turn, merged, var_made):
    nc.vector.tensor_tensor(mv[:, 0, :], st[:, :, 1], st[:, :, 4], ALU.add).then_inc(merged, 1)
    nc.vector.tensor_tensor(mv[:, 1, :], st[:, :, 1], st[:, :, 4], ALU.subtract).then_inc(merged, 1)
    nc.vector.tensor_tensor(mv[:, 2, :], st[:, :, 2], st[:, :, 5], ALU.add).then_inc(merged, 1)
    dve.wait_ge(merged, turn * 4 + 2)
    nc.vector.tensor_tensor(mv[:, 1, :], mv[:, 1, :], mv[:, 1, :], ALU.mult).then_inc(merged, 1)
    nc.vector.tensor_scalar(mv[:, 4, :], mv[:, 0, :], 0.5, None, ALU.mult)
    dve.wait_ge(merged, turn * 4 + 4)
    nc.vector.scalar_tensor_tensor(mv[:, 3, :], mv[:, 1, :], IN / 4.0, mv[:, 2, :], ALU.mult, ALU.add).then_inc(var_made, 1)


def prepare(nc, c, d):
    with ExitStack() as ctx:
        (consts_made, zeros_made, w_loaded, small_loaded, hi_loaded, hi_row_made, val_in_psum, counted, t_made, t_stored,
         t_loaded, dve_step, wa_made, wa_copied, x_loaded, stats, merged, var_made, sd_made, rs_made, xn_made,
         xT_made, xT_copied, h_made, h_copied, rows_staged, rows_stored, xs_zeroed, ew_zeroed) = semaphores(
            nc, ctx, "p_consts", "p_zeros", "p_w", "p_small", "p_hi", "p_hirow", "p_val", "p_counted", "p_tmade", "p_tstored",
            "p_tloaded", "p_step", "p_wa", "p_wacopied", "p_x", "p_stats", "p_merged", "p_var", "p_sd", "p_rs", "p_xn",
            "p_xT", "p_xTcopied", "p_h", "p_hcopied", "p_staged", "p_stored", "p_xszero", "p_ewzero")
        (tiles_gathered, rel_made, src_made, turned, turned_back, lists_stored, step2) = semaphores(
            nc, ctx, "p_tilegat", "p_rel", "p_srcf", "p_turned", "p_back", "p_lists", "p_step2")
        def work(at, *shape):
            n = 1
            for s in shape:
                n *= s
            ap = c.arena[:, EX_AT + at:EX_AT + at + n]
            return ap if len(shape) == 1 else ap.rearrange("p (a b) -> p a b", b=shape[-1])

        xg = work(0, GT, IN)
        stage = work(GT * IN, GT, HW)
        xT = work(GT * (IN + HW), 2, IN)
        stage_s = work(GT * (IN + HW) + 2 * IN, GT, H)
        w_nat = c.arena[:, W2_AT:W2_AT + KH * IN].rearrange("p (k i) -> p k i", k=KH)
        a_bd = c.arena[:, W2_AT + 512:W2_AT + 512 + KH * 2 * H].rearrange("p (k h) -> p k h", k=KH)
        hi_row = c.arena[0:1, W2_AT + 1024:W2_AT + 1024 + T]
        hi_tile = c.arena[0:1, W2_AT + 2048:W2_AT + 2048 + T]
        j_col = c.arena[:, W2_AT + 6400:W2_AT + 6400 + SG]
        j_col_i = c.arena[:, W2_AT + 6500:W2_AT + 6500 + SG]
        iota_t = c.arena[0:1, W2_AT + 3072:W2_AT + 3072 + T]
        val_row = c.arena[0:1, W2_AT + 4096:W2_AT + 4096 + T]
        below = c.arena[:, W2_AT + 5120:W2_AT + 5120 + T]
        slot_id = c.arena[:, W2_AT + 6144:W2_AT + 6144 + SG]
        t_col = c.arena[:, W2_AT + 6200:W2_AT + 6200 + SG]
        t_col_i = c.arena[:, W2_AT + 6300:W2_AT + 6300 + SG]
        zeros = c.arena[:, W2_AT + 8192:W2_AT + 8192 + 4 * IN]
        st = c.arena[:, W2_AT + 9300:W2_AT + 9300 + GT * 6].rearrange("p (k s) -> p k s", k=GT)
        mv = c.arena[:, W2_AT + 9400:W2_AT + 9400 + 5 * GT].rearrange("p (s k) -> p s k", k=GT)
        sd = c.arena[:, W2_AT + 9500:W2_AT + 9500 + GT]
        rs = c.arena[:, W2_AT + 9600:W2_AT + 9600 + GT]
        rhs_h = c.arena[:, W2_AT + 9728:W2_AT + 9728 + KH * HS].rearrange("p (k n) -> p k n", k=KH)
        h_all = c.arena[:, W1_AT:W1_AT + J * HW]
        at = B1_AT

        def slot_rows(words):
            nonlocal at
            at += SG * words
            return c.arena[:, at - SG * words:at].rearrange("p (g e) -> p g e", g=SG)

        dst_rows, src_rows, rel, src_f, ea_rows = (slot_rows(n) for n in (P, P, P, P, (EF + 1) * P))
        assert at <= B1_AT + B1_WORDS
        xn = c.arena[:, W2_AT + 10496:W2_AT + 10496 + GT * IN].rearrange("p (k i) -> p k i", k=GT)
        eps = c.eps
        ps = c.psum
        block = ctx.enter_context(nc.Block())

        @block.gpsimd
        def _(pool):
            ia = dict(allow_small_or_imprecise_dtypes=True)
            pool.iota(c.iota_row[:, :], [[1, P]], base=0, channel_multiplier=0, **ia).then_inc(consts_made, 1)
            pool.iota(c.iota_p[:, :], [[0, 1]], base=0, channel_multiplier=1, **ia).then_inc(consts_made, 1)
            pool.iota(iota_t, [[1, T]], base=0, channel_multiplier=0, **ia).then_inc(consts_made, 1)
            pool.iota(slot_id, [[P, SG]], base=0, channel_multiplier=1, **ia).then_inc(consts_made, 1)
            pool.memset(c.ones[:, :], 1.0).then_inc(consts_made, 1)
            pool.memset(eps[:, :], LN_EPS).then_inc(consts_made, 1)
            pool.memset(stage[:, :, :], 1.0).then_inc(consts_made, 1)
            pool.wait_ge(t_made, 2)
            for g in range(SG):
                for rows, table in ((dst_rows, d.dst_rows), (src_rows, d.src_rows), (ea_rows, d.ea_rows)):
                    rows = rows[:, g, :] if rows is ea_rows else rows[:, g, :].bitcast(I32)
                    pool.indirect_dma_start(rows, None, table, bass.IndirectOffsetOnAxis(ap=t_col_i[:, g:g + 1].bitcast(I32), axis=0)
                                            ).then_inc(tiles_gathered, 16)

        @block.sync
        def _(sp):
            sp.dma_start(w_nat, d.W.rearrange("(k p) i -> p k i", p=P)).then_inc(w_loaded, 16)
            sp.dma_start(a_bd, d.a_bd.rearrange("(k p) h -> p k h", p=P)).then_inc(w_loaded, 16)
            for k in range(KH):
                sp.dma_start(rhs_h[:, k, 0:HW].rearrange("p (h f) -> p h f", f=D + 1)[:, :, 0:D],
                             d.WT[k * P:(k + 1) * P, :].rearrange("p (h f) -> p h f", f=D)).then_inc(w_loaded, 16)
            with nc.allow_non_contiguous_dma(reason="last target of each edge tile"):
                sp.dma_start(hi_row.bitcast(I32), d.dst_rows.rearrange("t e -> e t")[P - 1:P, :]).then_inc(hi_loaded, 16)
            sp.wait_ge(ew_zeroed, 1)
            sp.dma_start(c.ew[0:EF + 1, :], d.ew).then_inc(small_loaded, 16)
            sp.dma_start(c.gnn_bias[:, :], d.gnn_bias.partition_broadcast(P)).then_inc(small_loaded, 16)
            sp.dma_start(c.wr[:, :, :], d.Wr.rearrange("(k p) e -> p k e", p=P)).then_inc(small_loaded, 16)
            sp.dma_start(c.br[:, :], d.br.partition_broadcast(P)).then_inc(small_loaded, 16)
            sp.dma_start(c.ln_g[:, :, :], d.ln_gT.rearrange("(k p) e -> p k e", p=P)).then_inc(small_loaded, 16)
            sp.dma_start(c.ln_b[:, :, :], d.ln_bT.rearrange("(k p) e -> p k e", p=P)).then_inc(small_loaded, 16)
            sp.wait_ge(zeros_made, 1)
            for q in range(XS_TILES // 4):
                sp.dma_start(d.xs[q * 4 * P:(q + 1) * 4 * P, :].rearrange("(p r) i -> p (r i)", r=4), zeros).then_inc(xs_zeroed, 16)
            sp.wait_ge(t_made, 2)
            with nc.allow_non_contiguous_dma(reason="column to row"):
                sp.dma_start(d.slot_j.rearrange("(g p) -> p g", p=P), j_col_i.bitcast(I32)).then_inc(t_stored, 16)
            sp.wait_ge(t_stored, 16)
            sp.dma_start(c.slot_j[:, :], d.slot_j.rearrange("(a s) -> a s", a=1)).then_inc(t_loaded, 16)
            with sp.Fori(0, GROUPS) as i:
                sp.wait_ge(xn_made, i * GT + GT)
                sp.dma_start(xg, d.x[ds(i * (GT * P), GT * P), :].rearrange("(k p) i -> p k i", p=P)).then_inc(x_loaded, 16)
                sp.wait_ge(rows_staged, i * (2 * GT) + (2 * GT + 4))
                sp.dma_start(d.h_tab[ds(i * (GT * P), GT * P), :].rearrange("(k p) i -> p k i", p=P), stage).then_inc(rows_stored, 16)
                sp.dma_start(d.s_tab[ds(i * (GT * P), GT * P), :].rearrange("(k p) i -> p k i", p=P), stage_s).then_inc(rows_stored, 16)
            sp.wait_ge(tiles_gathered, 16 * 3 * SG)
            for g in range(SG):
                sp.dma_start(d.ea_slots[:, g * P:(g + 1) * P, :].rearrange("f p e -> p f e"),
                             ea_rows[:, g, :].rearrange("p (f e) -> p f e", f=EF + 1)).then_inc(lists_stored, 16)
            sp.wait_ge(rel_made, 1)
            sp.dma_start(d.rel.rearrange("(g p) e -> p g e", p=P), rel).then_inc(lists_stored, 16)
            sp.wait_ge(lists_stored, 16 * (SG + 1))
            sp.wait_ge(rows_stored, 32 * GROUPS + 32)
            sp.wait_ge(t_loaded, 16)
            sp.wait_ge(small_loaded, 16 * 6)
            sp.wait_ge(xs_zeroed, 16 * (XS_TILES // 4))

        @block.scalar
        def _(act):
            with act.Fori(0, GROUPS) as i:
                act.wait_ge(var_made, i + 1)
                nc.scalar.activation(sd, mv[:, 3, :], ACT.Sqrt, bias=eps[:, :], scale=1.0 / IN).then_inc(sd_made, 1)
                for k in range(GT):
                    act.wait_ge(xT_made, i * GT + (k + 1))
                    act.wait_ge(h_made, i * GT + (k + 1))
                    nc.scalar.copy(xT[:, k % 2, :], ps[:, k % 2, 0:IN]).then_inc(xT_copied, 1)
                    act.wait_ge(rows_staged, i * (2 * GT) + (2 * k + 6))
                    nc.scalar.copy(h_all[:, ds((i * GT + k) * HW, HW)], ps[:, 2 + k % 2, 0:HW]).then_inc(h_copied, 1)

        @block.tensor
        def _(pe):
            pe.sem_inc(h_made, 2)
            pe.wait_ge(w_loaded, 16 * (2 + KH))
            for k in range(KH):
                for m in range(KH):
                    last = nc.tensor.matmul(ps[:, 4, k * 2 * H:(k + 1) * 2 * H], w_nat[:, m, k * P:(k + 1) * P], a_bd[:, m, :],
                                            start=(m == 0), stop=(m == KH - 1))
            last.then_inc(wa_made, 1)
            pe.wait_ge(hi_row_made, 1)
            for b in range(2):
                last = nc.tensor.matmul(ps[:, 5 + b, 0:T // 2], c.ones[0:1, 0:P], val_row[:, b * (T // 2):(b + 1) * (T // 2)],
                                        start=True, stop=True)
            last.then_inc(val_in_psum, 1)
            pe.wait_ge(wa_copied, 2)
            pe.wait_ge(c.consts_ready, 2)
            with pe.Fori(0, GROUPS) as i:
                for k in range(GT):
                    pe.wait_ge(xn_made, i * GT + (GT + k + 1))
                    pe.wait_ge(xT_copied, i * GT + (k + 1))
                    for m in range(KH):
                        last = nc.tensor.transpose(ps[:, k % 2, m * P:(m + 1) * P], xn[:, k, m * P:(m + 1) * P], c.ident[:, :])
                    last.then_inc(xT_made, 1)
                    pe.wait_ge(xT_copied, i * GT + (k + 3))
                    pe.wait_ge(h_copied, i * GT + (k + 1))
                    pe.wait_ge(rows_staged, i * (2 * GT) + (2 * k + 2))
                    for m in range(KH):
                        last = nc.tensor.matmul(ps[:, 2 + k % 2, 0:HS], xT[:, k % 2, m * P:(m + 1) * P], rhs_h[:, m, :],
                                                start=(m == 0), stop=(m == KH - 1))
                    last.then_inc(h_made, 1)
            for n, (rows, made) in enumerate(((rel, rel_made), (src_f, src_made))):
                pe.wait_ge(made, 1)
                for g in range(SG):
                    if g in (0, 4) and n:
                        pe.wait_ge(turned_back, g // 4 + 1)
                    last = nc.tensor.transpose(ps[:, 6 + g // 4, g % 4 * P:(g % 4 + 1) * P], rows[:, g, :], c.ident[:, :])
                    if g in (3, SG - 1):
                        last.then_inc(turned, 1)

        @block.vector
        def _(dve):
            dve.sem_inc(xn_made, GT)
            dve.sem_inc(xT_copied, 2)
            dve.sem_inc(h_copied, 2)
            dve.sem_inc(rows_staged, 4)
            dve.sem_inc(rows_stored, 32)
            dve.sem_inc(rs_made, 1)
            nc.vector.memset(c.ew[:, :], 0.0).then_inc(ew_zeroed, 1)
            nc.vector.memset(zeros, 0.0).then_inc(zeros_made, 1)
            dve.wait_ge(consts_made, 7)
            nc.vector.tensor_scalar(c.ident[:, :], c.iota_row[:, :], c.iota_p[:, :], None, ALU.is_equal).then_inc(c.consts_ready, 1)
            nc.vector.tensor_scalar(c.tri[:, :], c.iota_row[:, :], c.iota_p[:, :], None, ALU.is_gt).then_inc(c.consts_ready, 1)
            dve.wait_ge(wa_made, 1)
            wa = ps[:, 4, 0:KH * 2 * H].rearrange("p (k s h) -> p k s h", k=KH, s=2)
            nc.vector.tensor_copy(rhs_h[:, :, HW:HS], wa[:, :, 0, :]).then_inc(wa_copied, 1)
            nc.vector.tensor_copy(rhs_h[:, :, D:HW:D + 1], wa[:, :, 1, :]).then_inc(wa_copied, 1)
            dve.wait_ge(hi_loaded, 16)
            nc.vector.tensor_scalar(hi_tile.bitcast(I32), hi_row.bitcast(I32), 7, None, ALU.logical_shift_right).then_inc(dve_step, 1)
            dve.wait_ge(dve_step, 1)
            nc.vector.tensor_tensor(val_row, hi_tile.bitcast(I32), iota_t, ALU.add).then_inc(hi_row_made, 1)
            dve.wait_ge(val_in_psum, 1)
            for g in range(SG):
                if g:
                    dve.wait_ge(counted, g)
                nc.vector.tensor_scalar(below.rearrange("p (b t) -> p b t", b=2), ps[:, 5:7, 0:T // 2], slot_id[:, g:g + 1], None,
                                        ALU.is_lt).then_inc(dve_step, 1)
                dve.wait_ge(dve_step, 2 + g)
                nc.vector.tensor_reduce(t_col[:, g:g + 1], below, AX.X, ALU.add).then_inc(counted, 1)
            dve.wait_ge(counted, SG)
            nc.vector.tensor_scalar(t_col, t_col, float(T - 1), None, ALU.min).then_inc(step2, 1)
            dve.wait_ge(step2, 1)
            nc.vector.tensor_tensor(j_col, slot_id, t_col, ALU.subtract).then_inc(step2, 1)
            nc.vector.tensor_copy(t_col_i.bitcast(I32), t_col).then_inc(t_made, 1)
            dve.wait_ge(step2, 2)
            nc.vector.tensor_scalar(j_col_i.bitcast(I32), j_col, float(HW), None, ALU.mult).then_inc(t_made, 1)
            nc.vector.tensor_scalar(j_col, j_col, float(P), None, ALU.mult).then_inc(step2, 1)
            with dve.Fori(0, GROUPS) as i:
                dve.wait_ge(x_loaded, i * 16 + 16)
                for k in range(GT):
                    nc.vector.bn_stats(st[:, k, :], xg[:, k, :]).then_inc(stats, 1)
                dve.wait_ge(stats, i * GT + GT)
                merge_stats(nc, dve, st, mv, i, merged, var_made)
                dve.wait_ge(sd_made, i + 1)
                nc.vector.reciprocal(rs, sd).then_inc(rs_made, 1)
                dve.wait_ge(rs_made, i + 2)
                for k in range(GT):
                    nc.vector.tensor_scalar(xn[:, k, :], xg[:, k, :], mv[:, 4, k:k + 1], rs[:, k:k + 1], ALU.subtract,
                                            ALU.mult).then_inc(xn_made, 1)
                dve.wait_ge(rows_stored, i * 32 + 32)
                for k in range(GT):
                    dve.wait_ge(h_made, i * GT + (k + 3))
                    nc.vector.tensor_copy(stage[:, k, :].rearrange("p (h f) -> p h f", f=D + 1)[:, :, 0:D],
                                          ps[:, 2 + k % 2, 0:HW].rearrange("p (h f) -> p h f", f=D + 1)[:, :, 0:D]).then_inc(rows_staged, 1)
                    nc.vector.tensor_copy(stage_s[:, k, :], ps[:, 2 + k % 2, HW:HS]).then_inc(rows_staged, 1)
            dve.wait_ge(tiles_gathered, 16 * 3 * SG)
            dve.wait_ge(step2, 3)
            nc.vector.tensor_tensor(rel, dst_rows.bitcast(I32), j_col.unsqueeze(2).to_broadcast([P, SG, P]), ALU.subtract).then_inc(rel_made, 1)
            nc.vector.tensor_copy(src_f, src_rows.bitcast(I32)).then_inc(src_made, 1)
            for n, cols in enumerate((c.rel, c.src)):
                for q in range(2):
                    dve.wait_ge(turned, 2 * n + q + 1)
                    slots = slice(q * 4 * P, min((q + 1) * 4 * P, SLOTS))
                    nc.vector.tensor_copy(cols[:, slots], ps[:, 6 + q, 0:slots.stop - slots.start]).then_inc(turned_back, 1)
            dve.wait_ge(turned_back, 4)


def load_words(nc, row, engine):
    _, values = nc.values_load_multi_w_load_instructions(
        row, engines=(engine,), min_val=0, max_val=(J - 1) * HW,
        skip_runtime_bounds_check_because="slot s has node tile s - t(s), from 0 to J - 1 as targets lie below N")
    return values


def score(nc, c, d):
    with ExitStack() as ctx:
        (prod_done, red_done, sum_done, relu_done, enc_done, hd_done, oht_done, gate_done, idx_copied) = semaphores(
            nc, ctx, "s_prod", "s_red", "s_sum", "s_relu", "s_enc", "s_hd", "s_oht", "s_gate", "s_idx")
        ea_loaded = semaphores(nc, ctx, "s_ea0", "s_ea1")
        rel_loaded = semaphores(nc, ctx, "s_rel0", "s_rel1")
        gathered = semaphores(nc, ctx, "s_gat0", "s_gat1")
        PR = R // 2

        a_all = c.arena[:, W2_AT:W2_AT + SLOTS * H]
        h_all = c.arena[:, W1_AT:W1_AT + J * HW]
        at = W2_AT + SLOTS * H

        def take(n):
            nonlocal at
            at += n
            assert at <= B1_AT
            return c.arena[:, at - n:at]

        renc = take(4 * HW).rearrange("p (b s n) -> p b s n", b=2, s=2)
        prod = take(4 * HW).rearrange("p (b s n) -> p b s n", b=2, s=2)
        red = take(2 * R * H).rearrange("p (b n) -> p b n", b=2)
        gat = take(2 * R * H).rearrange("p (b k n) -> p b k n", b=2, k=R)
        relb = c.arena[:, EX_AT:EX_AT + 2 * R * P].rearrange("p (b k e) -> p b k e", b=2, k=R)
        oht = c.arena[:, EX_AT + 2 * R * P:EX_AT + 4 * R * P].rearrange("p (b k e) -> p b k e", b=2, k=R)
        ea = c.arena[0:EF + 1, B1_AT:B1_AT + 2 * R * P].rearrange("p (b k e) -> p b k e", b=2, k=R)
        ps = c.psum
        block = ctx.enter_context(nc.Block())

        @block.sync
        def _(sp):
            sp.dma_start(relb[:, 0, :, :], d.rel[0:R, :].partition_broadcast(P)).then_inc(rel_loaded[0], 16)
            with sp.Fori(0, TURNS // 2) as i:
                for b in range(2):
                    sp.wait_ge(enc_done, i * (2 * PR) + (b + 1) * PR)
                    sp.dma_start(ea[:, b, :, :], d.ea_slots[:, ds(i * (2 * R) + b * R, R), :]).then_inc(ea_loaded[b], 16)
                    sp.wait_ge(oht_done, i * 2 + (b + 2))
                    sp.dma_start(relb[:, 1 - b, :, :], d.rel[ds(i * (2 * R) + (b + 1) * R, R), :].partition_broadcast(P)).then_inc(rel_loaded[1 - b], 16)

        @block.gpsimd
        def _(pool):
            pool.sem_inc(gate_done, 1)
            with pool.Fori(0, TURNS // 2) as i:
                for b in range(2):
                    pool.wait_ge(idx_copied, i * 2 + (b + 1))
                    pool.wait_ge(gate_done, i * 2 + (b + 1))
                    nc.gpsimd.tensor_tensor(c.gate[:, :], c.ones[0:1, 0:1], c.ones[0:1, 0:1], ALU.add).then_inc(gate_done, 1)
                    for k in range(R):
                        pool.indirect_dma_start(gat[:, b, k, :], None, d.s_tab[:, :],
                                                bass.IndirectOffsetOnAxis(ap=c.idx[:, b, k:k + 1], axis=0)).then_inc(gathered[b], 16)

        @block.scalar
        def _(act):
            act.sem_inc(relu_done, 2)
            with act.Fori(0, TURNS // 2) as i:
                for b in range(2):
                    act.wait_ge(sum_done, i * 2 + (b + 1))
                    nc.scalar.copy(c.idx[:, b, :], c.src[:, ds(i * (2 * R) + b * R, R)]).then_inc(idx_copied, 1)
                    for q in range(PR):
                        act.wait_ge(prod_done, i * (2 * PR) + (b * PR + q + 1))
                        act.wait_ge(enc_done, i * (2 * PR) + (2 * PR + b * PR + q + 1))
                        b0 = q % 2 * 2
                        nc.scalar.activation(renc[:, q % 2, :, :], ps[:, b0:b0 + 2, 0:HW], ACT.Relu).then_inc(relu_done, 1)

        @block.tensor
        def _(pe):
            pe.sem_inc(enc_done, 2 * PR)
            pe.sem_inc(hd_done, 2)
            with pe.Fori(0, TURNS // 2) as i:
                for b in range(2):
                    js = load_words(nc, c.slot_j[0:1, ds(i * (2 * R) + b * R, R)], mybir.EngineType.PE)
                    pe.wait_ge(ea_loaded[b], i * 16 + 16)
                    for q in range(PR):
                        b0 = q % 2 * 2
                        pe.wait_ge(relu_done, i * (2 * PR) + (b * PR + q + 1))
                        for k in range(2):
                            last = nc.tensor.matmul(ps[:, b0 + k, 0:HW], ea[:, b, 2 * q + k, :], c.ew[0:EF + 1, :], start=True, stop=True)
                        last.then_inc(enc_done, 1)
                        if q == 0:
                            pe.wait_ge(oht_done, i * 2 + (b + 3))
                        pe.wait_ge(prod_done, i * (2 * PR) + (b * PR + q + 1))
                        for k in range(2):
                            last = nc.tensor.matmul(ps[:, 4 + b0 + k, 0:HW], oht[:, b, 2 * q + k, :], h_all[:, ds(js[2 * q + k], HW)],
                                                    start=True, stop=True)
                        last.then_inc(hd_done, 1)

        @block.vector
        def _(dve):
            dve.sem_inc(prod_done, 2)
            dve.sem_inc(oht_done, 2)
            dve.sem_inc(red_done, 2)
            dve.sem_inc(sum_done, 2)

            def select(b, loads):
                dve.wait_ge(rel_loaded[b], loads * 16)
                nc.vector.tensor_scalar(oht[:, b, :, :], relb[:, b, :, :], c.iota_p[:, :], None, ALU.is_equal).then_inc(oht_done, 1)

            select(0, 1)
            with dve.Fori(0, TURNS // 2) as i:
                for b in range(2):
                    for q in range(PR):
                        n = b * PR + q
                        dve.wait_ge(relu_done, i * (2 * PR) + (n + 3))
                        dve.wait_ge(hd_done, i * (2 * PR) + (n + 3))
                        dve.wait_ge(red_done, i * (2 * PR) + (n + 1))
                        nc.vector.tensor_tensor(prod[:, q % 2, :, :], renc[:, q % 2, :, :], ps[:, 4 + q % 2 * 2:6 + q % 2 * 2, 0:HW],
                                                ALU.mult).then_inc(prod_done, 1)
                        if q == 1:
                            select(1 - b, i + 1 + b)
                        dve.wait_ge(prod_done, i * (2 * PR) + (n + 3))
                        if q == 0:
                            dve.wait_ge(sum_done, i * 2 + (b + 1))
                        nc.vector.tensor_reduce(red[:, b, 2 * q * H:(2 * q + 2) * H], prod[:, q % 2, :, :].rearrange("p s (h f) -> p (s h) f", f=D + 1), AX.X, ALU.add).then_inc(red_done, 1)
                    dve.wait_ge(gathered[b], i * (16 * R) + 16 * R)
                    dve.wait_ge(red_done, i * (2 * PR) + ((b + 1) * PR + 2))
                    nc.vector.tensor_tensor(a_all[:, ds(i * (2 * R * H) + b * R * H, R * H)], red[:, b, :],
                                            gat[:, b, :, :].rearrange("p k n -> p (k n)"), ALU.add).then_inc(sum_done, 1)


def softmax(nc, c, d):
    with ExitStack() as ctx:
        (dst_loaded, step, ends_out, ends_in, joined_out, joined_in, flipped, taken, alpha_made, shifted, exp_done,
         back, ex_stored) = semaphores(
            nc, ctx, "m_dst", "m_step", "m_endsout", "m_endsin", "m_joinedout", "m_joinedin", "m_flipped", "m_taken",
            "m_alpha", "m_shifted", "m_exp", "m_back", "m_exstored")
        a = c.arena[:, W2_AT:W2_AT + FLAT]
        s = c.arena[:, EX_AT:EX_AT + FLAT]
        alpha = c.arena[:, W1_AT:W1_AT + FLAT]
        link = c.arena[:, W1_AT + FLAT:W1_AT + 2 * FLAT + 1]
        fwd = c.arena[:, B1_AT:B1_AT + FLAT]
        targets = fwd
        top = c.arena[:, W2_AT + FLAT:W2_AT + 2 * FLAT]
        ex = c.arena[:, EX_AT:EX_AT + FLAT]
        at = B1_AT + FLAT
        ends = c.arena[:, at:at + CH * 4].rearrange("p (v c k) -> p v c k", v=2, k=2)
        joined = c.arena[:, at + CH * 4:at + CH * 6].rearrange("p (c k) -> p c k", k=2)
        chain_link = c.arena[0:H, W2_AT + 2 * FLAT:W2_AT + 2 * FLAT + CHAIN + 1]
        chain_raw = c.arena[0:H, EX_AT:EX_AT + 2 * CHAIN]
        chain = c.arena[0:H, EX_AT + 2 * CHAIN:EX_AT + 3 * CHAIN]
        chain_dst = fwd[0:H, 0:CHAIN]
        chain_fwd = fwd[0:H, CHAIN:2 * CHAIN]
        chain_top = fwd[0:H, 2 * CHAIN:3 * CHAIN]
        chain_out = fwd[0:H, 3 * CHAIN:4 * CHAIN]
        ps = c.psum
        BANKC = 4
        fills = [range(g, min(g + BANKC, CH)) for g in range(0, CH, BANKC)]
        PARTS = 4
        PW = FLAT // PARTS
        block = ctx.enter_context(nc.Block())

        @block.sync
        def _(sp):
            for h in range(H):
                sp.dma_start(targets[h * CT:(h + 1) * CT, :].rearrange("t (c e) -> t c e", e=P),
                             d.rel[0:SLOTS, :].rearrange("(c t) e -> t c e", t=CT)).then_inc(dst_loaded, 16)
            sp.wait_ge(step, 10)
            sp.dma_start(d.ends, ends.rearrange("p v c k -> p (v c k)")).then_inc(ends_out, 16)
            sp.wait_ge(ends_out, 16)
            sp.dma_start(chain_raw, d.ends.rearrange("(h t) n -> h (t n)", h=H)).then_inc(ends_in, 16)
            sp.wait_ge(step, 17)
            sp.dma_start(d.joined.rearrange("(h t) n -> h (t n)", h=H), chain_out).then_inc(joined_out, 16)
            sp.wait_ge(joined_out, 16)
            sp.dma_start(joined.rearrange("p c k -> p (c k)"), d.joined).then_inc(joined_in, 16)
            sp.wait_ge(joined_in, 16)

        @block.tensor
        def _(pe):
            for g, chunks in enumerate(fills):
                pe.wait_ge(alpha_made, min(-(-(chunks[-1] + 1) * P // PW), PARTS))
                if g >= 8:
                    pe.wait_ge(taken, g - 7)
                for n, ch in enumerate(chunks):
                    last = nc.tensor.transpose(ps[:, g % 8, n * P:(n + 1) * P],
                                               s[:, ch * P:(ch + 1) * P], c.ident[:, :])
                last.then_inc(flipped, 1)
            for g, chunks in enumerate(fills):
                pe.wait_ge(exp_done, g + 1)
                if g >= 8:
                    pe.wait_ge(ex_stored, g - 7)
                for n, ch in enumerate(chunks):
                    last = nc.tensor.transpose(ps[:, g % 8, n * P:(n + 1) * P], fwd[:, ch * P:(ch + 1) * P], c.ident[:, :])
                last.then_inc(back, 1)

        @block.scalar
        def _(act):
            for g, chunks in enumerate(fills):
                act.wait_ge(flipped, g + 1)
                nc.scalar.copy(alpha[:, chunks[0] * P:(chunks[-1] + 1) * P], ps[:, g % 8, 0:len(chunks) * P]).then_inc(taken, 1)
            for g, chunks in enumerate(fills):
                part = fwd[:, chunks[0] * P:(chunks[-1] + 1) * P]
                act.wait_ge(shifted, g + 1)
                nc.scalar.activation(part, part, ACT.Exp).then_inc(exp_done, 1)

        @block.vector
        def _(dve):
            for n in range(PARTS):
                cols = slice(n * PW, (n + 1) * PW)
                by_head = dict(t=CT, h=H)
                nc.vector.tensor_copy(alpha[:, cols].rearrange("p (c h t) -> p c h t", **by_head),
                                      a[:, cols].rearrange("p (c t h) -> p c h t", **by_head)).then_inc(c.alpha_sum, 1)
                dve.wait_ge(c.alpha_sum, n + 1)
                nc.vector.scalar_tensor_tensor(s[:, cols], alpha[:, cols], 0.2, alpha[:, cols], ALU.mult, ALU.max).then_inc(alpha_made, 1)
            dve.wait_ge(dst_loaded, 16 * H)
            nc.vector.tensor_tensor(link[:, 1:FLAT], targets[:, 1:FLAT], targets[:, 0:FLAT - 1], ALU.is_equal).then_inc(step, 1)
            nc.vector.tensor_copy(ends[:, 1, :, 0], targets[:, 0:FLAT:P]).then_inc(step, 1)
            nc.vector.tensor_copy(ends[:, 1, :, 1], targets[:, P - 1:FLAT:P]).then_inc(step, 1)
            dve.wait_ge(step, 3)
            nc.vector.tensor_scalar(link[:, 1:FLAT], link[:, 1:FLAT], -0.5, 2 * BIG, ALU.add, ALU.mult).then_inc(step, 1)
            dve.wait_ge(step, 4)
            nc.vector.memset(link[:, 0:FLAT:P], -BIG).then_inc(step, 1)
            nc.vector.memset(link[:, FLAT:FLAT + 1], -BIG).then_inc(step, 1)
            dve.wait_ge(step, 6)
            dve.wait_ge(taken, len(fills))
            nc.vector.tensor_tensor_scan(fwd, link[:, 0:FLAT], alpha, -BIG, ALU.min, ALU.max).then_inc(step, 1)
            dve.wait_ge(step, 7)
            nc.vector.tensor_tensor_scan(top[:, ::-1], link[:, 1:FLAT + 1][:, ::-1], fwd[:, ::-1], -BIG, ALU.min, ALU.max).then_inc(step, 1)
            dve.wait_ge(step, 8)
            nc.vector.tensor_copy(ends[:, 0, :, 0], top[:, 0:FLAT:P]).then_inc(step, 1)
            nc.vector.tensor_copy(ends[:, 0, :, 1], top[:, P - 1:FLAT:P]).then_inc(step, 1)
            dve.wait_ge(ends_in, 16)
            raw = chain_raw.rearrange("h (t v c k) -> h v c t k", t=CT, v=2, k=2)
            order = dict(c=CH, t=CT, k=2)
            nc.vector.tensor_copy(chain.rearrange("h (c t k) -> h c t k", **order), raw[:, 0]).then_inc(step, 1)
            nc.vector.tensor_copy(chain_dst.rearrange("h (c t k) -> h c t k", **order), raw[:, 1]).then_inc(step, 1)
            nc.vector.memset(chain_link[:, 0:CHAIN + 1:CHAIN], -BIG).then_inc(c.alpha_sum, 1)
            dve.wait_ge(step, 12)
            nc.vector.tensor_tensor(chain_link[:, 1:CHAIN], chain_dst[:, 1:CHAIN], chain_dst[:, 0:CHAIN - 1], ALU.is_equal).then_inc(step, 1)
            dve.wait_ge(step, 13)
            nc.vector.tensor_scalar(chain_link[:, 1:CHAIN], chain_link[:, 1:CHAIN], -0.5, 2 * BIG, ALU.add, ALU.mult).then_inc(step, 1)
            dve.wait_ge(step, 14)
            dve.wait_ge(c.alpha_sum, PARTS + 1)
            nc.vector.tensor_tensor_scan(chain_fwd, chain_link[:, 0:CHAIN], chain, -BIG, ALU.min, ALU.max).then_inc(step, 1)
            dve.wait_ge(step, 15)
            nc.vector.tensor_tensor_scan(chain_top[:, ::-1], chain_link[:, 1:CHAIN + 1][:, ::-1], chain_fwd[:, ::-1], -BIG, ALU.min,
                                         ALU.max).then_inc(step, 1)
            dve.wait_ge(step, 16)
            nc.vector.tensor_copy(chain_out.rearrange("h (t c k) -> h c t k", **order),
                                  chain_top.rearrange("h (c t k) -> h c t k", **order)).then_inc(step, 1)
            dve.wait_ge(joined_in, 16)
            nc.vector.tensor_copy(top[:, 0:FLAT:P], joined[:, :, 0]).then_inc(step, 1)
            nc.vector.tensor_copy(top[:, P - 1:FLAT:P], joined[:, :, 1]).then_inc(step, 1)
            dve.wait_ge(step, 19)
            nc.vector.tensor_tensor_scan(fwd, link[:, 0:FLAT], top, -BIG, ALU.min, ALU.max).then_inc(step, 1)
            dve.wait_ge(step, 20)
            nc.vector.tensor_tensor_scan(top[:, ::-1], link[:, 1:FLAT + 1][:, ::-1], fwd[:, ::-1], -BIG, ALU.min, ALU.max).then_inc(step, 1)
            dve.wait_ge(step, 21)
            for chunks in fills:
                cols = slice(chunks[0] * P, (chunks[-1] + 1) * P)
                nc.vector.tensor_tensor(fwd[:, cols], alpha[:, cols], top[:, cols], ALU.subtract).then_inc(shifted, 1)
            for g, chunks in enumerate(fills):
                dve.wait_ge(back, g + 1)
                n = len(chunks)
                nc.vector.tensor_copy(ex[:, chunks[0] * P:(chunks[-1] + 1) * P].rearrange("p (c t h) -> p c h t", c=n, h=H),
                                      ps[:, g % 8, 0:n * P].rearrange("p (c h t) -> p c h t", c=n, h=H)).then_inc(ex_stored, 1)


def aggregate(nc, c, d):
    with ExitStack() as ctx:
        (oh_done, msg_done, sum_done, acc_done, gate_done, idx_copied) = semaphores(nc, ctx, "g_oh", "g_msg", "g_sum", "g_acc", "g_gate", "g_idx")
        PR = R // 2
        gathered = semaphores(nc, ctx, *[f"g_gat{k}" for k in range(2 * PR)])
        acc = c.arena[:, W2_AT:W2_AT + J * HW]
        ex = c.arena[:, EX_AT:EX_AT + SLOTS * H]
        rows = c.arena[:, B1_AT:B1_AT + 2 * R * HW].rearrange("p (b k n) -> p b k n", b=2, k=R)
        oh = c.arena[:, W2_AT + J * HW:W2_AT + J * HW + 2 * R * P].rearrange("p (b k n) -> p b k n", b=2, k=R)
        w1 = c.arena[:, W1_AT:W1_AT + W1_WORDS].rearrange("p (k e n) -> p k e n", k=KH, e=X)
        ps = c.psum
        block = ctx.enter_context(nc.Block())

        @block.sync
        def _(sp):
            for e in range(X):
                sp.dma_start(w1[:, :, e, :], d.W1[e].rearrange("(k p) n -> p k n", p=P)).then_inc(c.w1_loaded, 16)

        @block.gpsimd
        def _(pool):
            pool.sem_inc(gate_done, 1)
            with pool.Fori(0, TURNS // 2) as i:
                for b in range(2):
                    for g in range(2):
                        pool.wait_ge(idx_copied, i * 2 + (b + 1))
                        pool.wait_ge(sum_done, i * (2 * PR) + (b * PR + (g + 1) * (PR // 2)))
                        pool.wait_ge(gate_done, i * 4 + (b * 2 + g + 1))
                        nc.gpsimd.tensor_tensor(c.gate[:, :], c.ones[0:1, 0:1], c.ones[0:1, 0:1], ALU.add).then_inc(gate_done, 1)
                        for k in range(g * PR, (g + 1) * PR):
                            pool.indirect_dma_start(rows[:, b, k, :], None, d.h_tab[:, :],
                                                    bass.IndirectOffsetOnAxis(ap=c.idx[:, b, k:k + 1], axis=0)).then_inc(gathered[b * PR + k // 2], 16)

        @block.scalar
        def _(act):
            with act.Fori(0, TURNS // 2) as i:
                for b in range(2):
                    act.wait_ge(sum_done, i * (2 * PR) + (b + 1) * PR)
                    nc.scalar.copy(c.idx[:, b, :], c.src[:, ds(i * (2 * R) + b * R, R)]).then_inc(idx_copied, 1)

        @block.tensor
        def _(pe):
            pe.sem_inc(sum_done, 2 * PR)
            with pe.Fori(0, TURNS // 2) as i:
                for b in range(2):
                    for q in range(PR):
                        n = b * PR + q
                        if q == 0:
                            pe.wait_ge(oh_done, i * 2 + (b + 1))
                        pe.wait_ge(msg_done, i * (2 * PR) + (n + 1))
                        pe.wait_ge(acc_done, i * (4 * PR) + (2 * n + 2))
                        for k in range(2):
                            last = nc.tensor.matmul(ps[:, 2 * q + k, 0:HW], oh[:, b, 2 * q + k, :], rows[:, b, 2 * q + k, :], start=True, stop=True)
                        last.then_inc(sum_done, 1)

        @block.vector
        def _(dve):
            nc.vector.memset(acc, 0.0).then_inc(acc_done, 8)

            def take(i, n, j):
                dve.wait_ge(sum_done, i * (2 * PR) + (2 * PR + n + 1))
                for k in range(2):
                    dve.wait_ge(acc_done, i * (4 * PR) + (8 + 2 * n + k))
                    a_j = acc[:, ds(j[k], HW)]
                    nc.vector.tensor_tensor(a_j, a_j, ps[:, 2 * (n % PR) + k, 0:HW], ALU.add).then_inc(acc_done, 1)

            with dve.Fori(0, TURNS // 2) as i:
                js = []
                for b in range(2):
                    js += load_words(nc, c.slot_j[0:1, ds(i * (2 * R) + b * R, R)], mybir.EngineType.DVE)
                    dve.wait_ge(sum_done, i * (2 * PR) + (b + 1) * PR)
                    nc.vector.tensor_tensor(oh[:, b, :, :], c.iota_row[:, :].unsqueeze(1).to_broadcast([P, R, P]),
                                            c.rel[:, ds(i * (2 * R) + b * R, R)].unsqueeze(2).to_broadcast([P, R, P]), ALU.is_equal).then_inc(oh_done, 1)
                    for q in range(PR):
                        n = b * PR + q
                        dve.wait_ge(gathered[n], i * 32 + 32)
                        row = rows[:, b, 2 * q:2 * q + 2, :].rearrange("p k (h f) -> p (k h) f", f=D + 1)
                        nc.vector.tensor_tensor(row, row, ex[:, ds(i * (2 * R * H) + 2 * n * H, 2 * H)].unsqueeze(2).to_broadcast([P, 2 * H, D + 1]),
                                                ALU.mult).then_inc(msg_done, 1)
                        if n:
                            take(i, n - 1, js[2 * n - 2:2 * n])
                take(i, 2 * PR - 1, js[-2:])


def attend(nc, c, d):
    with ExitStack() as ctx:
        (x_loaded, x2_made, x2_stored, stats1, merged1, var1, sd1, rs1, f_made, stats2, merged2, var2, sd2, rs2, xn_made,
         fT_made, fT_copied, logits_made, logits_copied, den_step, b_made, b_added) = semaphores(
            nc, ctx, "t_x", "t_x2", "t_x2st", "t_st1", "t_mg1", "t_var1", "t_sd1", "t_rs1", "t_f", "t_st2", "t_mg2", "t_var2", "t_sd2",
            "t_rs2", "t_xn", "t_fT", "t_fTc", "t_lg", "t_lgc", "t_den", "t_bm", "t_ba")
        acc = c.arena[:, W2_AT:W2_AT + J * HW]
        w1 = c.arena[:, W1_AT:W1_AT + W1_WORDS].rearrange("p (k e n) -> p k e n", k=KH, e=X)
        b1 = c.arena[:, B1_AT:B1_AT + B1_WORDS]
        logits = c.arena[:, LOGITS_AT:LOGITS_AT + J * X]
        GW = GT * IN
        xg = c.arena[:, EX_AT:EX_AT + GW].rearrange("p (k i) -> p k i", k=GT)
        f = c.arena[:, EX_AT + GW:EX_AT + 2 * GW].rearrange("p (k i) -> p k i", k=GT)
        att = c.arena[:, EX_AT + 2 * GW:EX_AT + 3 * GW]
        at = EX_AT + 3 * GW
        fT = c.arena[:, at:at + 2 * IN].rearrange("p (b i) -> p b i", b=2)
        at = LOGITS_AT + J * X
        den = c.arena[:, at:at + GT * H]
        st = c.arena[:, at + 64:at + 64 + GT * 6].rearrange("p (k s) -> p k s", k=GT)
        mv = c.arena[:, at + 128:at + 128 + 5 * GT].rearrange("p (s k) -> p s k", k=GT)
        mv2 = c.arena[:, at + 192:at + 192 + 5 * GT].rearrange("p (s k) -> p s k", k=GT)
        st2 = c.arena[:, at + 256:at + 256 + GT * 6].rearrange("p (k s) -> p k s", k=GT)
        sd, rs, sdb, rsb = (c.arena[:, at + 320 + 8 * n:at + 320 + 8 * n + GT] for n in range(4))
        ps = c.psum
        BIASES = [(e, b) for e in range(X) for b in range(HID // 512)]
        block = ctx.enter_context(nc.Block())

        @block.sync
        def _(sp):
            with sp.Fori(0, GROUPS) as i:
                sp.wait_ge(x2_stored, i * 16 + 16)
                sp.wait_ge(f_made, i * GT + GT)
                sp.dma_start(xg, d.x[ds(i * (GT * P), GT * P), :].rearrange("(k p) i -> p k i", p=P)).then_inc(x_loaded, 16)
                sp.wait_ge(x2_made, i + 1)
                sp.dma_start(d.x2[ds(i * (GT * P), GT * P), :].rearrange("(k p) i -> p k i", p=P), xg).then_inc(x2_stored, 16)
            sp.wait_ge(x2_stored, 16 * GROUPS + 16)

        @block.gpsimd
        def _(pool):
            pool.wait_ge(b_made, len(BIASES))
            for k in range(KH):
                for e in range(X):
                    nc.gpsimd.tensor_scalar(w1[:, k, e, :], w1[:, k, e, :], c.ln_g[:, k, e:e + 1], None, ALU.mult)

        @block.scalar
        def _(act):
            act.dma_start(b1, d.b1.rearrange("e n -> (e n)").partition_broadcast(P)).then_inc(c.w1_loaded, 16)
            with act.Fori(0, GROUPS) as i:
                act.wait_ge(var1, i + 1)
                nc.scalar.activation(sd, mv[:, 3, :], ACT.Sqrt, bias=c.eps[:, :], scale=1.0 / IN).then_inc(sd1, 1)
                act.wait_ge(var2, i + 1)
                nc.scalar.activation(sdb, mv2[:, 3, :], ACT.Sqrt, bias=c.eps[:, :], scale=1.0 / IN).then_inc(sd2, 1)
                for k in range(GT):
                    act.wait_ge(fT_made, i * GT + (k + 1))
                    act.wait_ge(logits_made, i * GT + (k + 1))
                    nc.scalar.copy(fT[:, k % 2, :], ps[:, k % 2, 0:IN]).then_inc(fT_copied, 1)

        @block.tensor
        def _(pe):
            pe.sem_inc(logits_made, 2)
            pe.wait_ge(c.w1_loaded, 16 * (X + 1))
            for n, (e, b) in enumerate(BIASES):
                if n >= 2:
                    pe.wait_ge(b_added, n - 1)
                for k in range(KH):
                    last = nc.tensor.matmul(ps[:, 4 + n % 2, :], c.ln_b[:, k, e:e + 1].to_broadcast([P, P]), w1[:, k, e, b * 512:(b + 1) * 512],
                                            start=(k == 0), stop=(k == KH - 1))
                last.then_inc(b_made, 1)
            with pe.Fori(0, GROUPS) as i:
                for k in range(GT):
                    pe.wait_ge(f_made, i * GT + (GT + k + 1))
                    pe.wait_ge(fT_copied, i * GT + (k + 1))
                    for m in range(KH):
                        last = nc.tensor.transpose(ps[:, k % 2, m * P:(m + 1) * P], f[:, k, m * P:(m + 1) * P], c.ident[:, :])
                    last.then_inc(fT_made, 1)
                    pe.wait_ge(fT_copied, i * GT + (k + 3))
                    if k == 0:
                        pe.wait_ge(logits_copied, i + 1)
                    for m in range(KH):
                        last = nc.tensor.matmul(ps[:, 2, k * X:(k + 1) * X], fT[:, k % 2, m * P:(m + 1) * P], c.wr[:, m, :],
                                                start=(m == 0), stop=(m == KH - 1))
                    last.then_inc(logits_made, 1)

        @block.vector
        def _(dve):
            dve.sem_inc(x2_stored, 16)
            dve.sem_inc(f_made, GT)
            dve.sem_inc(fT_copied, 2)
            dve.sem_inc(logits_copied, 1)
            for n, (e, b) in enumerate(BIASES):
                part = b1[:, e * HID + b * 512:e * HID + (b + 1) * 512]
                dve.wait_ge(b_made, n + 1)
                nc.vector.tensor_tensor(part, part, ps[:, 4 + n % 2, :], ALU.add).then_inc(b_added, 1)
            with dve.Fori(0, GROUPS) as i:
                sums = acc[:, ds(i * (GT * HW), GT * HW)].rearrange("p (q f) -> p q f", f=D + 1)
                nc.vector.tensor_scalar(den, sums[:, :, D], 1e-10, None, ALU.max).then_inc(den_step, 1)
                dve.wait_ge(den_step, i * 4 + 1)
                nc.vector.reciprocal(den, den).then_inc(den_step, 1)
                dve.wait_ge(den_step, i * 4 + 2)
                nc.vector.tensor_tensor(att.rearrange("p (q f) -> p q f", f=D), sums[:, :, 0:D],
                                        den.unsqueeze(2).to_broadcast([P, GT * H, D]), ALU.mult).then_inc(den_step, 1)
                dve.wait_ge(den_step, i * 4 + 3)
                att_k = att.rearrange("p (k i) -> p k i", k=GT)
                nc.vector.tensor_tensor(att_k, att_k, c.gnn_bias[:, :].unsqueeze(1).to_broadcast([P, GT, IN]), ALU.add).then_inc(den_step, 1)
                dve.wait_ge(den_step, i * 4 + 4)
                dve.wait_ge(x_loaded, i * 16 + 16)
                nc.vector.tensor_tensor(xg, xg, att_k, ALU.add).then_inc(x2_made, 1)
                dve.wait_ge(x2_made, i + 1)
                for k in range(GT):
                    nc.vector.bn_stats(st[:, k, :], xg[:, k, :]).then_inc(stats1, 1)
                dve.wait_ge(stats1, i * GT + GT)
                merge_stats(nc, dve, st, mv, i, merged1, var1)
                dve.wait_ge(sd1, i + 1)
                nc.vector.reciprocal(rs, sd).then_inc(rs1, 1)
                dve.wait_ge(rs1, i + 1)
                for k in range(GT):
                    nc.vector.tensor_scalar(f[:, k, :], xg[:, k, :], mv[:, 4, k:k + 1], rs[:, k:k + 1], ALU.subtract, ALU.mult).then_inc(f_made, 1)
                for k in range(GT):
                    dve.wait_ge(f_made, i * GT + (GT + k + 1))
                    nc.vector.bn_stats(st2[:, k, :], f[:, k, :]).then_inc(stats2, 1)
                dve.wait_ge(stats2, i * GT + GT)
                merge_stats(nc, dve, st2, mv2, i, merged2, var2)
                dve.wait_ge(sd2, i + 1)
                nc.vector.reciprocal(rsb, sdb).then_inc(rs2, 1)
                dve.wait_ge(rs2, i + 1)
                for k in range(GT):
                    nc.vector.tensor_scalar(acc[:, ds((i * GT + k) * HW, IN)], f[:, k, :], mv2[:, 4, k:k + 1], rsb[:, k:k + 1],
                                            ALU.subtract, ALU.mult).then_inc(xn_made, 1)
                dve.wait_ge(logits_made, i * GT + (GT + 2))
                nc.vector.tensor_tensor(logits[:, ds(i * (GT * X), GT * X)].rearrange("p (k e) -> p k e", e=X),
                                        ps[:, 2, 0:GT * X].rearrange("p (k e) -> p k e", e=X),
                                        c.br[:, :].unsqueeze(1).to_broadcast([P, GT, X]), ALU.add).then_inc(logits_copied, 1)


def route(nc, c, d):
    with ExitStack() as ctx:
        (iotas, step, p_made, ranks, tables, scattered) = semaphores(nc, ctx, "r_iotas", "r_step", "r_p", "r_ranks", "r_tables", "r_scattered")
        acc = c.arena[:, W2_AT:W2_AT + J * HW]
        logits = c.arena[:, LOGITS_AT:LOGITS_AT + J * X]
        C = J * X
        at = EX_AT

        def take(n):
            nonlocal at
            at += n
            assert at <= EX_AT + EX_WORDS
            return c.arena[:, at - n:at]

        same, score_, oh1, oh2, rest, total, before, tile_of = (take(C) for _ in range(8))
        top1, pick1, top2, pick2, gap, gate_sum = (take(J) for _ in range(6))
        rev, tiles, upto, offset, count = (take(X) for _ in range(5))
        tile_start = take(J)
        tile_id = take(XS_TILES)
        many = take(XS_TILES * X)
        place = take(TOPK * J)
        jx = lambda ap: ap.rearrange("p (j e) -> p j e", e=X)
        over_x = lambda ap: ap.unsqueeze(2).to_broadcast([P, J, X])
        over_j = lambda ap: ap.unsqueeze(1).to_broadcast([P, J, X])
        gate1, gate2 = c.gates[:, 0:J], c.gates[:, J:2 * J]
        ps = c.psum
        block = ctx.enter_context(nc.Block())

        @block.gpsimd
        def _(pool):
            ia = dict(allow_small_or_imprecise_dtypes=True)
            pool.iota(rev, [[-1, X]], base=X, channel_multiplier=0, **ia).then_inc(iotas, 1)
            pool.iota(tile_start, [[P, J]], base=0, channel_multiplier=0, **ia).then_inc(iotas, 1)
            pool.iota(tile_id, [[1, XS_TILES]], base=0, channel_multiplier=0, **ia).then_inc(iotas, 1)
            pool.wait_ge(tables, 2)
            for j in range(J):
                for k in range(TOPK):
                    pool.indirect_dma_start(d.xs[:, :], bass.IndirectOffsetOnAxis(ap=c.pos_i[:, k * J + j:k * J + j + 1], axis=0),
                                            acc[:, j * HW:j * HW + IN], None).then_inc(scattered, 16)
            pool.wait_ge(scattered, 16 * TOPK * J)

        @block.scalar
        def _(act):
            act.wait_ge(step, 12)
            nc.scalar.activation(gap, gap, ACT.Exp).then_inc(p_made, 1)

        @block.tensor
        def _(pe):
            pe.wait_ge(step, 13)
            nc.tensor.matmul(ps[:, 0, 0:C], c.tri[:, :], total, start=True, stop=True)
            nc.tensor.matmul(ps[:, 1, 0:C], c.ones[:, :], total, start=True, stop=True).then_inc(ranks, 1)

        @block.vector
        def _(dve):
            def choose(values, top, pick, onehot, n):
                nc.vector.tensor_reduce(top, jx(values), AX.X, ALU.max).then_inc(step, 1)
                dve.wait_ge(step, n + 1)
                nc.vector.tensor_tensor(jx(same), jx(values), over_x(top), ALU.is_equal).then_inc(step, 1)
                dve.wait_ge(step, n + 2)
                nc.vector.tensor_tensor(jx(score_), jx(same), over_j(rev), ALU.mult).then_inc(step, 1)
                dve.wait_ge(step, n + 3)
                nc.vector.tensor_reduce(pick, jx(score_), AX.X, ALU.max).then_inc(step, 1)
                dve.wait_ge(step, n + 4)
                nc.vector.tensor_tensor(jx(onehot), over_j(rev), over_x(pick), ALU.is_equal).then_inc(step, 1)
                dve.wait_ge(step, n + 5)

            dve.wait_ge(iotas, 3)
            choose(logits, top1, pick1, oh1, 0)
            nc.vector.scalar_tensor_tensor(rest, oh1, -3.0e38, logits, ALU.mult, ALU.add).then_inc(step, 1)
            dve.wait_ge(step, 6)
            choose(rest, top2, pick2, oh2, 6)
            nc.vector.tensor_tensor(gap, top2, top1, ALU.subtract).then_inc(step, 1)
            nc.vector.tensor_tensor(total, oh1, oh2, ALU.add).then_inc(step, 1)
            dve.wait_ge(p_made, 1)
            nc.vector.tensor_scalar(gate_sum, gap, 1.0, None, ALU.add).then_inc(step, 1)
            dve.wait_ge(step, 14)
            nc.vector.reciprocal(gate1, gate_sum).then_inc(step, 1)
            dve.wait_ge(step, 15)
            nc.vector.tensor_tensor(gate2, gap, gate1, ALU.mult).then_inc(step, 1)
            dve.wait_ge(ranks, 1)
            for e in range(X):
                nc.vector.tensor_tensor_scan(before[:, e:C:X], c.ones[:, 0:J], ps[:, 1, e:C:X], 0.0, ALU.mult, ALU.add).then_inc(step, 1)
            dve.wait_ge(step, 24)
            nc.vector.tensor_copy(count, before[:, (J - 1) * X:C]).then_inc(step, 1)
            dve.wait_ge(step, 25)
            nc.vector.tensor_tensor(before, before, ps[:, 1, 0:C], ALU.subtract).then_inc(step, 1)
            m = tile_of.rearrange("p (e j) -> p e j", e=X)
            nc.vector.tensor_tensor(m, count.unsqueeze(2).to_broadcast([P, X, J]), tile_start.unsqueeze(1).to_broadcast([P, X, J]),
                                    ALU.is_gt).then_inc(step, 1)
            dve.wait_ge(step, 27)
            nc.vector.tensor_reduce(tiles, m, AX.X, ALU.add).then_inc(step, 1)
            dve.wait_ge(step, 28)
            nc.vector.tensor_tensor_scan(upto, c.ones[:, 0:X], tiles, 0.0, ALU.mult, ALU.add).then_inc(step, 1)
            dve.wait_ge(step, 29)
            nc.vector.tensor_tensor(offset, upto, tiles, ALU.subtract).then_inc(step, 1)
            u = many.rearrange("p (u e) -> p u e", e=X)
            nc.vector.tensor_tensor(u, tile_id.unsqueeze(2).to_broadcast([P, XS_TILES, X]), upto.unsqueeze(1).to_broadcast([P, XS_TILES, X]),
                                    ALU.is_ge).then_inc(step, 1)
            dve.wait_ge(step, 31)
            nc.vector.tensor_scalar(offset, offset, float(P), None, ALU.mult).then_inc(step, 1)
            nc.vector.tensor_reduce(tile_id, u, AX.X, ALU.add).then_inc(step, 1)
            nc.vector.tensor_tensor(before, before, ps[:, 0, 0:C], ALU.add).then_inc(step, 1)
            dve.wait_ge(step, 34)
            nc.vector.tensor_scalar(c.tile_e[:, :], tile_id[0:1, :], float(X - 1), None, ALU.min).then_inc(step, 1)
            nc.vector.tensor_tensor(jx(before), jx(before), over_j(offset), ALU.add).then_inc(step, 1)
            dve.wait_ge(step, 36)
            nc.vector.tensor_tensor(oh1, oh1, before, ALU.mult).then_inc(step, 1)
            nc.vector.tensor_tensor(oh2, oh2, before, ALU.mult).then_inc(step, 1)
            dve.wait_ge(step, 38)
            nc.vector.tensor_reduce(place[:, 0:J], jx(oh1), AX.X, ALU.add).then_inc(step, 1)
            nc.vector.tensor_reduce(place[:, J:2 * J], jx(oh2), AX.X, ALU.add).then_inc(step, 1)
            dve.wait_ge(step, 40)
            nc.vector.tensor_copy(c.pos_i[:, :], place).then_inc(tables, 2)


def experts(nc, c, d):
    with ExitStack() as ctx:
        (x_loaded0, x_loaded1, b2_loaded, xT_made, xT_copied, up_done, pre_made, preT_made, gelu_done, down_done, y_made, y_stored0, y_stored1) = semaphores(
            nc, ctx, "e_x0", "e_x1", "e_b2", "e_xT", "e_xTc", "e_up", "e_pre", "e_preT", "e_gelu", "e_down", "e_y", "e_yst0", "e_yst1")
        x_loaded, y_stored = (x_loaded0, x_loaded1), (y_stored0, y_stored1)
        w1 = c.arena[:, W1_AT:W1_AT + W1_WORDS]
        w2 = c.arena[:, W2_AT:W2_AT + W2_WORDS]
        b1 = c.arena[:, B1_AT:B1_AT + B1_WORDS]
        HC = HID // P
        at = EX_AT

        def take(n):
            nonlocal at
            at += n
            assert at <= EX_AT + EX_WORDS
            return c.arena[:, at - n:at]

        pre = take(HID)
        hT = take(HID)
        b2 = take(X * IN)
        xt = take(2 * IN).rearrange("p (b i) -> p b i", b=2)
        xT = take(2 * IN).rearrange("p (b i) -> p b i", b=2)
        y = take(2 * IN).rearrange("p (b i) -> p b i", b=2)
        ps = c.psum
        UP, PRET, DOWN, XT = 0, 2, 4, 6
        PAIRS = MOE_TILES // 2
        block = ctx.enter_context(nc.Block())

        @block.sync
        def _(sp):
            sp.dma_start(b2, d.b2.rearrange("e n -> (e n)").partition_broadcast(P)).then_inc(b2_loaded, 16)
            for b in range(2):
                sp.dma_start(xt[:, b, :], d.xs[b * P:(b + 1) * P, :]).then_inc(x_loaded[b], 16)
            for e in range(X):
                sp.dma_start(w2.rearrange("p (h e n) -> p h e n", e=X, n=IN)[:, :, e, :],
                             d.W2[e].rearrange("(h p) n -> p h n", p=P)).then_inc(c.w2_loaded, 16)
            with sp.Fori(0, PAIRS) as i:
                for b in range(2):
                    sp.wait_ge(xT_made, i * 2 + (b + 1))
                    sp.dma_start(xt[:, b, :], d.xs[ds((i * 2 + (2 + b)) * P, P), :]).then_inc(x_loaded[b], 16)
                    sp.wait_ge(y_made, i * 2 + (b + 1))
                    sp.dma_start(d.ys[ds((i * 2 + b) * P, P), :], y[:, b, :]).then_inc(y_stored[b], 16)
            for b in range(2):
                sp.wait_ge(x_loaded[b], 16 * (PAIRS + 1))
                sp.wait_ge(y_stored[b], 16 * (PAIRS + 1))

        @block.tensor
        def _(pe):
            def turn_rows(n, b):
                for m in range(KH):
                    last = nc.tensor.transpose(ps[:, XT + b, m * P:(m + 1) * P], xt[:, b, m * P:(m + 1) * P], c.ident[:, :])
                last.then_inc(xT_made, 1)

            def up(e, b):
                for n in range(HID // 512):
                    for m in range(KH):
                        last = nc.tensor.matmul(ps[:, UP + n, :], xT[:, b, m * P:(m + 1) * P], w1[:, ds(e * HID + (m * X * HID + n * 512), 512)],
                                                start=(m == 0), stop=(m == KH - 1))
                last.then_inc(up_done, 1)

            pe.wait_ge(x_loaded[0], 16)
            turn_rows(0, 0)
            pe.wait_ge(x_loaded[1], 16)
            turn_rows(1, 1)
            pe.wait_ge(xT_copied, 1)
            up(pe.value_load(c.tile_e[0:1, 0:1], min_val=0, max_val=X - 1), 0)
            pe.wait_ge(c.w2_loaded, 16 * X)
            with pe.Fori(0, PAIRS) as i:
                for b in range(2):
                    e_now = pe.value_load(c.tile_e[0:1, ds(i * 2 + b, 1)], min_val=0, max_val=X - 1)
                    e_next = pe.value_load(c.tile_e[0:1, ds(i * 2 + (b + 1), 1)], min_val=0, max_val=X - 1)
                    pe.wait_ge(pre_made, i * 2 + (b + 1))
                    for h in range(HC):
                        last = nc.tensor.transpose(ps[:, PRET + h // 4, h % 4 * P:(h % 4 + 1) * P], pre[:, h * P:(h + 1) * P], c.ident[:, :])
                        if h % 4 == 3:
                            last.then_inc(preT_made, 1)
                    pe.wait_ge(xT_copied, i * 2 + (b + 2))
                    up(e_next, 1 - b)
                    pe.wait_ge(x_loaded[b], i * 16 + 32)
                    pe.wait_ge(xT_copied, i * 2 + (b + 1))
                    turn_rows(0, b)
                    pe.wait_ge(gelu_done, i * 4 + (2 * b + 2))
                    pe.wait_ge(y_made, i * 2 + (b + 1) - 1) if b else None
                    for h in range(HC):
                        last = nc.tensor.matmul(ps[:, DOWN + b, 0:IN], hT[:, h * P:(h + 1) * P], w2[:, ds(e_now * IN + h * X * IN, IN)],
                                                start=(h == 0), stop=(h == HC - 1))
                    last.then_inc(down_done, 1)

        @block.scalar
        def _(act):
            act.wait_ge(xT_made, 1)
            nc.scalar.copy(xT[:, 0, :], ps[:, XT, 0:IN]).then_inc(xT_copied, 1)
            act.wait_ge(xT_made, 2)
            nc.scalar.copy(xT[:, 1, :], ps[:, XT + 1, 0:IN]).then_inc(xT_copied, 1)
            with act.Fori(0, PAIRS) as i:
                for b in range(2):
                    for n in range(2):
                        act.wait_ge(preT_made, i * 4 + (2 * b + n + 1))
                        nc.scalar.activation(hT[:, n * 512:(n + 1) * 512], ps[:, PRET + n, :], ACT.Gelu).then_inc(gelu_done, 1)
                    act.wait_ge(xT_made, i * 2 + (b + 3))
                    nc.scalar.copy(xT[:, b, :], ps[:, XT + b, 0:IN]).then_inc(xT_copied, 1)

        @block.vector
        def _(dve):
            dve.sem_inc(y_stored[0], 16)
            dve.sem_inc(y_stored[1], 16)

            def bias(n, e):
                for q in range(2):
                    part = slice(q * 512, (q + 1) * 512)
                    last = nc.vector.tensor_tensor(pre[:, part], ps[:, UP + q, :], b1[:, ds(e * HID + q * 512, 512)], ALU.add)
                last.then_inc(pre_made, 1)

            dve.wait_ge(b2_loaded, 16)
            dve.wait_ge(up_done, 1)
            bias(0, dve.value_load(c.tile_e[0:1, 0:1], min_val=0, max_val=X - 1))
            with dve.Fori(0, PAIRS) as i:
                for b in range(2):
                    e_now = dve.value_load(c.tile_e[0:1, ds(i * 2 + b, 1)], min_val=0, max_val=X - 1)
                    e_next = dve.value_load(c.tile_e[0:1, ds(i * 2 + (b + 1), 1)], min_val=0, max_val=X - 1)
                    dve.wait_ge(up_done, i * 2 + (b + 2))
                    bias(0, e_next)
                    dve.wait_ge(down_done, i * 2 + (b + 1))
                    dve.wait_ge(y_stored[b], i * 16 + 16)
                    nc.vector.tensor_tensor(y[:, b, :], ps[:, DOWN + b, 0:IN], b2[:, ds(e_now * IN, IN)], ALU.add).then_inc(y_made, 1)


def combine(nc, c, d):
    with ExitStack() as ctx:
        (x_loaded, first_done, out_made, out_stored) = semaphores(nc, ctx, "c_x", "c_first", "c_out", "c_stored")
        gathered = semaphores(nc, ctx, *[f"c_gat{k}" for k in range(GT)])
        GW = GT * IN
        xg = c.arena[:, W1_AT:W1_AT + GW].rearrange("p (k i) -> p k i", k=GT)
        og = c.arena[:, W1_AT + GW:W1_AT + 2 * GW].rearrange("p (k i) -> p k i", k=GT)
        yg = c.arena[:, W1_AT + 2 * GW:W1_AT + 4 * GW].rearrange("p (k n i) -> p k n i", k=GT, n=TOPK)
        block = ctx.enter_context(nc.Block())

        @block.gpsimd
        def _(pool):
            for j in range(J):
                k = j % GT
                if j >= GT:
                    pool.wait_ge(out_made, j - GT + 1 + GT)
                for n in range(TOPK):
                    pool.indirect_dma_start(yg[:, k, n, :], None, d.ys[:, :],
                                            bass.IndirectOffsetOnAxis(ap=c.pos_i[:, n * J + j:n * J + j + 1], axis=0)).then_inc(gathered[k], 16)

        @block.sync
        def _(sp):
            with sp.Fori(0, GROUPS) as i:
                sp.wait_ge(out_made, i * GT + GT)
                sp.dma_start(xg, d.x2[ds(i * (GT * P), GT * P), :].rearrange("(k p) i -> p k i", p=P)).then_inc(x_loaded, 16)
                sp.wait_ge(out_made, i * GT + 2 * GT)
                sp.dma_start(d.out[ds(i * (GT * P), GT * P), :].rearrange("(k p) i -> p k i", p=P), og).then_inc(out_stored, 16)
            sp.wait_ge(out_stored, 16 * GROUPS + 16)

        @block.vector
        def _(dve):
            dve.sem_inc(out_made, GT)
            dve.sem_inc(out_stored, 16)
            with dve.Fori(0, GROUPS) as i:
                dve.wait_ge(x_loaded, i * 16 + 16)
                dve.wait_ge(out_stored, i * 16 + 16)
                for k in range(GT):
                    dve.wait_ge(gathered[k], i * 32 + 32)
                    nc.vector.scalar_tensor_tensor(xg[:, k, :], yg[:, k, 0, :], c.gates[:, ds(i * GT + k, 1)], xg[:, k, :], ALU.mult,
                                                   ALU.add).then_inc(first_done, 1)
                    dve.wait_ge(first_done, i * GT + (k + 1))
                    nc.vector.scalar_tensor_tensor(og[:, k, :], yg[:, k, 1, :], c.gates[:, ds(i * GT + (J + k), 1)], xg[:, k, :], ALU.mult,
                                                   ALU.add).then_inc(out_made, 1)



STAGES = [prepare, score, softmax, aggregate, attend, route, experts, combine]


def program(nc, d):
    c = Chip()
    with ExitStack() as ctx:
        def sb(name, shape, dt=F32):
            return ctx.enter_context(nc.sbuf_tensor(name, shape, dt))

        c.arena = sb("arena", [P, ARENA])
        c.psum = ctx.enter_context(nc.psum_tensor("psum", [P, 8, 512], F32))
        c.iota_row = sb("iota_row", [P, P])
        c.iota_p = sb("iota_p", [P, 1])
        c.ident = sb("ident", [P, P])
        c.tri = sb("tri", [P, P])
        c.ones = sb("ones", [P, P])
        c.eps = sb("eps", [P, 1])
        c.ew = sb("ew", [P, HW])
        c.src = sb("src", [P, SLOTS], I32)
        c.rel = sb("rel", [P, SLOTS])
        c.slot_j = sb("slot_j", [1, SG * P], I32)
        c.gnn_bias = sb("gnn_bias", [P, HD])
        c.wr = sb("wr", [P, KH, X])
        c.br = sb("br", [P, X])
        c.ln_g = sb("ln_g", [P, KH, X])
        c.ln_b = sb("ln_b", [P, KH, X])
        c.idx = sb("idx", [P, 2, R], I32)
        c.gate = sb("gate", [1, 1])
        c.pos_i = sb("pos_i", [P, TOPK * J], I32)
        c.gates = sb("gates", [P, TOPK * J])
        c.tile_e = sb("tile_e", [1, XS_TILES], I32)
        (c.consts_ready, c.alpha_sum, c.w1_loaded, c.w2_loaded) = semaphores(nc, ctx, "consts_ready", "m_alphasum", "w1_loaded", "w2_loaded")
        d.h_tab = nc.dram_tensor("h_tab", [NP, HW], F32)
        d.s_tab = nc.dram_tensor("s_tab", [NP, H], F32)
        d.slot_j = nc.dram_tensor("slot_j_list", [SG * P], I32)
        d.rel = nc.dram_tensor("rel_list", [SG * P, P], F32)
        d.ea_slots = nc.dram_tensor("ea_slots", [EF + 1, SG * P, P], F32)
        d.xs = nc.dram_tensor("xs", [XS_TILES * P, IN], F32)
        d.ys = nc.dram_tensor("ys", [MOE_TILES * P, IN], F32)
        d.x2 = nc.dram_tensor("x2", [NP, IN], F32)
        d.ends = nc.dram_tensor("ends", [P, CH * 4], F32).ap()
        d.joined = nc.dram_tensor("joined", [P, CH * 2], F32).ap()
        for stage in STAGES:
            stage(nc, c, d)


def kernel(**inputs):
    import numpy as np
    import concourse.bacc as bacc
    from concourse.bass_utils import run_bass_kernel_spmd as run

    f = np.float32
    x = np.concatenate([np.asarray(inputs["x"]), np.zeros((NP - N, IN), f)])
    src = np.concatenate([np.asarray(inputs["src"]), np.zeros(EP - E, np.int32)])
    dst = np.concatenate([np.asarray(inputs["dst"]), np.full(EP - E, NP - 1, np.int32)])
    ea = np.zeros((EF + 1, EP), f)
    ea[:EF, :E] = np.asarray(inputs["edge_attr_3"]).T
    ea[EF] = 1.0
    W = np.ascontiguousarray(inputs["L0_gnn_W"])
    a_bd = np.zeros((H, D, 2, H), f)
    for h in range(H):
        a_bd[h, :, 0, h] = inputs["L0_gnn_a_src"][h]
        a_bd[h, :, 1, h] = inputs["L0_gnn_a_dst"][h]
    ew = np.zeros((EF + 1, H, D + 1), f)
    ew[:EF, :, :D] = np.asarray(inputs["L0_gnn_edge_W"]).T.reshape(EF, H, D)
    ew[EF, :, :D] = np.asarray(inputs["L0_gnn_edge_b"]).reshape(H, D)
    ew[EF, :, D] = 1.0
    arrays = {
        "x": x, "src_rows": src.reshape(T, P), "dst_rows": dst.reshape(T, P),
        "ea_rows": ea.reshape(EF + 1, T, P).swapaxes(0, 1).reshape(T, (EF + 1) * P), "W": W, "WT": W.T, "a_bd": a_bd.reshape(HD, 2 * H), "ew": ew.reshape(EF + 1, HW),
        "gnn_bias": inputs["L0_gnn_bias"], "Wr": inputs["L0_ffn_Wr"], "br": inputs["L0_ffn_br"],
        "ln_gT": np.asarray(inputs["L0_ffn_ln_g"]).T, "ln_bT": np.asarray(inputs["L0_ffn_ln_b"]).T,
        "W1": inputs["L0_ffn_W1"], "b1": inputs["L0_ffn_b1"], "W2": inputs["L0_ffn_W2"], "b2": inputs["L0_ffn_b2"],
    }
    arrays = {k: np.ascontiguousarray(v) for k, v in arrays.items()}

    class Dram:
        pass

    nc = bacc.Bacc("TRN2", target_bir_lowering=False, num_devices=1)
    d = Dram()
    for name, a in arrays.items():
        d.__dict__[name] = nc.dram_tensor(f"in_{name}", a.shape, mybir.dt.from_np(a.dtype), kind="ExternalInput").ap()
    d.out = nc.dram_tensor("out_rows", (NP, IN), F32, kind="ExternalOutput").ap()
    program(nc, d)
    r = run(nc, [{f"in_{k}": v for k, v in arrays.items()}], core_ids=[0])
    return r.results[0]["out_rows"][:N]
```

```python
from contextlib import ExitStack

import concourse.bass as bass
from concourse import mybir

F32 = mybir.dt.float32
I32 = mybir.dt.int32
ALU = mybir.AluOpType
ACT = mybir.ActivationFunctionType
AX = mybir.AxisListType
ds = bass.ds

P = 128
N, IN, H, D, EF, E = 6250, 256, 8, 32, 3, 100000
X, HID, TOPK = 8, 1024, 2
HD = H * D
KH = IN // P
HW = H * (D + 1)
HS = HW + H
J = -(-N // P)
NP = J * P
GT = 7
GROUPS = J // GT
CT = 16
SLOTS = -(-(-(-E // P) + J - 1) // CT) * CT
T = SLOTS - J + 1
CH = SLOTS // CT
EP = T * P
R = 8
TURNS = SLOTS // R
SG = -(-SLOTS // P)
MOE_TILES = (TOPK * NP + X * (P - 1)) // P
MOE_TILES += MOE_TILES % 2
XS_TILES = MOE_TILES + 2
XW = IN + 2
LN_EPS = 1e-5
BIG = 1.5e38
FLAT = CH * P
CHAIN = SLOTS * 2
assert GROUPS * GT == J and TURNS * R == SLOTS and XS_TILES % 4 == 0

W1_AT = 0
W1_WORDS = KH * X * HID
W2_AT = W1_AT + W1_WORDS
W2_WORDS = HID // P * X * IN
B1_AT = W2_AT + W2_WORDS
B1_WORDS = X * HID
EX_AT = B1_AT + B1_WORDS
EX_WORDS = SLOTS * H
ARENA = EX_AT + EX_WORDS
LOGITS_AT = W2_AT + J * HW


class Chip:
    pass


def semaphores(nc, ctx, *names):
    return [ctx.enter_context(nc.semaphore(n)) for n in names]


def merge_stats(nc, dve, st, mv, turn, merged, var_made):
    nc.vector.tensor_tensor(mv[:, 0, :], st[:, :, 1], st[:, :, 4], ALU.add).then_inc(merged, 1)
    nc.vector.tensor_tensor(mv[:, 1, :], st[:, :, 1], st[:, :, 4], ALU.subtract).then_inc(merged, 1)
    nc.vector.tensor_tensor(mv[:, 2, :], st[:, :, 2], st[:, :, 5], ALU.add).then_inc(merged, 1)
    dve.wait_ge(merged, turn * 4 + 2)
    nc.vector.tensor_tensor(mv[:, 1, :], mv[:, 1, :], mv[:, 1, :], ALU.mult).then_inc(merged, 1)
    nc.vector.tensor_scalar(mv[:, 4, :], mv[:, 0, :], 0.5, None, ALU.mult)
    dve.wait_ge(merged, turn * 4 + 4)
    nc.vector.scalar_tensor_tensor(mv[:, 3, :], mv[:, 1, :], IN / 4.0, mv[:, 2, :], ALU.mult, ALU.add).then_inc(var_made, 1)


def prepare(nc, c, d):
    with ExitStack() as ctx:
        (consts_made, zeros_made, w_loaded, small_loaded, hi_loaded, hi_tile_made, hi_row_made, val_in_psum, below_made, counted,
         t_capped, j_made, t_made, t_stored, t_loaded, wa_made, wa_copied, stats, merged, var_made, sd_made, rs_made, xn_made,
         xT_made, xT_copied, h_made, h_copied, rows_stored, xs_zeroed, ew_zeroed, tiles_gathered, rel_made, src_made, turned,
         turned_back, lists_stored) = semaphores(
            nc, ctx, "p_consts", "p_zeros", "p_w", "p_small", "p_hi", "p_hitile", "p_hirow", "p_val", "p_below", "p_counted",
            "p_tcap", "p_j", "p_tmade", "p_tstored", "p_tloaded", "p_wa", "p_wacopied", "p_stats", "p_merged", "p_var", "p_sd", "p_rs",
            "p_xn", "p_xT", "p_xTcopied", "p_h", "p_hcopied", "p_stored", "p_xszero", "p_ewzero", "p_tilegat", "p_rel", "p_srcf",
            "p_turned", "p_back", "p_lists")
        x_loaded = semaphores(nc, ctx, *[f"p_x{i}" for i in range(GROUPS)])

        class Region:

            def __init__(self, start, end):
                self.at, self.end = start, end

            def take(self, n, rows=slice(0, P)):
                self.at += n
                assert self.at <= self.end
                return c.arena[rows, self.at - n:self.at]

        in_w1, in_w2, in_b1, in_ex = Region(W1_AT, W2_AT), Region(W2_AT, B1_AT), Region(B1_AT, EX_AT), Region(EX_AT, ARENA)
        row = slice(0, 1)
        h_all = in_w1.take(J * HW)
        hi_row, hi_tile, iota_t, val_row = (in_w1.take(T, row) for _ in range(4))
        x_all = in_w2.take(J * IN)
        w_nat = in_w2.take(KH * IN).rearrange("p (k i) -> p k i", k=KH)
        a_bd = in_w2.take(KH * 2 * H).rearrange("p (k h) -> p k h", k=KH)
        rhs_h = in_w2.take(KH * HS).rearrange("p (k n) -> p k n", k=KH)
        filler = in_w2.take(4 * XW)
        below = in_w2.take(T)
        slot_id, t_col, t_col_i, j_col, j_col_i = (in_w2.take(SG) for _ in range(5))
        st = in_w2.take(GT * 6).rearrange("p (k s) -> p k s", k=GT)
        mv = in_w2.take(5 * GT).rearrange("p (s k) -> p s k", k=GT)
        sd, rs = in_w2.take(GT), in_w2.take(GT)
        dst_rows, src_rows, rel, src_f, ea_rows = (in_b1.take(SG * n).rearrange("p (g e) -> p g e", g=SG) for n in (P, P, P, P, (EF + 1) * P))
        xn = in_ex.take(GT * IN).rearrange("p (k i) -> p k i", k=GT)
        xT = in_ex.take(3 * IN).rearrange("p (b i) -> p b i", b=3)
        s_all = in_ex.take(J * H)
        eps = c.eps
        ps = c.psum
        XT, HB, VAL, WA = 0, 3, 6, 7
        WA_COL = T // 2
        bank = lambda k: 2 if k == GT - 1 else k % 2
        block = ctx.enter_context(nc.Block())

        @block.gpsimd
        def _(pool):
            ia = dict(allow_small_or_imprecise_dtypes=True)
            pool.iota(c.iota_row[:, :], [[1, P]], base=0, channel_multiplier=0, **ia).then_inc(consts_made, 1)
            pool.iota(c.iota_p[:, :], [[0, 1]], base=0, channel_multiplier=1, **ia).then_inc(consts_made, 1)
            pool.memset(eps[:, :], LN_EPS).then_inc(consts_made, 1)
            pool.memset(c.ones[:, :], 1.0).then_inc(consts_made, 1)
            pool.iota(iota_t, [[1, T]], base=0, channel_multiplier=0, **ia).then_inc(consts_made, 1)
            pool.iota(slot_id, [[P, SG]], base=0, channel_multiplier=1, **ia).then_inc(consts_made, 1)
            pool.wait_ge(t_made, 2)
            for g in range(SG):
                for rows, table in ((dst_rows, d.dst_rows), (src_rows, d.src_rows), (ea_rows, d.ea_rows)):
                    rows = rows[:, g, :] if rows is ea_rows else rows[:, g, :].bitcast(I32)
                    pool.indirect_dma_start(rows, None, table, bass.IndirectOffsetOnAxis(ap=t_col_i[:, g:g + 1].bitcast(I32), axis=0)
                                            ).then_inc(tiles_gathered, 16)

        @block.sync
        def _(sp):
            with nc.allow_non_contiguous_dma(reason="last target of each edge tile"):
                sp.dma_start(hi_row.bitcast(I32), d.dst_rows.rearrange("t e -> e t")[P - 1:P, :]).then_inc(hi_loaded, 16)
            for i in range(GROUPS):
                sp.dma_start(x_all[:, i * GT * IN:(i + 1) * GT * IN].rearrange("p (k i) -> p k i", k=GT), d.x[i * GT * P:(i + 1) * GT * P, :].rearrange("(k p) i -> p k i", p=P)
                             ).then_inc(x_loaded[i], 16)
            sp.wait_ge(zeros_made, 2)
            for q in range(XS_TILES // 4):
                sp.dma_start(d.xs[q * 4 * P:(q + 1) * 4 * P, :].rearrange("(r p) i -> p r i", p=P),
                             filler.rearrange("p (r i) -> p r i", r=4)).then_inc(xs_zeroed, 16)
            sp.dma_start(d.out[NP:NP + P, :], filler[:, 0:IN]).then_inc(xs_zeroed, 16)
            sp.wait_ge(t_made, 2)
            with nc.allow_non_contiguous_dma(reason="column to row"):
                sp.dma_start(d.slot_j.rearrange("(g p) -> p g", p=P), j_col_i.bitcast(I32)).then_inc(t_stored, 16)
            sp.wait_ge(t_stored, 16)
            sp.dma_start(c.slot_j[:, :], d.slot_j.rearrange("(a s) -> a s", a=1)).then_inc(t_loaded, 16)
            with sp.Fori(0, GROUPS) as i:
                sp.wait_ge(h_copied, i * GT + (GT + 2))
                sp.dma_start(d.h_tab[ds(i * (GT * P), GT * P), :].rearrange("(k p) n -> p k n", p=P),
                             h_all[:, ds(i * (GT * HW), GT * HW)].rearrange("p (k n) -> p k n", k=GT)).then_inc(rows_stored, 16)
                sp.dma_start(d.s_tab[ds(i * (GT * P), GT * P), :].rearrange("(k p) n -> p k n", p=P),
                             s_all[:, ds(i * (GT * H), GT * H)].rearrange("p (k n) -> p k n", k=GT)).then_inc(rows_stored, 16)
            sp.wait_ge(rel_made, 1)
            sp.dma_start(d.rel.rearrange("(g p) e -> p g e", p=P), rel).then_inc(lists_stored, 16)
            sp.wait_ge(tiles_gathered, 16 * 3 * SG)
            for g in range(SG):
                sp.dma_start(d.ea_slots[:, g * P:(g + 1) * P, :].rearrange("f p e -> p f e"),
                             ea_rows[:, g, :].rearrange("p (f e) -> p f e", f=EF + 1)).then_inc(lists_stored, 16)
            sp.wait_ge(lists_stored, 16 * (SG + 1))
            sp.wait_ge(rows_stored, 32 * GROUPS)
            sp.wait_ge(t_loaded, 16)
            sp.wait_ge(small_loaded, 16 * 6)
            sp.wait_ge(xs_zeroed, 16 * (XS_TILES // 4 + 1))

        @block.scalar
        def _(act):
            act.sem_inc(h_copied, 2)
            act.dma_start(w_nat, d.W.rearrange("(k p) i -> p k i", p=P)).then_inc(w_loaded, 16)
            act.dma_start(a_bd, d.a_bd.rearrange("(k p) h -> p k h", p=P)).then_inc(w_loaded, 16)
            for k in range(KH):
                act.dma_start(rhs_h[:, k, 0:HW].rearrange("p (h f) -> p h f", f=D + 1)[:, :, 0:D],
                              d.WT[k * P:(k + 1) * P, :].rearrange("p (h f) -> p h f", f=D)).then_inc(w_loaded, 16)
            act.wait_ge(ew_zeroed, 1)
            act.dma_start(c.ew[0:EF + 1, :], d.ew).then_inc(small_loaded, 16)
            act.dma_start(c.gnn_bias[:, :], d.gnn_bias.partition_broadcast(P)).then_inc(small_loaded, 16)
            act.dma_start(c.wr[:, :, :], d.Wr.rearrange("(k p) e -> p k e", p=P)).then_inc(small_loaded, 16)
            act.dma_start(c.br[:, :], d.br.partition_broadcast(P)).then_inc(small_loaded, 16)
            act.dma_start(c.ln_g[:, :, :], d.ln_gT.rearrange("(k p) e -> p k e", p=P)).then_inc(small_loaded, 16)
            act.dma_start(c.ln_b[:, :, :], d.ln_bT.rearrange("(k p) e -> p k e", p=P)).then_inc(small_loaded, 16)

            def deviation(i):
                act.wait_ge(var_made, i + 1)
                nc.scalar.activation(sd, mv[:, 3, :], ACT.Sqrt, bias=eps[:, :], scale=1.0 / IN).then_inc(sd_made, 1)

            def take_xT(i, k):
                act.wait_ge(xT_made, i * GT + (k + 1))
                act.wait_ge(h_made, i * GT + (k + 1))
                nc.scalar.copy(xT[:, bank(k), :], ps[:, XT + bank(k), 0:IN]).then_inc(xT_copied, 1)

            def take_h(i, k):
                act.wait_ge(h_made, i * GT + (k + 3))
                nc.scalar.copy(h_all[:, ds((i * GT + k) * HW, HW)], ps[:, HB + bank(k), 0:HW])
                nc.scalar.copy(s_all[:, ds((i * GT + k) * H, H)], ps[:, HB + bank(k), HW:HS]).then_inc(h_copied, 1)

            def group(i, after):
                for k in range(GT):
                    if k + 1 < GT:
                        take_xT(i, k + 1)
                    elif after is not None:
                        take_xT(after, 0)
                    take_h(i, k)

            deviation(0)
            take_xT(0, 0)
            with act.Fori(0, GROUPS - 1) as i:
                deviation(i + 1)
                group(i, i + 1)
            group(GROUPS - 1, None)

        @block.tensor
        def _(pe):
            pe.sem_inc(h_made, 2)
            pe.wait_ge(w_loaded, 16 * (2 + KH))
            for k in range(KH):
                for m in range(KH):
                    last = nc.tensor.matmul(ps[:, WA, WA_COL + k * 2 * H:WA_COL + (k + 1) * 2 * H], w_nat[:, m, k * P:(k + 1) * P], a_bd[:, m, :],
                                            start=(m == 0), stop=(m == KH - 1))
            last.then_inc(wa_made, 1)
            pe.wait_ge(wa_copied, 2)
            pe.wait_ge(hi_row_made, 1)
            for b in range(2):
                last = nc.tensor.matmul(ps[:, VAL + b, 0:T // 2], c.ones[0:1, 0:P], val_row[:, b * (T // 2):(b + 1) * (T // 2)],
                                        start=True, stop=True)
            last.then_inc(val_in_psum, 1)
            pe.wait_ge(c.consts_ready, 2)

            def turn(i, k):
                pe.wait_ge(xn_made, i * GT + (k + 1))
                pe.wait_ge(xT_copied, i * GT + (k + 1))
                for m in range(KH):
                    last = nc.tensor.transpose(ps[:, XT + bank(k), m * P:(m + 1) * P], xn[:, k, m * P:(m + 1) * P], c.ident[:, :])
                last.then_inc(xT_made, 1)

            def project(i, k):
                pe.wait_ge(xT_copied, i * GT + (k + 3))
                pe.wait_ge(h_copied, i * GT + (k + 1))
                for m in range(KH):
                    last = nc.tensor.matmul(ps[:, HB + bank(k), 0:HS], xT[:, bank(k), m * P:(m + 1) * P], rhs_h[:, m, :],
                                            start=(m == 0), stop=(m == KH - 1))
                last.then_inc(h_made, 1)

            def group(i, after):
                for k in range(GT):
                    if k + 1 < GT:
                        turn(i, k + 1)
                    elif after is not None:
                        turn(after, 0)
                    project(i, k)

            turn(0, 0)
            with pe.Fori(0, GROUPS - 1) as i:
                group(i, i + 1)
            group(GROUPS - 1, None)
            for n, (rows, made) in enumerate(((rel, rel_made), (src_f, src_made))):
                pe.wait_ge(made, 1)
                for g in range(SG):
                    if g in (0, 4) and n:
                        pe.wait_ge(turned_back, g // 4 + 1)
                    last = nc.tensor.transpose(ps[:, VAL + g // 4, g % 4 * P:(g % 4 + 1) * P], rows[:, g, :], c.ident[:, :])
                    if g in (3, SG - 1):
                        last.then_inc(turned, 1)

        @block.vector
        def _(dve):
            dve.sem_inc(xT_copied, 2)
            nc.vector.memset(c.ew[:, :], 0.0).then_inc(ew_zeroed, 1)
            nc.vector.memset(filler, 0.0).then_inc(zeros_made, 1)
            dve.wait_ge(consts_made, 6)
            dve.wait_ge(zeros_made, 1)
            nc.vector.tensor_scalar(filler.bitcast(I32)[:, IN:4 * XW:XW], c.iota_p[:, :].to_broadcast([P, 4]), float(NP), None,
                                    ALU.add).then_inc(zeros_made, 1)
            nc.vector.tensor_scalar(c.ident[:, :], c.iota_row[:, :], c.iota_p[:, :], None, ALU.is_equal).then_inc(c.consts_ready, 1)
            nc.vector.tensor_scalar(c.tri[:, :], c.iota_row[:, :], c.iota_p[:, :], None, ALU.is_gt).then_inc(c.consts_ready, 1)
            dve.wait_ge(hi_loaded, 16)
            nc.vector.tensor_scalar(hi_tile.bitcast(I32), hi_row.bitcast(I32), 7, None, ALU.logical_shift_right).then_inc(hi_tile_made, 1)
            dve.wait_ge(hi_tile_made, 1)
            nc.vector.tensor_tensor(val_row, hi_tile.bitcast(I32), iota_t, ALU.add).then_inc(hi_row_made, 1)

            def statistics(i):
                for k in range(GT):
                    nc.vector.bn_stats(st[:, k, :], x_all[:, ds((i * GT + k) * IN, IN)]).then_inc(stats, 1)
                dve.wait_ge(stats, i * GT + GT)
                merge_stats(nc, dve, st, mv, i, merged, var_made)
                dve.wait_ge(sd_made, i + 1)
                nc.vector.reciprocal(rs, sd).then_inc(rs_made, 1)
                dve.wait_ge(rs_made, i + 1)

            def normalise(i, k):
                nc.vector.tensor_scalar(xn[:, k, :], x_all[:, ds((i * GT + k) * IN, IN)], mv[:, 4, k:k + 1],
                                        rs[:, k:k + 1], ALU.subtract, ALU.mult).then_inc(xn_made, 1)

            dve.wait_ge(x_loaded[0], 16)
            statistics(0)
            for k in range(GT):
                normalise(0, k)
            dve.wait_ge(wa_made, 1)
            wa = ps[:, WA, WA_COL:WA_COL + KH * 2 * H].rearrange("p (k s h) -> p k s h", k=KH, s=2)
            nc.vector.tensor_copy(rhs_h[:, :, HW:HS], wa[:, :, 0, :]).then_inc(wa_copied, 1)
            nc.vector.tensor_copy(rhs_h[:, :, D:HW:D + 1], wa[:, :, 1, :]).then_inc(wa_copied, 1)
            dve.wait_ge(val_in_psum, 1)
            for g in range(SG):
                if g:
                    dve.wait_ge(counted, g)
                nc.vector.tensor_scalar(below.rearrange("p (b t) -> p b t", b=2), ps[:, VAL:VAL + 2, 0:T // 2], slot_id[:, g:g + 1], None,
                                        ALU.is_lt).then_inc(below_made, 1)
                dve.wait_ge(below_made, g + 1)
                nc.vector.tensor_reduce(t_col[:, g:g + 1], below, AX.X, ALU.add).then_inc(counted, 1)
            dve.wait_ge(counted, SG)
            nc.vector.tensor_scalar(t_col, t_col, float(T - 1), None, ALU.min).then_inc(t_capped, 1)
            dve.wait_ge(t_capped, 1)
            nc.vector.tensor_tensor(j_col, slot_id, t_col, ALU.subtract).then_inc(j_made, 1)
            nc.vector.tensor_copy(t_col_i.bitcast(I32), t_col).then_inc(t_made, 1)
            dve.wait_ge(j_made, 1)
            nc.vector.tensor_scalar(j_col_i.bitcast(I32), j_col, float(HW), None, ALU.mult).then_inc(t_made, 1)
            nc.vector.tensor_scalar(j_col, j_col, float(P), None, ALU.mult).then_inc(j_made, 1)
            for i in range(1, GROUPS):
                dve.wait_ge(x_loaded[i], 16)
            with dve.Fori(0, GROUPS - 1) as i:
                statistics(i + 1)
                for k in range(GT):
                    dve.wait_ge(xT_made, i * GT + (k + 1))
                    normalise(i + 1, k)
            dve.wait_ge(tiles_gathered, 16 * 3 * SG)
            dve.wait_ge(j_made, 2)
            nc.vector.tensor_tensor(rel, dst_rows.bitcast(I32), j_col.unsqueeze(2).to_broadcast([P, SG, P]), ALU.subtract).then_inc(rel_made, 1)
            nc.vector.tensor_copy(src_f, src_rows.bitcast(I32)).then_inc(src_made, 1)
            for n, cols in enumerate((c.rel, c.src)):
                for q in range(2):
                    dve.wait_ge(turned, 2 * n + q + 1)
                    slots = slice(q * 4 * P, min((q + 1) * 4 * P, SLOTS))
                    nc.vector.tensor_copy(cols[:, slots], ps[:, VAL + q, 0:slots.stop - slots.start]).then_inc(turned_back, 1)
            dve.wait_ge(turned_back, 4)


def load_words(nc, row, engine):
    _, values = nc.values_load_multi_w_load_instructions(
        row, engines=(engine,), min_val=0, max_val=(J - 1) * HW,
        skip_runtime_bounds_check_because="slot s has node tile s - t(s), from 0 to J - 1 as targets lie below N")
    return values


def score(nc, c, d):
    with ExitStack() as ctx:
        (prod_done, red_done, sum_done, relu_done, enc_done, hd_done, oht_done, gate_done, idx_copied) = semaphores(
            nc, ctx, "s_prod", "s_red", "s_sum", "s_relu", "s_enc", "s_hd", "s_oht", "s_gate", "s_idx")
        (ea_zeroed,) = semaphores(nc, ctx, "s_eazero")
        ea_loaded = semaphores(nc, ctx, "s_ea0", "s_ea1")
        rel_loaded = semaphores(nc, ctx, "s_rel0", "s_rel1")
        gathered = semaphores(nc, ctx, "s_gat0", "s_gat1")
        PR = R // 2

        a_all = c.arena[:, W2_AT:W2_AT + SLOTS * H]
        h_all = c.arena[:, W1_AT:W1_AT + J * HW]
        at = W2_AT + SLOTS * H

        def take(n):
            nonlocal at
            at += n
            assert at <= B1_AT
            return c.arena[:, at - n:at]

        renc = take(4 * HW).rearrange("p (b s n) -> p b s n", b=2, s=2)
        prod = take(4 * HW).rearrange("p (b s n) -> p b s n", b=2, s=2)
        red = take(2 * R * H).rearrange("p (b n) -> p b n", b=2)
        gat = take(2 * R * H).rearrange("p (b k n) -> p b k n", b=2, k=R)
        relb = c.arena[:, EX_AT:EX_AT + 2 * R * P].rearrange("p (b k e) -> p b k e", b=2, k=R)
        oht = c.arena[:, EX_AT + 2 * R * P:EX_AT + 4 * R * P].rearrange("p (b k e) -> p b k e", b=2, k=R)
        ea = c.arena[:, B1_AT:B1_AT + 2 * R * P].rearrange("p (b k e) -> p b k e", b=2, k=R)
        ps = c.psum
        block = ctx.enter_context(nc.Block())

        @block.sync
        def _(sp):
            sp.wait_ge(ea_zeroed, 1)
            sp.dma_start(relb[:, 0, :, :], d.rel[0:R, :].partition_broadcast(P)).then_inc(rel_loaded[0], 16)
            with sp.Fori(0, TURNS // 2) as i:
                for b in range(2):
                    sp.wait_ge(enc_done, i * (2 * PR) + (b + 1) * PR)
                    sp.dma_start(ea[0:EF + 1, b, :, :], d.ea_slots[:, ds(i * (2 * R) + b * R, R), :]).then_inc(ea_loaded[b], 16)
                    sp.wait_ge(oht_done, i * 2 + (b + 2))
                    sp.dma_start(relb[:, 1 - b, :, :], d.rel[ds(i * (2 * R) + (b + 1) * R, R), :].partition_broadcast(P)).then_inc(rel_loaded[1 - b], 16)

        @block.gpsimd
        def _(pool):
            pool.sem_inc(gate_done, 1)
            with pool.Fori(0, TURNS // 2) as i:
                for b in range(2):
                    pool.wait_ge(idx_copied, i * 2 + (b + 1))
                    pool.wait_ge(gate_done, i * 2 + (b + 1))
                    nc.gpsimd.tensor_tensor(c.gate[:, :], c.ones[0:1, 0:1], c.ones[0:1, 0:1], ALU.add).then_inc(gate_done, 1)
                    for k in range(R):
                        pool.indirect_dma_start(gat[:, b, k, :], None, d.s_tab[:, :],
                                                bass.IndirectOffsetOnAxis(ap=c.idx[:, b, k:k + 1], axis=0)).then_inc(gathered[b], 16)

        @block.scalar
        def _(act):
            act.sem_inc(relu_done, 2)
            with act.Fori(0, TURNS // 2) as i:
                for b in range(2):
                    act.wait_ge(sum_done, i * 2 + (b + 1))
                    nc.scalar.copy(c.idx[:, b, :], c.src[:, ds(i * (2 * R) + b * R, R)]).then_inc(idx_copied, 1)
                    for q in range(PR):
                        act.wait_ge(prod_done, i * (2 * PR) + (b * PR + q + 1))
                        act.wait_ge(enc_done, i * (2 * PR) + (2 * PR + b * PR + q + 1))
                        b0 = q % 2 * 2
                        nc.scalar.activation(renc[:, q % 2, :, :], ps[:, b0:b0 + 2, 0:HW], ACT.Relu).then_inc(relu_done, 1)

        @block.tensor
        def _(pe):
            pe.sem_inc(enc_done, 2 * PR)
            pe.sem_inc(hd_done, 2)
            with pe.Fori(0, TURNS // 2) as i:
                for b in range(2):
                    js = load_words(nc, c.slot_j[0:1, ds(i * (2 * R) + b * R, R)], mybir.EngineType.PE)
                    pe.wait_ge(ea_loaded[b], i * 16 + 16)
                    for q in range(PR):
                        b0 = q % 2 * 2
                        pe.wait_ge(relu_done, i * (2 * PR) + (b * PR + q + 1))
                        for k in range(2):
                            last = nc.tensor.matmul(ps[:, b0 + k, 0:HW], ea[:, b, 2 * q + k, :], c.ew[:, :], start=True, stop=True)
                        last.then_inc(enc_done, 1)
                        if q == 0:
                            pe.wait_ge(oht_done, i * 2 + (b + 3))
                        pe.wait_ge(prod_done, i * (2 * PR) + (b * PR + q + 1))
                        for k in range(2):
                            last = nc.tensor.matmul(ps[:, 4 + b0 + k, 0:HW], oht[:, b, 2 * q + k, :], h_all[:, ds(js[2 * q + k], HW)],
                                                    start=True, stop=True)
                        last.then_inc(hd_done, 1)

        @block.vector
        def _(dve):
            nc.vector.memset(ea, 0.0).then_inc(ea_zeroed, 1)
            dve.sem_inc(prod_done, 2)
            dve.sem_inc(oht_done, 2)
            dve.sem_inc(red_done, 2)
            dve.sem_inc(sum_done, 2)

            def select(b, loads):
                dve.wait_ge(rel_loaded[b], loads * 16)
                nc.vector.tensor_scalar(oht[:, b, :, :], relb[:, b, :, :], c.iota_p[:, :], None, ALU.is_equal).then_inc(oht_done, 1)

            select(0, 1)
            with dve.Fori(0, TURNS // 2) as i:
                for b in range(2):
                    for q in range(PR):
                        n = b * PR + q
                        dve.wait_ge(relu_done, i * (2 * PR) + (n + 3))
                        dve.wait_ge(hd_done, i * (2 * PR) + (n + 3))
                        dve.wait_ge(red_done, i * (2 * PR) + (n + 1))
                        nc.vector.tensor_tensor(prod[:, q % 2, :, :], renc[:, q % 2, :, :], ps[:, 4 + q % 2 * 2:6 + q % 2 * 2, 0:HW],
                                                ALU.mult).then_inc(prod_done, 1)
                        if q == 1:
                            select(1 - b, i + 1 + b)
                        dve.wait_ge(prod_done, i * (2 * PR) + (n + 3))
                        if q == 0:
                            dve.wait_ge(sum_done, i * 2 + (b + 1))
                        nc.vector.tensor_reduce(red[:, b, 2 * q * H:(2 * q + 2) * H], prod[:, q % 2, :, :].rearrange("p s (h f) -> p (s h) f", f=D + 1), AX.X, ALU.add).then_inc(red_done, 1)
                    dve.wait_ge(gathered[b], i * (16 * R) + 16 * R)
                    dve.wait_ge(red_done, i * (2 * PR) + ((b + 1) * PR + 2))
                    nc.vector.tensor_tensor(a_all[:, ds(i * (2 * R * H) + b * R * H, R * H)], red[:, b, :],
                                            gat[:, b, :, :].rearrange("p k n -> p (k n)"), ALU.add).then_inc(sum_done, 1)


def softmax(nc, c, d):
    with ExitStack() as ctx:
        (dst_loaded, step, ends_out, ends_in, joined_out, joined_in, flipped, taken, alpha_made, shifted, exp_done,
         back, ex_stored) = semaphores(
            nc, ctx, "m_dst", "m_step", "m_endsout", "m_endsin", "m_joinedout", "m_joinedin", "m_flipped", "m_taken",
            "m_alpha", "m_shifted", "m_exp", "m_back", "m_exstored")
        a = c.arena[:, W2_AT:W2_AT + FLAT]
        s = c.arena[:, EX_AT:EX_AT + FLAT]
        alpha = c.arena[:, W1_AT:W1_AT + FLAT]
        link = c.arena[:, W1_AT + FLAT:W1_AT + 2 * FLAT + 1]
        fwd = c.arena[:, B1_AT:B1_AT + FLAT]
        targets = fwd
        top = c.arena[:, W2_AT + FLAT:W2_AT + 2 * FLAT]
        ex = c.arena[:, EX_AT:EX_AT + FLAT]
        at = B1_AT + FLAT
        ends = c.arena[:, at:at + CH * 4].rearrange("p (v c k) -> p v c k", v=2, k=2)
        joined = c.arena[:, at + CH * 4:at + CH * 6].rearrange("p (c k) -> p c k", k=2)
        chain_link = c.arena[0:H, W2_AT + 2 * FLAT:W2_AT + 2 * FLAT + CHAIN + 1]
        chain_raw = c.arena[0:H, EX_AT:EX_AT + 2 * CHAIN]
        chain = c.arena[0:H, EX_AT + 2 * CHAIN:EX_AT + 3 * CHAIN]
        chain_dst = fwd[0:H, 0:CHAIN]
        chain_fwd = fwd[0:H, CHAIN:2 * CHAIN]
        chain_top = fwd[0:H, 2 * CHAIN:3 * CHAIN]
        chain_out = fwd[0:H, 3 * CHAIN:4 * CHAIN]
        ps = c.psum
        BANKC = 4
        fills = [range(g, min(g + BANKC, CH)) for g in range(0, CH, BANKC)]
        PARTS = 4
        PW = FLAT // PARTS
        block = ctx.enter_context(nc.Block())

        @block.sync
        def _(sp):
            for h in range(H):
                sp.dma_start(targets[h * CT:(h + 1) * CT, :].rearrange("t (c e) -> t c e", e=P),
                             d.rel[0:SLOTS, :].rearrange("(c t) e -> t c e", t=CT)).then_inc(dst_loaded, 16)
            sp.wait_ge(step, 10)
            sp.dma_start(d.ends, ends.rearrange("p v c k -> p (v c k)")).then_inc(ends_out, 16)
            sp.wait_ge(ends_out, 16)
            sp.dma_start(chain_raw, d.ends.rearrange("(h t) n -> h (t n)", h=H)).then_inc(ends_in, 16)
            sp.wait_ge(step, 17)
            sp.dma_start(d.joined.rearrange("(h t) n -> h (t n)", h=H), chain_out).then_inc(joined_out, 16)
            sp.wait_ge(joined_out, 16)
            sp.dma_start(joined.rearrange("p c k -> p (c k)"), d.joined).then_inc(joined_in, 16)
            sp.wait_ge(joined_in, 16)

        @block.tensor
        def _(pe):
            for g, chunks in enumerate(fills):
                pe.wait_ge(alpha_made, min(-(-(chunks[-1] + 1) * P // PW), PARTS))
                if g >= 8:
                    pe.wait_ge(taken, g - 7)
                for n, ch in enumerate(chunks):
                    last = nc.tensor.transpose(ps[:, g % 8, n * P:(n + 1) * P],
                                               s[:, ch * P:(ch + 1) * P], c.ident[:, :])
                last.then_inc(flipped, 1)
            for g, chunks in enumerate(fills):
                pe.wait_ge(exp_done, g + 1)
                if g >= 8:
                    pe.wait_ge(ex_stored, g - 7)
                for n, ch in enumerate(chunks):
                    last = nc.tensor.transpose(ps[:, g % 8, n * P:(n + 1) * P], fwd[:, ch * P:(ch + 1) * P], c.ident[:, :])
                last.then_inc(back, 1)

        @block.scalar
        def _(act):
            for g, chunks in enumerate(fills):
                act.wait_ge(flipped, g + 1)
                nc.scalar.copy(alpha[:, chunks[0] * P:(chunks[-1] + 1) * P], ps[:, g % 8, 0:len(chunks) * P]).then_inc(taken, 1)
            for g, chunks in enumerate(fills):
                part = fwd[:, chunks[0] * P:(chunks[-1] + 1) * P]
                act.wait_ge(shifted, g + 1)
                nc.scalar.activation(part, part, ACT.Exp).then_inc(exp_done, 1)

        @block.vector
        def _(dve):
            for n in range(PARTS):
                cols = slice(n * PW, (n + 1) * PW)
                by_head = dict(t=CT, h=H)
                nc.vector.tensor_copy(alpha[:, cols].rearrange("p (c h t) -> p c h t", **by_head),
                                      a[:, cols].rearrange("p (c t h) -> p c h t", **by_head)).then_inc(c.alpha_sum, 1)
                dve.wait_ge(c.alpha_sum, n + 1)
                nc.vector.scalar_tensor_tensor(s[:, cols], alpha[:, cols], 0.2, alpha[:, cols], ALU.mult, ALU.max).then_inc(alpha_made, 1)
            dve.wait_ge(dst_loaded, 16 * H)
            nc.vector.tensor_tensor(link[:, 1:FLAT], targets[:, 1:FLAT], targets[:, 0:FLAT - 1], ALU.is_equal).then_inc(step, 1)
            nc.vector.tensor_copy(ends[:, 1, :, 0], targets[:, 0:FLAT:P]).then_inc(step, 1)
            nc.vector.tensor_copy(ends[:, 1, :, 1], targets[:, P - 1:FLAT:P]).then_inc(step, 1)
            dve.wait_ge(step, 3)
            nc.vector.tensor_scalar(link[:, 1:FLAT], link[:, 1:FLAT], -0.5, 2 * BIG, ALU.add, ALU.mult).then_inc(step, 1)
            dve.wait_ge(step, 4)
            nc.vector.memset(link[:, 0:FLAT:P], -BIG).then_inc(step, 1)
            nc.vector.memset(link[:, FLAT:FLAT + 1], -BIG).then_inc(step, 1)
            dve.wait_ge(step, 6)
            dve.wait_ge(taken, len(fills))
            nc.vector.tensor_tensor_scan(fwd, link[:, 0:FLAT], alpha, -BIG, ALU.min, ALU.max).then_inc(step, 1)
            dve.wait_ge(step, 7)
            nc.vector.tensor_tensor_scan(top[:, ::-1], link[:, 1:FLAT + 1][:, ::-1], fwd[:, ::-1], -BIG, ALU.min, ALU.max).then_inc(step, 1)
            dve.wait_ge(step, 8)
            nc.vector.tensor_copy(ends[:, 0, :, 0], top[:, 0:FLAT:P]).then_inc(step, 1)
            nc.vector.tensor_copy(ends[:, 0, :, 1], top[:, P - 1:FLAT:P]).then_inc(step, 1)
            dve.wait_ge(ends_in, 16)
            raw = chain_raw.rearrange("h (t v c k) -> h v c t k", t=CT, v=2, k=2)
            order = dict(c=CH, t=CT, k=2)
            nc.vector.tensor_copy(chain.rearrange("h (c t k) -> h c t k", **order), raw[:, 0]).then_inc(step, 1)
            nc.vector.tensor_copy(chain_dst.rearrange("h (c t k) -> h c t k", **order), raw[:, 1]).then_inc(step, 1)
            nc.vector.memset(chain_link[:, 0:CHAIN + 1:CHAIN], -BIG).then_inc(c.alpha_sum, 1)
            dve.wait_ge(step, 12)
            nc.vector.tensor_tensor(chain_link[:, 1:CHAIN], chain_dst[:, 1:CHAIN], chain_dst[:, 0:CHAIN - 1], ALU.is_equal).then_inc(step, 1)
            dve.wait_ge(step, 13)
            nc.vector.tensor_scalar(chain_link[:, 1:CHAIN], chain_link[:, 1:CHAIN], -0.5, 2 * BIG, ALU.add, ALU.mult).then_inc(step, 1)
            dve.wait_ge(step, 14)
            dve.wait_ge(c.alpha_sum, PARTS + 1)
            nc.vector.tensor_tensor_scan(chain_fwd, chain_link[:, 0:CHAIN], chain, -BIG, ALU.min, ALU.max).then_inc(step, 1)
            dve.wait_ge(step, 15)
            nc.vector.tensor_tensor_scan(chain_top[:, ::-1], chain_link[:, 1:CHAIN + 1][:, ::-1], chain_fwd[:, ::-1], -BIG, ALU.min,
                                         ALU.max).then_inc(step, 1)
            dve.wait_ge(step, 16)
            nc.vector.tensor_copy(chain_out.rearrange("h (t c k) -> h c t k", **order),
                                  chain_top.rearrange("h (c t k) -> h c t k", **order)).then_inc(step, 1)
            dve.wait_ge(joined_in, 16)
            nc.vector.tensor_copy(top[:, 0:FLAT:P], joined[:, :, 0]).then_inc(step, 1)
            nc.vector.tensor_copy(top[:, P - 1:FLAT:P], joined[:, :, 1]).then_inc(step, 1)
            dve.wait_ge(step, 19)
            nc.vector.tensor_tensor_scan(fwd, link[:, 0:FLAT], top, -BIG, ALU.min, ALU.max).then_inc(step, 1)
            dve.wait_ge(step, 20)
            nc.vector.tensor_tensor_scan(top[:, ::-1], link[:, 1:FLAT + 1][:, ::-1], fwd[:, ::-1], -BIG, ALU.min, ALU.max).then_inc(step, 1)
            dve.wait_ge(step, 21)
            for chunks in fills:
                cols = slice(chunks[0] * P, (chunks[-1] + 1) * P)
                nc.vector.tensor_tensor(fwd[:, cols], alpha[:, cols], top[:, cols], ALU.subtract).then_inc(shifted, 1)
            for g, chunks in enumerate(fills):
                dve.wait_ge(back, g + 1)
                n = len(chunks)
                nc.vector.tensor_copy(ex[:, chunks[0] * P:(chunks[-1] + 1) * P].rearrange("p (c t h) -> p c h t", c=n, h=H),
                                      ps[:, g % 8, 0:n * P].rearrange("p (c h t) -> p c h t", c=n, h=H)).then_inc(ex_stored, 1)


def aggregate(nc, c, d):
    with ExitStack() as ctx:
        (msg_done, den_done, sum_done, acc_done, gate_done, idx_copied) = semaphores(nc, ctx, "g_msg", "g_den", "g_sum", "g_acc", "g_gate", "g_idx")
        PR = R // 2
        gathered = semaphores(nc, ctx, *[f"g_gat{k}" for k in range(2 * PR)])
        acc = c.arena[:, W2_AT:W2_AT + J * HW]
        ex = c.arena[:, EX_AT:EX_AT + SLOTS * H]
        rows = c.arena[:, B1_AT:B1_AT + 2 * R * HW].rearrange("p (b k n) -> p b k n", b=2, k=R)
        oh = c.arena[:, W2_AT + J * HW:W2_AT + J * HW + 2 * R * P].rearrange("p (b k n) -> p b k n", b=2, k=R)
        w1 = c.arena[:, W1_AT:W1_AT + W1_WORDS].rearrange("p (k e n) -> p k e n", k=KH, e=X)
        ps = c.psum
        block = ctx.enter_context(nc.Block())

        @block.sync
        def _(sp):
            for e in range(X):
                sp.dma_start(w1[:, :, e, :], d.W1[e].rearrange("(k p) n -> p k n", p=P)).then_inc(c.w1_loaded, 16)

        @block.gpsimd
        def _(pool):
            pool.sem_inc(gate_done, 1)
            with pool.Fori(0, TURNS // 2) as i:
                for b in range(2):
                    for g in range(2):
                        pool.wait_ge(idx_copied, i * 2 + (b + 1))
                        pool.wait_ge(sum_done, i * (2 * PR) + (b * PR + (g + 1) * (PR // 2)))
                        pool.wait_ge(gate_done, i * 4 + (b * 2 + g + 1))
                        nc.gpsimd.tensor_tensor(c.gate[:, :], c.ones[0:1, 0:1], c.ones[0:1, 0:1], ALU.add).then_inc(gate_done, 1)
                        for k in range(g * PR, (g + 1) * PR):
                            pool.indirect_dma_start(rows[:, b, k, :], None, d.h_tab[:, :],
                                                    bass.IndirectOffsetOnAxis(ap=c.idx[:, b, k:k + 1], axis=0)).then_inc(gathered[b * PR + k // 2], 16)

        @block.scalar
        def _(act):
            def indices(i, b):
                nc.scalar.copy(c.idx[:, b, :], c.src[:, ds(i * (2 * R) + b * R, R)]).then_inc(idx_copied, 1)

            def weights(i, n):
                b, q = divmod(n, PR)
                act.wait_ge(gathered[n], i * 32 + 32)
                nc.scalar.copy(rows[:, b, 2 * q:2 * q + 2, D:HW:D + 1],
                               ex[:, ds(i * (2 * R * H) + 2 * n * H, 2 * H)].rearrange("p (k h) -> p k h", k=2)).then_inc(den_done, 1)

            indices(0, 0)
            indices(0, 1)
            with act.Fori(0, TURNS // 2 - 1) as i:
                for b in range(2):
                    for q in range(PR):
                        weights(i, b * PR + q)
                    indices(i + 1, b)
            for n in range(2 * PR):
                weights(TURNS // 2 - 1, n)

        @block.tensor
        def _(pe):
            pe.sem_inc(sum_done, 2 * PR)
            with pe.Fori(0, TURNS // 2) as i:
                for n in range(2 * PR):
                    b, q = divmod(n, PR)
                    pe.wait_ge(den_done, i * (2 * PR) + (n + 1))
                    pe.wait_ge(msg_done, i * (2 * PR) + (n + 1))
                    pe.wait_ge(acc_done, i * (4 * PR) + (2 * n + 2))
                    for k in range(2):
                        last = nc.tensor.matmul(ps[:, 2 * q + k, 0:HW], oh[:, b, 2 * q + k, :], rows[:, b, 2 * q + k, :], start=True, stop=True)
                    last.then_inc(sum_done, 1)

        @block.vector
        def _(dve):
            nc.vector.memset(acc, 0.0).then_inc(acc_done, 8)
            STEPS, PAIRS = TURNS // 2, 2 * PR

            def one_hot(i, n):
                b, q = divmod(n, PR)
                dve.wait_ge(sum_done, i * PAIRS + (n + 1))
                nc.vector.tensor_tensor(oh[:, b, 2 * q:2 * q + 2, :], c.iota_row[:, :].unsqueeze(1).to_broadcast([P, 2, P]),
                                        c.rel[:, ds(i * (2 * R) + 2 * n, 2)].unsqueeze(2).to_broadcast([P, 2, P]), ALU.is_equal)

            def message(i, n):
                b, q = divmod(n, PR)
                dve.wait_ge(gathered[n], i * 32 + 32)
                row = rows[:, b, 2 * q:2 * q + 2, :].rearrange("p k (h f) -> p (k h) f", f=D + 1)[:, :, 0:D]
                nc.vector.tensor_tensor(row, row, ex[:, ds(i * (2 * R * H) + 2 * n * H, 2 * H)].unsqueeze(2).to_broadcast([P, 2 * H, D]),
                                        ALU.mult).then_inc(msg_done, 1)

            def take(i, n, k, j):
                if k == 0:
                    dve.wait_ge(sum_done, i * PAIRS + (PAIRS + n + 1))
                dve.wait_ge(acc_done, i * (2 * PAIRS) + (8 + 2 * n + k))
                a_j = acc[:, ds(j, HW)]
                nc.vector.tensor_tensor(a_j, a_j, ps[:, 2 * (n % PR) + k, 0:HW], ALU.add).then_inc(acc_done, 1)

            def step(i, then):
                for n in range(PAIRS):
                    if n % PR == 0:
                        js = load_words(nc, c.slot_j[0:1, ds(i * (2 * R) + 2 * n, R)], mybir.EngineType.DVE)
                    ahead = (i, n + LEAD) if n + LEAD < PAIRS else (then, n + LEAD - PAIRS)
                    if ahead[0] is not None:
                        one_hot(*ahead)
                    take(i, n, 0, js[2 * (n % PR)])
                    if ahead[0] is not None:
                        message(*ahead)
                    take(i, n, 1, js[2 * (n % PR) + 1])

            LEAD = 2
            for n in range(LEAD):
                one_hot(0, n)
                message(0, n)
            with dve.Fori(0, STEPS - 1) as i:
                step(i, i + 1)
            step(STEPS - 1, None)


def attend(nc, c, d):
    with ExitStack() as ctx:
        (x_loaded, x2_made, x2_stored, stats1, merged1, var1, sd1, rs1, f_made, stats2, merged2, var2, sd2, rs2, xn_made,
         fT_made, fT_copied, logits_made, logits_copied, den_step) = semaphores(
            nc, ctx, "t_x", "t_x2", "t_x2st", "t_st1", "t_mg1", "t_var1", "t_sd1", "t_rs1", "t_f", "t_st2", "t_mg2", "t_var2", "t_sd2",
            "t_rs2", "t_xn", "t_fT", "t_fTc", "t_lg", "t_lgc", "t_den")
        acc = c.arena[:, W2_AT:W2_AT + J * HW]
        logits = c.arena[:, LOGITS_AT:LOGITS_AT + J * X]
        GW = GT * IN
        xg = c.arena[:, EX_AT:EX_AT + GW].rearrange("p (k i) -> p k i", k=GT)
        f = c.arena[:, EX_AT + GW:EX_AT + 2 * GW].rearrange("p (k i) -> p k i", k=GT)
        att = c.arena[:, EX_AT + 2 * GW:EX_AT + 3 * GW]
        at = EX_AT + 3 * GW
        fT = c.arena[:, at:at + 3 * IN].rearrange("p (b i) -> p b i", b=3)
        assert at + 3 * IN <= ARENA
        at = LOGITS_AT + J * X
        den = c.arena[:, at:at + GT * H]
        st = c.arena[:, at + 64:at + 64 + GT * 6].rearrange("p (k s) -> p k s", k=GT)
        mv = c.arena[:, at + 128:at + 128 + 5 * GT].rearrange("p (s k) -> p s k", k=GT)
        mv2 = c.arena[:, at + 192:at + 192 + 5 * GT].rearrange("p (s k) -> p s k", k=GT)
        st2 = c.arena[:, at + 256:at + 256 + GT * 6].rearrange("p (k s) -> p k s", k=GT)
        sd, rs, sdb, rsb = (c.arena[:, at + 320 + 8 * n:at + 320 + 8 * n + GT] for n in range(4))
        ps = c.psum
        LG = 3
        bank = lambda k: 2 if k == GT - 1 else k % 2
        block = ctx.enter_context(nc.Block())

        @block.sync
        def _(sp):
            with sp.Fori(0, GROUPS) as i:
                sp.wait_ge(x2_stored, i * 16 + 16)
                sp.wait_ge(f_made, i * GT + GT)
                sp.dma_start(xg, d.x[ds(i * (GT * P), GT * P), :].rearrange("(k p) i -> p k i", p=P)).then_inc(x_loaded, 16)
                sp.wait_ge(x2_made, i + 1)
                sp.dma_start(d.out[ds(i * (GT * P), GT * P), :].rearrange("(k p) i -> p k i", p=P), xg).then_inc(x2_stored, 16)
            sp.wait_ge(x2_stored, 16 * GROUPS + 16)

        @block.scalar
        def _(act):
            act.dma_start(c.arena[:, B1_AT:B1_AT + B1_WORDS], d.b1.rearrange("e n -> (e n)").partition_broadcast(P)).then_inc(c.w1_loaded, 16)
            with act.Fori(0, GROUPS) as i:
                act.wait_ge(var1, i + 1)
                nc.scalar.activation(sd, mv[:, 3, :], ACT.Sqrt, bias=c.eps[:, :], scale=1.0 / IN).then_inc(sd1, 1)
                act.wait_ge(var2, i + 1)
                nc.scalar.activation(sdb, mv2[:, 3, :], ACT.Sqrt, bias=c.eps[:, :], scale=1.0 / IN).then_inc(sd2, 1)
                for k in range(GT):
                    act.wait_ge(fT_made, i * GT + (k + 1))
                    act.wait_ge(logits_made, i * GT + (k + 1))
                    nc.scalar.copy(fT[:, bank(k), :], ps[:, bank(k), 0:IN]).then_inc(fT_copied, 1)

        @block.tensor
        def _(pe):
            pe.sem_inc(logits_made, 2)

            def turn(i, k):
                pe.wait_ge(f_made, i * GT + (GT + k + 1))
                pe.wait_ge(fT_copied, i * GT + (k + 1))
                for m in range(KH):
                    last = nc.tensor.transpose(ps[:, bank(k), m * P:(m + 1) * P], f[:, k, m * P:(m + 1) * P], c.ident[:, :])
                last.then_inc(fT_made, 1)

            with pe.Fori(0, GROUPS) as i:
                turn(i, 0)
                for k in range(GT):
                    if k + 1 < GT:
                        turn(i, k + 1)
                    pe.wait_ge(fT_copied, i * GT + (k + 3))
                    for m in range(KH):
                        last = nc.tensor.matmul(ps[:, LG, ds((i * GT + k) * X, X)], fT[:, bank(k), m * P:(m + 1) * P], c.wr[:, m, :],
                                                start=(m == 0), stop=(m == KH - 1))
                    last.then_inc(logits_made, 1)

        @block.vector
        def _(dve):
            dve.sem_inc(x2_stored, 16)
            dve.sem_inc(f_made, GT)
            dve.sem_inc(fT_copied, 2)
            with dve.Fori(0, GROUPS) as i:
                sums = acc[:, ds(i * (GT * HW), GT * HW)].rearrange("p (q f) -> p q f", f=D + 1)
                nc.vector.tensor_scalar(den, sums[:, :, D], 1e-10, None, ALU.max).then_inc(den_step, 1)
                dve.wait_ge(den_step, i * 4 + 1)
                nc.vector.reciprocal(den, den).then_inc(den_step, 1)
                dve.wait_ge(den_step, i * 4 + 2)
                nc.vector.tensor_tensor(att.rearrange("p (q f) -> p q f", f=D), sums[:, :, 0:D],
                                        den.unsqueeze(2).to_broadcast([P, GT * H, D]), ALU.mult).then_inc(den_step, 1)
                dve.wait_ge(den_step, i * 4 + 3)
                att_k = att.rearrange("p (k i) -> p k i", k=GT)
                nc.vector.tensor_tensor(att_k, att_k, c.gnn_bias[:, :].unsqueeze(1).to_broadcast([P, GT, IN]), ALU.add).then_inc(den_step, 1)
                dve.wait_ge(den_step, i * 4 + 4)
                dve.wait_ge(x_loaded, i * 16 + 16)
                nc.vector.tensor_tensor(xg, xg, att_k, ALU.add).then_inc(x2_made, 1)
                dve.wait_ge(x2_made, i + 1)
                for k in range(GT):
                    nc.vector.bn_stats(st[:, k, :], xg[:, k, :]).then_inc(stats1, 1)
                dve.wait_ge(stats1, i * GT + GT)
                merge_stats(nc, dve, st, mv, i, merged1, var1)
                dve.wait_ge(sd1, i + 1)
                nc.vector.reciprocal(rs, sd).then_inc(rs1, 1)
                dve.wait_ge(rs1, i + 1)
                dve.wait_ge(fT_copied, i * GT + 2)
                for k in range(GT):
                    nc.vector.tensor_scalar(f[:, k, :], xg[:, k, :], mv[:, 4, k:k + 1], rs[:, k:k + 1], ALU.subtract, ALU.mult).then_inc(f_made, 1)
                for k in range(GT):
                    dve.wait_ge(f_made, i * GT + (GT + k + 1))
                    nc.vector.bn_stats(st2[:, k, :], f[:, k, :]).then_inc(stats2, 1)
                dve.wait_ge(stats2, i * GT + GT)
                merge_stats(nc, dve, st2, mv2, i, merged2, var2)
                dve.wait_ge(sd2, i + 1)
                nc.vector.reciprocal(rsb, sdb).then_inc(rs2, 1)
                dve.wait_ge(rs2, i + 1)
                for k in range(GT):
                    nc.vector.tensor_scalar(acc[:, ds((i * GT + k) * HW, IN)], f[:, k, :], mv2[:, 4, k:k + 1], rsb[:, k:k + 1],
                                            ALU.subtract, ALU.mult).then_inc(xn_made, 1)
            dve.wait_ge(logits_made, J + 2)
            nc.vector.tensor_tensor(logits.rearrange("p (j e) -> p j e", e=X), ps[:, LG, 0:J * X].rearrange("p (j e) -> p j e", e=X),
                                    c.br[:, :].unsqueeze(1).to_broadcast([P, J, X]), ALU.add).then_inc(logits_copied, 1)
            dve.wait_ge(logits_copied, 1)


def route(nc, c, d):
    with ExitStack() as ctx:
        (b_made, b_added) = semaphores(nc, ctx, "r_bm", "r_ba")
        (iotas, step, p_made, ranks, tables, scattered) = semaphores(nc, ctx, "r_iotas", "r_step", "r_p", "r_ranks", "r_tables", "r_scattered")
        acc = c.arena[:, W2_AT:W2_AT + J * HW]
        logits = c.arena[:, LOGITS_AT:LOGITS_AT + J * X]
        C = J * X
        at = EX_AT

        def take(n):
            nonlocal at
            at += n
            assert at <= EX_AT + EX_WORDS
            return c.arena[:, at - n:at]

        same, score_, oh1, oh2, rest, total, before, tile_of = (take(C) for _ in range(8))
        top1, pick1, top2, pick2, gap, gate_sum = (take(J) for _ in range(6))
        rev, tiles, upto, offset, count = (take(X) for _ in range(5))
        tile_start = take(J)
        tile_id = take(XS_TILES)
        many = take(XS_TILES * X)
        place = take(TOPK * J)
        jx = lambda ap: ap.rearrange("p (j e) -> p j e", e=X)
        over_x = lambda ap: ap.unsqueeze(2).to_broadcast([P, J, X])
        over_j = lambda ap: ap.unsqueeze(1).to_broadcast([P, J, X])
        gate1, gate2 = take(J), take(J)
        w1 = c.arena[:, W1_AT:W1_AT + W1_WORDS].rearrange("p (k e n) -> p k e n", k=KH, e=X)
        b1 = c.arena[:, B1_AT:B1_AT + B1_WORDS]
        BIASES = [(e, b) for e in range(X) for b in range(HID // 512)]
        ps = c.psum
        block = ctx.enter_context(nc.Block())

        @block.gpsimd
        def _(pool):
            ia = dict(allow_small_or_imprecise_dtypes=True)
            pool.iota(rev, [[-1, X]], base=X, channel_multiplier=0, **ia).then_inc(iotas, 1)
            pool.iota(tile_start, [[P, J]], base=0, channel_multiplier=0, **ia).then_inc(iotas, 1)
            pool.iota(tile_id, [[1, XS_TILES]], base=0, channel_multiplier=0, **ia).then_inc(iotas, 1)
            for k in range(TOPK):
                pool.wait_ge(tables, k + 1)
                for j in range(J):
                    pool.indirect_dma_start(d.xs[:, :], bass.IndirectOffsetOnAxis(ap=c.pos_i[:, k * J + j:k * J + j + 1], axis=0),
                                            acc[:, j * HW:j * HW + XW], None).then_inc(scattered, 16)
                pool.wait_ge(scattered, 16 * J * (k + 1))

        @block.scalar
        def _(act):
            act.wait_ge(step, 12)
            nc.scalar.activation(gap, gap, ACT.Exp).then_inc(p_made, 1)

        @block.tensor
        def _(pe):
            pe.wait_ge(step, 13)
            nc.tensor.matmul(ps[:, 0, 0:C], c.tri[:, :], total, start=True, stop=True)
            nc.tensor.matmul(ps[:, 1, 0:C], c.ones[:, :], total, start=True, stop=True).then_inc(ranks, 1)
            pe.wait_ge(c.w1_loaded, 16 * (X + 1))
            for n, (e, b) in enumerate(BIASES):
                if n >= 4:
                    pe.wait_ge(b_added, n - 3)
                for k in range(KH):
                    last = nc.tensor.matmul(ps[:, 4 + n % 4, :], c.ln_b[:, k, e:e + 1].to_broadcast([P, P]), w1[:, k, e, b * 512:(b + 1) * 512],
                                            start=(k == 0), stop=(k == KH - 1))
                last.then_inc(b_made, 1)

        @block.vector
        def _(dve):
            def choose(values, top, pick, onehot, n):
                nc.vector.tensor_reduce(top, jx(values), AX.X, ALU.max).then_inc(step, 1)
                dve.wait_ge(step, n + 1)
                nc.vector.tensor_tensor(jx(same), jx(values), over_x(top), ALU.is_equal).then_inc(step, 1)
                dve.wait_ge(step, n + 2)
                nc.vector.tensor_tensor(jx(score_), jx(same), over_j(rev), ALU.mult).then_inc(step, 1)
                dve.wait_ge(step, n + 3)
                nc.vector.tensor_reduce(pick, jx(score_), AX.X, ALU.max).then_inc(step, 1)
                dve.wait_ge(step, n + 4)
                nc.vector.tensor_tensor(jx(onehot), over_j(rev), over_x(pick), ALU.is_equal).then_inc(step, 1)
                dve.wait_ge(step, n + 5)

            dve.wait_ge(iotas, 3)
            choose(logits, top1, pick1, oh1, 0)
            nc.vector.scalar_tensor_tensor(rest, oh1, -3.0e38, logits, ALU.mult, ALU.add).then_inc(step, 1)
            dve.wait_ge(step, 6)
            choose(rest, top2, pick2, oh2, 6)
            nc.vector.tensor_tensor(gap, top2, top1, ALU.subtract).then_inc(step, 1)
            nc.vector.tensor_tensor(total, oh1, oh2, ALU.add).then_inc(step, 1)
            dve.wait_ge(p_made, 1)
            nc.vector.tensor_scalar(gate_sum, gap, 1.0, None, ALU.add).then_inc(step, 1)
            dve.wait_ge(step, 14)
            nc.vector.reciprocal(gate1, gate_sum).then_inc(step, 1)
            dve.wait_ge(step, 15)
            nc.vector.tensor_tensor(gate2, gap, gate1, ALU.mult).then_inc(step, 1)
            dve.wait_ge(ranks, 1)
            for e in range(X):
                nc.vector.tensor_tensor_scan(before[:, e:C:X], c.ones[:, 0:J], ps[:, 1, e:C:X], 0.0, ALU.mult, ALU.add).then_inc(step, 1)
            dve.wait_ge(step, 24)
            nc.vector.tensor_copy(count, before[:, (J - 1) * X:C]).then_inc(step, 1)
            dve.wait_ge(step, 25)
            nc.vector.tensor_tensor(before, before, ps[:, 1, 0:C], ALU.subtract).then_inc(step, 1)
            m = tile_of.rearrange("p (e j) -> p e j", e=X)
            nc.vector.tensor_tensor(m, count.unsqueeze(2).to_broadcast([P, X, J]), tile_start.unsqueeze(1).to_broadcast([P, X, J]),
                                    ALU.is_gt).then_inc(step, 1)
            dve.wait_ge(step, 27)
            nc.vector.tensor_reduce(tiles, m, AX.X, ALU.add).then_inc(step, 1)
            dve.wait_ge(step, 28)
            nc.vector.tensor_tensor_scan(upto, c.ones[:, 0:X], tiles, 0.0, ALU.mult, ALU.add).then_inc(step, 1)
            dve.wait_ge(step, 29)
            nc.vector.tensor_tensor(offset, upto, tiles, ALU.subtract).then_inc(step, 1)
            u = many.rearrange("p (u e) -> p u e", e=X)
            nc.vector.tensor_tensor(u, tile_id.unsqueeze(2).to_broadcast([P, XS_TILES, X]), upto.unsqueeze(1).to_broadcast([P, XS_TILES, X]),
                                    ALU.is_ge).then_inc(step, 1)
            dve.wait_ge(step, 31)
            nc.vector.tensor_scalar(offset, offset, float(P), None, ALU.mult).then_inc(step, 1)
            nc.vector.tensor_reduce(tile_id, u, AX.X, ALU.add).then_inc(step, 1)
            nc.vector.tensor_tensor(before, before, ps[:, 0, 0:C], ALU.add).then_inc(step, 1)
            dve.wait_ge(step, 34)
            nc.vector.tensor_scalar(c.tile_e[:, :], tile_id[0:1, :], float(X - 1), None, ALU.min).then_inc(step, 1)
            nc.vector.tensor_tensor(jx(before), jx(before), over_j(offset), ALU.add).then_inc(step, 1)
            dve.wait_ge(step, 36)
            nc.vector.tensor_tensor(oh1, oh1, before, ALU.mult).then_inc(step, 1)
            nc.vector.tensor_tensor(oh2, oh2, before, ALU.mult).then_inc(step, 1)
            dve.wait_ge(step, 38)
            nc.vector.tensor_reduce(place[:, 0:J], jx(oh1), AX.X, ALU.add).then_inc(step, 1)
            nc.vector.tensor_reduce(place[:, J:2 * J], jx(oh2), AX.X, ALU.add).then_inc(step, 1)
            dve.wait_ge(step, 40)
            nc.vector.tensor_copy(c.pos_i[:, :], place)
            nc.vector.tensor_scalar(acc.bitcast(I32)[:, IN:J * HW:HW], tile_start, c.iota_p[:, :], None, ALU.add)
            nc.vector.tensor_copy(acc[:, IN + 1:J * HW:HW], gate1).then_inc(tables, 1)
            for n, (e, b) in enumerate(BIASES):
                part = b1[:, e * HID + b * 512:e * HID + (b + 1) * 512]
                dve.wait_ge(b_made, n + 1)
                nc.vector.tensor_tensor(part, part, ps[:, 4 + n % 4, :], ALU.add).then_inc(b_added, 1)
            dve.wait_ge(b_added, len(BIASES))
            dve.wait_ge(scattered, 16 * J)
            nc.vector.tensor_copy(acc[:, IN + 1:J * HW:HW], gate2).then_inc(tables, 1)


def experts_of(nc, row, engine):
    _, values = nc.values_load_multi_w_load_instructions(
        row, engines=(engine,), min_val=0, max_val=X - 1, skip_runtime_bounds_check_because="route caps the table at X - 1")
    return values


def experts(nc, c, d):
    with ExitStack() as ctx:
        (x_loaded0, x_loaded1, b2_loaded, xT_made, xT_copied, up_done, pre_made, preT_made, gelu_done, down_done, sum_made, y_made, gate_done) = semaphores(
            nc, ctx, "e_x0", "e_x1", "e_b2", "e_xT", "e_xTc", "e_up", "e_pre", "e_preT", "e_gelu", "e_down", "e_sum", "e_y", "e_gate")
        meta_loaded, y_stored = semaphores(nc, ctx, "e_meta0", "e_meta1"), semaphores(nc, ctx, "e_yst0", "e_yst1")
        x_loaded = (x_loaded0, x_loaded1)
        w1 = c.arena[:, W1_AT:W1_AT + W1_WORDS]
        w2 = c.arena[:, W2_AT:W2_AT + W2_WORDS]
        b1 = c.arena[:, B1_AT:B1_AT + B1_WORDS]
        HC = HID // P
        at = EX_AT

        def take(n):
            nonlocal at
            at += n
            assert at <= EX_AT + EX_WORDS
            return c.arena[:, at - n:at]

        pre = take(HID)
        hT = take(HID)
        b2 = take(X * IN)
        xt = take(2 * IN).rearrange("p (b i) -> p b i", b=2)
        meta = take(4).rearrange("p (b i) -> p b i", b=2)
        xT = take(2 * IN).rearrange("p (b i) -> p b i", b=2)
        y = take(2 * IN).rearrange("p (b i) -> p b i", b=2)
        ps = c.psum
        UP, PRET, DOWN, XT = 0, 2, 4, 6
        PAIRS = MOE_TILES // 2
        block = ctx.enter_context(nc.Block())

        @block.sync
        def _(sp):
            sp.dma_start(b2, d.b2.rearrange("e n -> (e n)").partition_broadcast(P)).then_inc(b2_loaded, 16)
            for b in range(2):
                sp.dma_start(xt[:, b, :], d.xs[b * P:(b + 1) * P, 0:IN]).then_inc(x_loaded[b], 16)
            for e in range(X):
                sp.dma_start(w2.rearrange("p (h e n) -> p h e n", e=X, n=IN)[:, :, e, :],
                             d.W2[e].rearrange("(h p) n -> p h n", p=P)).then_inc(c.w2_loaded, 16)
            with sp.Fori(0, PAIRS) as i:
                for b in range(2):
                    sp.wait_ge(xT_made, i * 2 + (b + 1))
                    sp.dma_start(xt[:, b, :], d.xs[ds((i * 2 + (2 + b)) * P, P), 0:IN]).then_inc(x_loaded[b], 16)
                    sp.wait_ge(gate_done, i * 2 + (b + 1))
                    with nc.allow_non_contiguous_dma(reason="two words of each row"):
                        sp.dma_start(meta[:, b, :], d.xs[ds((i * 2 + b) * P, P), IN:XW]).then_inc(meta_loaded[b], 16)
            for b in range(2):
                sp.wait_ge(x_loaded[b], 16 * (PAIRS + 1))

        @block.gpsimd
        def _(pool):
            pool.sem_inc(gate_done, 1)

            def add_rows(i, b):
                pool.wait_ge(y_made, i * 2 + (b + 1))
                if b:
                    pool.wait_ge(y_stored[0], i * 16 + 16)
                elif not isinstance(i, int):
                    pool.wait_ge(y_stored[1], i * 16)
                pool.wait_ge(gate_done, i * 2 + (b + 1))
                nc.gpsimd.tensor_tensor(c.gate[:, :], c.ones[0:1, 0:1], c.ones[0:1, 0:1], ALU.add).then_inc(gate_done, 1)
                pool.indirect_dma_start(d.out[:, :], bass.IndirectOffsetOnAxis(ap=meta[:, b, 0:1].bitcast(I32), axis=0), y[:, b, :], None,
                                        compute_op=ALU.add).then_inc(y_stored[b], 16)

            add_rows(0, 0)
            add_rows(0, 1)
            with pool.Fori(1, PAIRS) as i:
                for b in range(2):
                    add_rows(i, b)
            for b in range(2):
                pool.wait_ge(y_stored[b], 16 * PAIRS)

        @block.tensor
        def _(pe):
            def turn_rows(n, b):
                for m in range(KH):
                    last = nc.tensor.transpose(ps[:, XT + b, m * P:(m + 1) * P], xt[:, b, m * P:(m + 1) * P], c.ident[:, :])
                last.then_inc(xT_made, 1)

            def up(e, b):
                for n in range(HID // 512):
                    for m in range(KH):
                        last = nc.tensor.matmul(ps[:, UP + n, :], xT[:, b, m * P:(m + 1) * P], w1[:, ds(e * HID + (m * X * HID + n * 512), 512)],
                                                start=(m == 0), stop=(m == KH - 1))
                last.then_inc(up_done, 1)

            pe.wait_ge(x_loaded[0], 16)
            turn_rows(0, 0)
            pe.wait_ge(x_loaded[1], 16)
            turn_rows(1, 1)
            pe.wait_ge(xT_copied, 1)
            up(pe.value_load(c.tile_e[0:1, 0:1], min_val=0, max_val=X - 1), 0)
            pe.wait_ge(c.w2_loaded, 16 * X)
            with pe.Fori(0, PAIRS) as i:
                for b in range(2):
                    e_now, e_next = experts_of(nc, c.tile_e[0:1, ds(i * 2 + b, 2)], mybir.EngineType.PE)
                    pe.wait_ge(pre_made, i * 2 + (b + 1))
                    for h in range(HC):
                        last = nc.tensor.transpose(ps[:, PRET + h // 4, h % 4 * P:(h % 4 + 1) * P], pre[:, h * P:(h + 1) * P], c.ident[:, :])
                        if h % 4 == 3:
                            last.then_inc(preT_made, 1)
                    pe.wait_ge(xT_copied, i * 2 + (b + 2))
                    up(e_next, 1 - b)
                    pe.wait_ge(x_loaded[b], i * 16 + 32)
                    pe.wait_ge(xT_copied, i * 2 + (b + 1))
                    turn_rows(0, b)
                    pe.wait_ge(gelu_done, i * 4 + (2 * b + 2))
                    pe.wait_ge(y_made, i * 2 + (b + 1) - 1) if b else None
                    for h in range(HC):
                        last = nc.tensor.matmul(ps[:, DOWN + b, 0:IN], hT[:, h * P:(h + 1) * P], w2[:, ds(e_now * IN + h * X * IN, IN)],
                                                start=(h == 0), stop=(h == HC - 1))
                    last.then_inc(down_done, 1)

        @block.scalar
        def _(act):
            with act.Fori(0, PAIRS) as i:
                for b in range(2):
                    for n in range(2):
                        act.wait_ge(preT_made, i * 4 + (2 * b + n + 1))
                        nc.scalar.activation(hT[:, n * 512:(n + 1) * 512], ps[:, PRET + n, :], ACT.Gelu).then_inc(gelu_done, 1)

        @block.vector
        def _(dve):
            def bias(n, e):
                for q in range(2):
                    part = slice(q * 512, (q + 1) * 512)
                    last = nc.vector.tensor_tensor(pre[:, part], ps[:, UP + q, :], b1[:, ds(e * HID + q * 512, 512)], ALU.add)
                last.then_inc(pre_made, 1)

            def scale(b, e):
                for m in range(KH):
                    last = nc.vector.tensor_scalar(xT[:, b, m * P:(m + 1) * P], ps[:, XT + b, m * P:(m + 1) * P], c.ln_g[:, m, ds(e, 1)], None,
                                                   ALU.mult)
                last.then_inc(xT_copied, 1)

            for b in range(2):
                dve.wait_ge(xT_made, b + 1)
                scale(b, dve.value_load(c.tile_e[0:1, b:b + 1], min_val=0, max_val=X - 1))
            dve.wait_ge(b2_loaded, 16)
            dve.wait_ge(up_done, 1)
            bias(0, dve.value_load(c.tile_e[0:1, 0:1], min_val=0, max_val=X - 1))
            with dve.Fori(0, PAIRS) as i:
                for b in range(2):
                    e_now, e_next, e_after = experts_of(nc, c.tile_e[0:1, ds(i * 2 + b, 3)], mybir.EngineType.DVE)
                    dve.wait_ge(up_done, i * 2 + (b + 2))
                    bias(0, e_next)
                    dve.wait_ge(xT_made, i * 2 + (b + 3))
                    scale(b, e_after)
                    dve.wait_ge(down_done, i * 2 + (b + 1))
                    dve.wait_ge(meta_loaded[b], i * 16 + 16)
                    nc.vector.tensor_tensor(y[:, b, :], ps[:, DOWN + b, 0:IN], b2[:, ds(e_now * IN, IN)], ALU.add).then_inc(sum_made, 1)
                    dve.wait_ge(sum_made, i * 2 + (b + 1))
                    nc.vector.tensor_scalar(y[:, b, :], y[:, b, :], meta[:, b, 1:2], None, ALU.mult).then_inc(y_made, 1)


STAGES = [prepare, score, softmax, aggregate, attend, route, experts]


def program(nc, d):
    c = Chip()
    with ExitStack() as ctx:
        def sb(name, shape, dt=F32):
            return ctx.enter_context(nc.sbuf_tensor(name, shape, dt))

        c.arena = sb("arena", [P, ARENA])
        c.psum = ctx.enter_context(nc.psum_tensor("psum", [P, 8, 512], F32))
        c.iota_row = sb("iota_row", [P, P])
        c.iota_p = sb("iota_p", [P, 1])
        c.ident = sb("ident", [P, P])
        c.tri = sb("tri", [P, P])
        c.ones = sb("ones", [P, P])
        c.eps = sb("eps", [P, 1])
        c.ew = sb("ew", [P, HW])
        c.src = sb("src", [P, SLOTS], I32)
        c.rel = sb("rel", [P, SLOTS])
        c.slot_j = sb("slot_j", [1, SG * P], I32)
        c.gnn_bias = sb("gnn_bias", [P, HD])
        c.wr = sb("wr", [P, KH, X])
        c.br = sb("br", [P, X])
        c.ln_g = sb("ln_g", [P, KH, X])
        c.ln_b = sb("ln_b", [P, KH, X])
        c.idx = sb("idx", [P, 2, R], I32)
        c.gate = sb("gate", [1, 1])
        c.pos_i = sb("pos_i", [P, TOPK * J], I32)
        c.tile_e = sb("tile_e", [1, XS_TILES], I32)
        (c.consts_ready, c.alpha_sum, c.w1_loaded, c.w2_loaded) = semaphores(nc, ctx, "consts_ready", "m_alphasum", "w1_loaded", "w2_loaded")
        d.h_tab = nc.dram_tensor("h_tab", [NP, HW], F32)
        d.s_tab = nc.dram_tensor("s_tab", [NP, H], F32)
        d.slot_j = nc.dram_tensor("slot_j_list", [SG * P], I32)
        d.rel = nc.dram_tensor("rel_list", [SG * P, P], F32)
        d.ea_slots = nc.dram_tensor("ea_slots", [EF + 1, SG * P, P], F32)
        d.xs = nc.dram_tensor("xs", [XS_TILES * P, XW], F32)
        d.ends = nc.dram_tensor("ends", [P, CH * 4], F32).ap()
        d.joined = nc.dram_tensor("joined", [P, CH * 2], F32).ap()
        for stage in STAGES:
            stage(nc, c, d)


def kernel(**inputs):
    import numpy as np
    import concourse.bacc as bacc
    from concourse.bass_utils import run_bass_kernel_spmd as run

    f = np.float32
    x = np.concatenate([np.asarray(inputs["x"]), np.zeros((NP - N, IN), f)])
    src = np.concatenate([np.asarray(inputs["src"]), np.zeros(EP - E, np.int32)])
    dst = np.concatenate([np.asarray(inputs["dst"]), np.full(EP - E, NP - 1, np.int32)])
    ea = np.zeros((EF + 1, EP), f)
    ea[:EF, :E] = np.asarray(inputs["edge_attr_3"]).T
    ea[EF] = 1.0
    W = np.ascontiguousarray(inputs["L0_gnn_W"])
    a_bd = np.zeros((H, D, 2, H), f)
    for h in range(H):
        a_bd[h, :, 0, h] = inputs["L0_gnn_a_src"][h]
        a_bd[h, :, 1, h] = inputs["L0_gnn_a_dst"][h]
    ew = np.zeros((EF + 1, H, D + 1), f)
    ew[:EF, :, :D] = np.asarray(inputs["L0_gnn_edge_W"]).T.reshape(EF, H, D)
    ew[EF, :, :D] = np.asarray(inputs["L0_gnn_edge_b"]).reshape(H, D)
    ew[EF, :, D] = 1.0
    arrays = {
        "x": x, "src_rows": src.reshape(T, P), "dst_rows": dst.reshape(T, P),
        "ea_rows": ea.reshape(EF + 1, T, P).swapaxes(0, 1).reshape(T, (EF + 1) * P), "W": W, "WT": W.T, "a_bd": a_bd.reshape(HD, 2 * H), "ew": ew.reshape(EF + 1, HW),
        "gnn_bias": inputs["L0_gnn_bias"], "Wr": inputs["L0_ffn_Wr"], "br": inputs["L0_ffn_br"],
        "ln_gT": np.asarray(inputs["L0_ffn_ln_g"]).T, "ln_bT": np.asarray(inputs["L0_ffn_ln_b"]).T,
        "W1": inputs["L0_ffn_W1"], "b1": inputs["L0_ffn_b1"], "W2": inputs["L0_ffn_W2"], "b2": inputs["L0_ffn_b2"],
    }
    arrays = {k: np.ascontiguousarray(v) for k, v in arrays.items()}

    class Dram:
        pass

    nc = bacc.Bacc("TRN2", target_bir_lowering=False, num_devices=1)
    d = Dram()
    for name, a in arrays.items():
        d.__dict__[name] = nc.dram_tensor(f"in_{name}", a.shape, mybir.dt.from_np(a.dtype), kind="ExternalInput").ap()
    d.out = nc.dram_tensor("out_rows", (NP + P, IN), F32, kind="ExternalOutput").ap()
    program(nc, d)
    r = run(nc, [{f"in_{k}": v for k, v in arrays.items()}], core_ids=[0])
    return r.results[0]["out_rows"][:N]
```

```python
from contextlib import ExitStack

import concourse.bass as bass
from concourse import mybir

F32 = mybir.dt.float32
I32 = mybir.dt.int32
ALU = mybir.AluOpType
ACT = mybir.ActivationFunctionType
AX = mybir.AxisListType
ds = bass.ds

P = 128
N, IN, H, D, EF, E = 6250, 256, 8, 32, 3, 100000
X, HID, TOPK = 8, 1024, 2
HD = H * D
KH = IN // P
HW = H * (D + 1)
HS = HW + H
J = -(-N // P)
NP = J * P
GT = 7
GROUPS = J // GT
CT = 16
SLOTS = -(-(-(-E // P) + J - 1) // CT) * CT
T = SLOTS - J + 1
CH = SLOTS // CT
EP = T * P
R = 8
TURNS = SLOTS // R
SG = -(-SLOTS // P)
MOE_TILES = (TOPK * NP + X * (P - 1)) // P
MOE_TILES += MOE_TILES % 2
XS_TILES = MOE_TILES + 2
AHEAD = 3
LIST_TILES = MOE_TILES + AHEAD + 1
LN_EPS = 1e-5
BIG = 1.5e38
FLAT = CH * P
CHAIN = SLOTS * 2
assert GROUPS * GT == J and TURNS * R == SLOTS

W1_AT = 0
W1_WORDS = KH * X * HID
W2_AT = W1_AT + W1_WORDS
W2_WORDS = HID // P * X * IN
B1_AT = W2_AT + W2_WORDS
B1_WORDS = X * HID
EX_AT = B1_AT + B1_WORDS
EX_WORDS = SLOTS * H
ARENA = EX_AT + EX_WORDS
LOGITS_AT = ARENA - J * X


SRC_TILES_AT = EX_AT + 4 * R * P
SLOT_T_AT = SRC_TILES_AT + T + R
assert SLOT_T_AT + SLOTS <= ARENA


class Chip:
    pass


def semaphores(nc, ctx, *names):
    return [ctx.enter_context(nc.semaphore(n)) for n in names]


def merge_stats(nc, dve, st, mv, turn, merged, var_made):
    nc.vector.tensor_tensor(mv[:, 0, :], st[:, :, 1], st[:, :, 4], ALU.add).then_inc(merged, 1)
    nc.vector.tensor_tensor(mv[:, 1, :], st[:, :, 1], st[:, :, 4], ALU.subtract).then_inc(merged, 1)
    nc.vector.tensor_tensor(mv[:, 2, :], st[:, :, 2], st[:, :, 5], ALU.add).then_inc(merged, 1)
    dve.wait_ge(merged, turn * 4 + 2)
    nc.vector.tensor_tensor(mv[:, 1, :], mv[:, 1, :], mv[:, 1, :], ALU.mult).then_inc(merged, 1)
    nc.vector.tensor_scalar(mv[:, 4, :], mv[:, 0, :], 0.5, None, ALU.mult)
    dve.wait_ge(merged, turn * 4 + 4)
    nc.vector.scalar_tensor_tensor(mv[:, 3, :], mv[:, 1, :], IN / 4.0, mv[:, 2, :], ALU.mult, ALU.add).then_inc(var_made, 1)


def prepare(nc, c, d):
    with ExitStack() as ctx:
        (consts_made, zeros_made, w_loaded, small_loaded, hi_loaded, hi_tile_made, hi_row_made, val_in_psum, below_made, counted,
         t_capped, j_made, t_made, t_stored, t_loaded, wa_made, wa_copied, stats, merged, var_made, sd_made, rs_made, xn_made,
         xT_made, xT_copied, h_made, h_copied, rows_stored, zeros_stored, ew_zeroed, tiles_gathered, rel_made, src_made, turned,
         turned_back, lists_stored) = semaphores(
            nc, ctx, "p_consts", "p_zeros", "p_w", "p_small", "p_hi", "p_hitile", "p_hirow", "p_val", "p_below", "p_counted",
            "p_tcap", "p_j", "p_tmade", "p_tstored", "p_tloaded", "p_wa", "p_wacopied", "p_stats", "p_merged", "p_var", "p_sd", "p_rs",
            "p_xn", "p_xT", "p_xTcopied", "p_h", "p_hcopied", "p_stored", "p_zerost", "p_ewzero", "p_tilegat", "p_rel", "p_srcf",
            "p_turned", "p_back", "p_lists")
        x_loaded = semaphores(nc, ctx, *[f"p_x{i}" for i in range(GROUPS)])

        class Region:

            def __init__(self, start, end):
                self.at, self.end = start, end

            def take(self, n, rows=slice(0, P)):
                self.at += n
                assert self.at <= self.end
                return c.arena[rows, self.at - n:self.at]

        in_w1, in_w2, in_b1, in_ex = Region(W1_AT, W2_AT), Region(W2_AT, B1_AT), Region(B1_AT, EX_AT), Region(EX_AT, ARENA)
        row = slice(0, 1)
        h_all = in_w1.take(J * HW)
        hi_row, hi_tile, iota_t, val_row = (in_w1.take(T, row) for _ in range(4))
        x_all = in_w2.take(J * IN)
        w_nat = in_w2.take(KH * IN).rearrange("p (k i) -> p k i", k=KH)
        a_bd = in_w2.take(KH * 2 * H).rearrange("p (k h) -> p k h", k=KH)
        rhs_h = in_w2.take(KH * HS).rearrange("p (k n) -> p k n", k=KH)
        zeros = in_w2.take(IN)
        below = in_w2.take(T)
        slot_id, t_col, t_col_i, t_at_i, j_col, j_col_i = (in_w2.take(SG) for _ in range(6))
        st = in_w2.take(GT * 6).rearrange("p (k s) -> p k s", k=GT)
        mv = in_w2.take(5 * GT).rearrange("p (s k) -> p s k", k=GT)
        sd, rs = in_w2.take(GT), in_w2.take(GT)
        dst_rows, src_rows, rel, src_f, ea_rows = (in_b1.take(SG * n).rearrange("p (g e) -> p g e", g=SG) for n in (P, P, P, P, (EF + 1) * P))
        assert EX_AT + 4 * R * P <= in_ex.end
        xn = in_ex.take(GT * IN).rearrange("p (k i) -> p k i", k=GT)
        xT = in_ex.take(3 * IN).rearrange("p (b i) -> p b i", b=3)
        s_all = in_ex.take(J * H)
        assert in_ex.at <= SRC_TILES_AT
        eps = c.eps
        ps = c.psum
        XT, HB, VAL, WA = 0, 3, 6, 7
        WA_COL = T // 2
        bank = lambda k: 2 if k == GT - 1 else k % 2
        block = ctx.enter_context(nc.Block())

        @block.gpsimd
        def _(pool):
            ia = dict(allow_small_or_imprecise_dtypes=True)
            pool.iota(c.iota_row[:, :], [[1, P]], base=0, channel_multiplier=0, **ia).then_inc(consts_made, 1)
            pool.iota(c.iota_p[:, :], [[0, 1]], base=0, channel_multiplier=1, **ia).then_inc(consts_made, 1)
            pool.memset(eps[:, :], LN_EPS).then_inc(consts_made, 1)
            pool.memset(c.ones[:, :], 1.0).then_inc(consts_made, 1)
            pool.iota(iota_t, [[1, T]], base=0, channel_multiplier=0, **ia).then_inc(consts_made, 1)
            pool.iota(slot_id, [[P, SG]], base=0, channel_multiplier=1, **ia).then_inc(consts_made, 1)
            pool.wait_ge(t_made, 3)
            for g in range(SG):
                for rows, table in ((dst_rows, d.dst_rows), (src_rows, d.src_rows), (ea_rows, d.ea_rows)):
                    rows = rows[:, g, :] if rows is ea_rows else rows[:, g, :].bitcast(I32)
                    pool.indirect_dma_start(rows, None, table, bass.IndirectOffsetOnAxis(ap=t_col_i[:, g:g + 1].bitcast(I32), axis=0)
                                            ).then_inc(tiles_gathered, 16)

        @block.sync
        def _(sp):
            with nc.allow_non_contiguous_dma(reason="last target of each edge tile"):
                sp.dma_start(hi_row.bitcast(I32), d.dst_rows.rearrange("t e -> e t")[P - 1:P, :]).then_inc(hi_loaded, 16)
            for i in range(GROUPS):
                sp.dma_start(x_all[:, i * GT * IN:(i + 1) * GT * IN].rearrange("p (k i) -> p k i", k=GT), d.x[i * GT * P:(i + 1) * GT * P, :].rearrange("(k p) i -> p k i", p=P)
                             ).then_inc(x_loaded[i], 16)
            sp.wait_ge(zeros_made, 1)
            sp.dma_start(d.xn[NP:NP + P, :], zeros).then_inc(zeros_stored, 16)
            sp.dma_start(d.out[NP:NP + P, :], zeros).then_inc(zeros_stored, 16)
            sp.dma_start(d.gates[TOPK * NP:TOPK * (NP + P), :].rearrange("(p k) n -> p (k n)", k=TOPK), zeros[:, 0:TOPK]).then_inc(zeros_stored, 16)
            sp.wait_ge(t_made, 3)
            with nc.allow_non_contiguous_dma(reason="column to row"):
                sp.dma_start(d.slot_t.rearrange("(g p) -> p g", p=P), t_at_i.bitcast(I32)).then_inc(t_stored, 16)
                sp.dma_start(d.slot_j.rearrange("(g p) -> p g", p=P), j_col_i.bitcast(I32)).then_inc(t_stored, 16)
            sp.wait_ge(t_stored, 32)
            sp.dma_start(c.slot_t, d.slot_t[0:SLOTS].rearrange("(a s) -> a s", a=1)).then_inc(t_loaded, 16)
            sp.dma_start(c.slot_j[:, :], d.slot_j.rearrange("(a s) -> a s", a=1)).then_inc(t_loaded, 16)
            def tables(i):
                sp.wait_ge(h_copied, i * GT + (GT + 2))
                sp.dma_start(d.h_tab[ds(i * (GT * P), GT * P), :].rearrange("(k p) n -> p k n", p=P),
                             h_all[:, ds(i * (GT * HW), GT * HW)].rearrange("p (k n) -> p k n", k=GT)).then_inc(rows_stored, 16)
                sp.dma_start(d.s_tab[ds(i * (GT * P), GT * P), :].rearrange("(k p) n -> p k n", p=P),
                             s_all[:, ds(i * (GT * H), GT * H)].rearrange("p (k n) -> p k n", k=GT)).then_inc(rows_stored, 16)

            with sp.Fori(0, GROUPS - 1) as i:
                tables(i)
            sp.wait_ge(rel_made, 1)
            sp.dma_start(d.rel.rearrange("(g p) e -> p g e", p=P), rel).then_inc(lists_stored, 16)
            sp.wait_ge(tiles_gathered, 16 * 3 * SG)
            for g in range(SG):
                sp.dma_start(d.ea_slots[:, g * P:(g + 1) * P, :].rearrange("f p e -> p f e"),
                             ea_rows[:, g, :].rearrange("p (f e) -> p f e", f=EF + 1)).then_inc(lists_stored, 16)
            tables(GROUPS - 1)
            sp.wait_ge(lists_stored, 16 * (SG + 1))
            sp.wait_ge(rows_stored, 32 * GROUPS)
            sp.wait_ge(t_loaded, 32)
            sp.wait_ge(small_loaded, 16 * 7)
            sp.wait_ge(zeros_stored, 48)

        @block.scalar
        def _(act):
            act.sem_inc(h_copied, 2)
            act.dma_start(w_nat, d.W.rearrange("(k p) i -> p k i", p=P)).then_inc(w_loaded, 16)
            act.dma_start(a_bd, d.a_bd.rearrange("(k p) h -> p k h", p=P)).then_inc(w_loaded, 16)
            for k in range(KH):
                act.dma_start(rhs_h[:, k, 0:HW].rearrange("p (h f) -> p h f", f=D + 1)[:, :, 0:D],
                              d.WT[k * P:(k + 1) * P, :].rearrange("p (h f) -> p h f", f=D)).then_inc(w_loaded, 16)
            act.wait_ge(ew_zeroed, 1)
            act.dma_start(c.ew[0:EF + 1, :], d.ew).then_inc(small_loaded, 16)
            act.dma_start(c.src_tiles, d.src_cols).then_inc(small_loaded, 16)
            act.dma_start(c.gnn_bias[:, :], d.gnn_bias.partition_broadcast(P)).then_inc(small_loaded, 16)
            act.dma_start(c.wr[:, :, :], d.Wr.rearrange("(k p) e -> p k e", p=P)).then_inc(small_loaded, 16)
            act.dma_start(c.br[:, :], d.br.partition_broadcast(P)).then_inc(small_loaded, 16)
            act.dma_start(c.ln_g[:, :, :], d.ln_gT.rearrange("(k p) e -> p k e", p=P)).then_inc(small_loaded, 16)
            act.dma_start(c.ln_b[:, :, :], d.ln_bT.rearrange("(k p) e -> p k e", p=P)).then_inc(small_loaded, 16)

            def deviation(i):
                act.wait_ge(var_made, i + 1)
                nc.scalar.activation(sd, mv[:, 3, :], ACT.Sqrt, bias=eps[:, :], scale=1.0 / IN).then_inc(sd_made, 1)

            def take_xT(i, k):
                act.wait_ge(xT_made, i * GT + (k + 1))
                act.wait_ge(h_made, i * GT + (k + 1))
                nc.scalar.copy(xT[:, bank(k), :], ps[:, XT + bank(k), 0:IN]).then_inc(xT_copied, 1)

            def take_h(i, k):
                act.wait_ge(h_made, i * GT + (k + 3))
                nc.scalar.copy(h_all[:, ds((i * GT + k) * HW, HW)], ps[:, HB + bank(k), 0:HW])
                nc.scalar.copy(s_all[:, ds((i * GT + k) * H, H)], ps[:, HB + bank(k), HW:HS]).then_inc(h_copied, 1)

            def group(i, after):
                for k in range(GT):
                    if k + 1 < GT:
                        take_xT(i, k + 1)
                    elif after is not None:
                        take_xT(after, 0)
                    take_h(i, k)

            deviation(0)
            take_xT(0, 0)
            with act.Fori(0, GROUPS - 1) as i:
                deviation(i + 1)
                group(i, i + 1)
            group(GROUPS - 1, None)

        @block.tensor
        def _(pe):
            pe.sem_inc(h_made, 2)
            pe.wait_ge(w_loaded, 16 * (2 + KH))
            for k in range(KH):
                for m in range(KH):
                    last = nc.tensor.matmul(ps[:, WA, WA_COL + k * 2 * H:WA_COL + (k + 1) * 2 * H], w_nat[:, m, k * P:(k + 1) * P], a_bd[:, m, :],
                                            start=(m == 0), stop=(m == KH - 1))
            last.then_inc(wa_made, 1)
            pe.wait_ge(wa_copied, 2)
            pe.wait_ge(hi_row_made, 1)
            for b in range(2):
                last = nc.tensor.matmul(ps[:, VAL + b, 0:T // 2], c.ones[0:1, 0:P], val_row[:, b * (T // 2):(b + 1) * (T // 2)],
                                        start=True, stop=True)
            last.then_inc(val_in_psum, 1)
            pe.wait_ge(c.consts_ready, 2)

            def turn(i, k):
                pe.wait_ge(xn_made, i * GT + (k + 1))
                pe.wait_ge(xT_copied, i * GT + (k + 1))
                for m in range(KH):
                    last = nc.tensor.transpose(ps[:, XT + bank(k), m * P:(m + 1) * P], xn[:, k, m * P:(m + 1) * P], c.ident[:, :])
                last.then_inc(xT_made, 1)

            def project(i, k):
                pe.wait_ge(xT_copied, i * GT + (k + 3))
                pe.wait_ge(h_copied, i * GT + (k + 1))
                for m in range(KH):
                    last = nc.tensor.matmul(ps[:, HB + bank(k), 0:HS], xT[:, bank(k), m * P:(m + 1) * P], rhs_h[:, m, :],
                                            start=(m == 0), stop=(m == KH - 1))
                last.then_inc(h_made, 1)

            def group(i, after):
                for k in range(GT):
                    if k + 1 < GT:
                        turn(i, k + 1)
                    elif after is not None:
                        turn(after, 0)
                    project(i, k)

            turn(0, 0)
            with pe.Fori(0, GROUPS - 1) as i:
                group(i, i + 1)
            group(GROUPS - 1, None)
            for n, (rows, made) in enumerate(((rel, rel_made), (src_f, src_made))):
                pe.wait_ge(made, 1)
                for g in range(SG):
                    if g in (0, 4) and n:
                        pe.wait_ge(turned_back, g // 4 + 1)
                    last = nc.tensor.transpose(ps[:, VAL + g // 4, g % 4 * P:(g % 4 + 1) * P], rows[:, g, :], c.ident[:, :])
                    if g in (3, SG - 1):
                        last.then_inc(turned, 1)

        @block.vector
        def _(dve):
            dve.sem_inc(xT_copied, 2)
            nc.vector.memset(c.ew[:, :], 0.0).then_inc(ew_zeroed, 1)
            nc.vector.memset(zeros, 0.0).then_inc(zeros_made, 1)
            dve.wait_ge(consts_made, 6)
            nc.vector.tensor_scalar(c.ident[:, :], c.iota_row[:, :], c.iota_p[:, :], None, ALU.is_equal).then_inc(c.consts_ready, 1)
            nc.vector.tensor_scalar(c.tri[:, :], c.iota_row[:, :], c.iota_p[:, :], None, ALU.is_gt).then_inc(c.consts_ready, 1)
            dve.wait_ge(hi_loaded, 16)
            nc.vector.tensor_scalar(hi_tile.bitcast(I32), hi_row.bitcast(I32), 7, None, ALU.logical_shift_right).then_inc(hi_tile_made, 1)
            dve.wait_ge(hi_tile_made, 1)
            nc.vector.tensor_tensor(val_row, hi_tile.bitcast(I32), iota_t, ALU.add).then_inc(hi_row_made, 1)

            def statistics(i):
                for k in range(GT):
                    nc.vector.bn_stats(st[:, k, :], x_all[:, ds((i * GT + k) * IN, IN)]).then_inc(stats, 1)
                dve.wait_ge(stats, i * GT + GT)
                merge_stats(nc, dve, st, mv, i, merged, var_made)
                dve.wait_ge(sd_made, i + 1)
                nc.vector.reciprocal(rs, sd).then_inc(rs_made, 1)
                dve.wait_ge(rs_made, i + 1)

            def normalise(i, k):
                nc.vector.tensor_scalar(xn[:, k, :], x_all[:, ds((i * GT + k) * IN, IN)], mv[:, 4, k:k + 1],
                                        rs[:, k:k + 1], ALU.subtract, ALU.mult).then_inc(xn_made, 1)

            dve.wait_ge(x_loaded[0], 16)
            statistics(0)
            for k in range(GT):
                normalise(0, k)

            def next_group(i):
                statistics(i + 1)
                for k in range(GT):
                    dve.wait_ge(xT_made, i * GT + (k + 1))
                    normalise(i + 1, k)

            dve.wait_ge(wa_made, 1)
            wa = ps[:, WA, WA_COL:WA_COL + KH * 2 * H].rearrange("p (k s h) -> p k s h", k=KH, s=2)
            nc.vector.tensor_copy(rhs_h[:, :, HW:HS], wa[:, :, 0, :]).then_inc(wa_copied, 1)
            nc.vector.tensor_copy(rhs_h[:, :, D:HW:D + 1], wa[:, :, 1, :]).then_inc(wa_copied, 1)
            dve.wait_ge(x_loaded[1], 16)
            next_group(0)
            dve.wait_ge(val_in_psum, 1)
            for g in range(SG):
                if g:
                    dve.wait_ge(counted, g)
                nc.vector.tensor_scalar(below.rearrange("p (b t) -> p b t", b=2), ps[:, VAL:VAL + 2, 0:T // 2], slot_id[:, g:g + 1], None,
                                        ALU.is_lt).then_inc(below_made, 1)
                dve.wait_ge(below_made, g + 1)
                nc.vector.tensor_reduce(t_col[:, g:g + 1], below, AX.X, ALU.add).then_inc(counted, 1)
            dve.wait_ge(counted, SG)
            nc.vector.tensor_scalar(t_col, t_col, float(T - 1), None, ALU.min).then_inc(t_capped, 1)
            dve.wait_ge(t_capped, 1)
            nc.vector.tensor_tensor(j_col, slot_id, t_col, ALU.subtract).then_inc(j_made, 1)
            nc.vector.tensor_copy(t_col_i.bitcast(I32), t_col).then_inc(t_made, 1)
            nc.vector.tensor_scalar(t_at_i.bitcast(I32), t_col, float(H), None, ALU.mult).then_inc(t_made, 1)
            dve.wait_ge(j_made, 1)
            nc.vector.tensor_scalar(j_col_i.bitcast(I32), j_col, float(HW), None, ALU.mult).then_inc(t_made, 1)
            nc.vector.tensor_scalar(j_col, j_col, float(P), None, ALU.mult).then_inc(j_made, 1)
            for i in range(2, GROUPS):
                dve.wait_ge(x_loaded[i], 16)
            with dve.Fori(1, GROUPS - 1) as i:
                next_group(i)
            dve.wait_ge(tiles_gathered, 16 * 3 * SG)
            dve.wait_ge(j_made, 2)
            nc.vector.tensor_tensor(rel, dst_rows.bitcast(I32), j_col.unsqueeze(2).to_broadcast([P, SG, P]), ALU.subtract).then_inc(rel_made, 1)
            nc.vector.tensor_copy(src_f, src_rows.bitcast(I32)).then_inc(src_made, 1)
            for n, cols in enumerate((c.rel, c.src)):
                for q in range(2):
                    dve.wait_ge(turned, 2 * n + q + 1)
                    slots = slice(q * 4 * P, min((q + 1) * 4 * P, SLOTS))
                    nc.vector.tensor_copy(cols[:, slots], ps[:, VAL + q, 0:slots.stop - slots.start]).then_inc(turned_back, 1)
            dve.wait_ge(turned_back, 4)


def load_words(nc, row, engine, most=(J - 1) * HW):
    _, values = nc.values_load_multi_w_load_instructions(
        row, engines=(engine,), min_val=0, max_val=most,
        skip_runtime_bounds_check_because="t(s) is capped at T - 1, and s - t(s) lies from 0 to J - 1 as targets lie below N")
    return values


def score(nc, c, d):
    with ExitStack() as ctx:
        (prod_done, red_done, sum_done, relu_done, enc_done, hd_done, oht_done, gate_done, idx_copied, spread) = semaphores(
            nc, ctx, "s_prod", "s_red", "s_sum", "s_relu", "s_enc", "s_hd", "s_oht", "s_gate", "s_idx", "s_spread")
        (ea_zeroed,) = semaphores(nc, ctx, "s_eazero")
        ea_loaded = semaphores(nc, ctx, "s_ea0", "s_ea1")
        rel_loaded = semaphores(nc, ctx, "s_rel0", "s_rel1")
        gathered = semaphores(nc, ctx, "s_gat0", "s_gat1")
        PR = R // 2

        a_all = c.arena[:, W2_AT:W2_AT + SLOTS * H]
        h_all = c.arena[:, W1_AT:W1_AT + J * HW]
        at = W2_AT + SLOTS * H

        def take(n):
            nonlocal at
            at += n
            assert at <= B1_AT
            return c.arena[:, at - n:at]

        renc = take(4 * HW).rearrange("p (b s n) -> p b s n", b=2, s=2)
        prod = take(4 * HW).rearrange("p (b s n) -> p b s n", b=2, s=2)
        red = take(2 * R * H).rearrange("p (b n) -> p b n", b=2)
        gat = take(2 * R * H).rearrange("p (b k n) -> p b k n", b=2, k=R)
        s_src = take(T * H)
        EDGE_TURNS = T // R
        EDGE_STEPS, STEPS = EDGE_TURNS // 2, TURNS // 2
        relb = c.arena[:, EX_AT:EX_AT + 2 * R * P].rearrange("p (b k e) -> p b k e", b=2, k=R)
        oht = c.arena[:, EX_AT + 2 * R * P:EX_AT + 4 * R * P].rearrange("p (b k e) -> p b k e", b=2, k=R)
        ea = c.arena[:, B1_AT:B1_AT + 2 * R * P].rearrange("p (b k e) -> p b k e", b=2, k=R)
        ps = c.psum
        block = ctx.enter_context(nc.Block())

        @block.sync
        def _(sp):
            sp.wait_ge(ea_zeroed, 1)
            sp.dma_start(relb[:, 0, :, :], d.rel[0:R, :].partition_broadcast(P)).then_inc(rel_loaded[0], 16)
            with sp.Fori(0, TURNS // 2) as i:
                for b in range(2):
                    sp.wait_ge(enc_done, i * (2 * PR) + (b + 1) * PR)
                    sp.dma_start(ea[0:EF + 1, b, :, :], d.ea_slots[:, ds(i * (2 * R) + b * R, R), :]).then_inc(ea_loaded[b], 16)
                    sp.wait_ge(oht_done, i * 2 + (b + 2))
                    sp.dma_start(relb[:, 1 - b, :, :], d.rel[ds(i * (2 * R) + (b + 1) * R, R), :].partition_broadcast(P)).then_inc(rel_loaded[1 - b], 16)

        @block.gpsimd
        def _(pool):
            pool.sem_inc(gate_done, 1)
            with pool.Fori(0, EDGE_STEPS) as i:
                for b in range(2):
                    pool.wait_ge(idx_copied, i * 2 + (b + 1))
                    pool.wait_ge(gate_done, i * 2 + (b + 1))
                    nc.gpsimd.tensor_tensor(c.gate[:, :], c.ones[0:1, 0:1], c.ones[0:1, 0:1], ALU.add).then_inc(gate_done, 1)
                    for k in range(R):
                        pool.indirect_dma_start(gat[:, b, k, :], None, d.s_tab[:, :],
                                                bass.IndirectOffsetOnAxis(ap=c.idx[:, b, k:k + 1], axis=0)).then_inc(gathered[b], 16)

        @block.scalar
        def _(act):
            act.sem_inc(relu_done, 2)

            def indices(i, b):
                nc.scalar.copy(c.idx[:, b, :], c.src_tiles[:, ds(i * (2 * R) + b * R, R)]).then_inc(idx_copied, 1)

            def take_rows(i, b):
                act.wait_ge(gathered[b], i * (16 * R) + 16 * R)
                nc.scalar.copy(s_src[:, ds(i * (2 * R * H) + b * R * H, R * H)], gat[:, b, :, :].rearrange("p k n -> p (k n)")).then_inc(spread, 1)

            def relu(i, n):
                b0 = n % 2 * 2
                act.wait_ge(prod_done, i * (2 * PR) + (n + 1))
                act.wait_ge(enc_done, i * (2 * PR) + (2 * PR + n + 1))
                nc.scalar.activation(renc[:, n % 2, :, :], ps[:, b0:b0 + 2, 0:HW], ACT.Relu).then_inc(relu_done, 1)

            def step(i, beside):
                for n in range(2 * PR):
                    relu(i, n)
                    if n % PR == PR // 2 - 1:
                        beside(i, n // PR)

            def first(i, b):
                if b:
                    take_rows(0, 0)
                    indices(1, 0)

            def before(i, b):
                take_rows(i if b else i - 1, 1 - b)
                indices(i if not b else i + 1, 1 - b)

            def last(i, b):
                if not b:
                    take_rows(EDGE_STEPS - 1, 1)

            assert EDGE_TURNS % 2 == 0 and EDGE_STEPS < STEPS
            indices(0, 0)
            indices(0, 1)
            step(0, first)
            with act.Fori(1, EDGE_STEPS) as i:
                step(i, before)
            step(EDGE_STEPS, last)
            with act.Fori(EDGE_STEPS + 1, STEPS) as i:
                step(i, lambda i, b: None)
            act.wait_ge(idx_copied, EDGE_TURNS + 1)

        @block.tensor
        def _(pe):
            pe.sem_inc(enc_done, 2 * PR)
            pe.sem_inc(hd_done, 2)
            with pe.Fori(0, TURNS // 2) as i:
                for b in range(2):
                    js = load_words(nc, c.slot_j[0:1, ds(i * (2 * R) + b * R, R)], mybir.EngineType.PE)
                    pe.wait_ge(ea_loaded[b], i * 16 + 16)
                    for q in range(PR):
                        b0 = q % 2 * 2
                        pe.wait_ge(relu_done, i * (2 * PR) + (b * PR + q + 1))
                        for k in range(2):
                            last = nc.tensor.matmul(ps[:, b0 + k, 0:HW], ea[:, b, 2 * q + k, :], c.ew[:, :], start=True, stop=True)
                        last.then_inc(enc_done, 1)
                        if q == 0:
                            pe.wait_ge(oht_done, i * 2 + (b + 3))
                        pe.wait_ge(prod_done, i * (2 * PR) + (b * PR + q + 1))
                        for k in range(2):
                            last = nc.tensor.matmul(ps[:, 4 + b0 + k, 0:HW], oht[:, b, 2 * q + k, :], h_all[:, ds(js[2 * q + k], HW)],
                                                    start=True, stop=True)
                        last.then_inc(hd_done, 1)

        @block.vector
        def _(dve):
            nc.vector.memset(ea, 0.0).then_inc(ea_zeroed, 1)
            dve.sem_inc(prod_done, 2)
            dve.sem_inc(oht_done, 2)
            dve.sem_inc(red_done, 2)
            dve.sem_inc(sum_done, 2)

            def select(b, loads):
                dve.wait_ge(rel_loaded[b], loads * 16)
                nc.vector.tensor_scalar(oht[:, b, :, :], relb[:, b, :, :], c.iota_p[:, :], None, ALU.is_equal).then_inc(oht_done, 1)

            def add_rows(i, b, tiles):
                ts = load_words(nc, c.slot_t[0:1, ds(i * (2 * R) + b * R, R)], mybir.EngineType.DVE, (T - 1) * H)
                dve.wait_ge(spread, tiles)
                dve.wait_ge(red_done, i * (2 * PR) + ((b + 1) * PR + 2))
                for k in range(R):
                    last = nc.vector.tensor_tensor(a_all[:, ds(i * (2 * R * H) + (b * R + k) * H, H)], red[:, b, k * H:(k + 1) * H],
                                                   s_src[:, ds(ts[k], H)], ALU.add)
                last.then_inc(sum_done, 1)

            def step(i, tiles):
                for b in range(2):
                    for q in range(PR):
                        n = b * PR + q
                        dve.wait_ge(relu_done, i * (2 * PR) + (n + 3))
                        dve.wait_ge(hd_done, i * (2 * PR) + (n + 3))
                        dve.wait_ge(red_done, i * (2 * PR) + (n + 1))
                        nc.vector.tensor_tensor(prod[:, q % 2, :, :], renc[:, q % 2, :, :], ps[:, 4 + q % 2 * 2:6 + q % 2 * 2, 0:HW],
                                                ALU.mult).then_inc(prod_done, 1)
                        if q == 1:
                            select(1 - b, i + 1 + b)
                        dve.wait_ge(prod_done, i * (2 * PR) + (n + 3))
                        if q == 0:
                            dve.wait_ge(sum_done, i * 2 + (b + 1))
                        nc.vector.tensor_reduce(red[:, b, 2 * q * H:(2 * q + 2) * H], prod[:, q % 2, :, :].rearrange("p s (h f) -> p (s h) f", f=D + 1),
                                                AX.X, ALU.add).then_inc(red_done, 1)
                        if q == 1 and (b or not isinstance(i, int)):
                            add_rows(i if b else i - 1, 1 - b, tiles(i, b))

            select(0, 1)
            step(0, lambda i, b: 1)
            with dve.Fori(1, EDGE_STEPS) as i:
                step(i, lambda i, b: i * 2 + b)
            with dve.Fori(EDGE_STEPS, STEPS) as i:
                step(i, lambda i, b: EDGE_TURNS)
            add_rows(STEPS - 1, 1, EDGE_TURNS)
            dve.wait_ge(sum_done, 2 + TURNS)


def softmax(nc, c, d):
    with ExitStack() as ctx:
        (dst_loaded, step, ends_out, ends_in, joined_out, joined_in, flipped, taken, alpha_made, shifted, exp_done,
         back, ex_stored, by_head_made, chain_cut, zeroed) = semaphores(
            nc, ctx, "m_dst", "m_step", "m_endsout", "m_endsin", "m_joinedout", "m_joinedin", "m_flipped", "m_taken",
            "m_alpha", "m_shifted", "m_exp", "m_back", "m_exstored", "m_byhead", "m_chaincut", "m_zeroed")
        a = c.arena[:, W2_AT:W2_AT + FLAT]
        s = c.arena[:, EX_AT:EX_AT + FLAT]
        alpha = c.arena[:, W1_AT:W1_AT + FLAT]
        link = c.arena[:, W1_AT + FLAT:W1_AT + 2 * FLAT + 1]
        fwd = c.arena[:, B1_AT:B1_AT + FLAT]
        targets = fwd
        top = c.arena[:, W2_AT + FLAT:W2_AT + 2 * FLAT]
        ex = c.arena[:, EX_AT:EX_AT + FLAT]
        at = B1_AT + FLAT
        ends = c.arena[:, at:at + CH * 4].rearrange("p (v c k) -> p v c k", v=2, k=2)
        joined = c.arena[:, at + CH * 4:at + CH * 6].rearrange("p (c k) -> p c k", k=2)
        chain_link = c.arena[0:H, W2_AT + 2 * FLAT:W2_AT + 2 * FLAT + CHAIN + 1]
        chain_raw = c.arena[0:H, EX_AT:EX_AT + 2 * CHAIN]
        chain = c.arena[0:H, EX_AT + 2 * CHAIN:EX_AT + 3 * CHAIN]
        chain_dst = fwd[0:H, 0:CHAIN]
        chain_fwd = fwd[0:H, CHAIN:2 * CHAIN]
        chain_top = fwd[0:H, 2 * CHAIN:3 * CHAIN]
        chain_out = fwd[0:H, 3 * CHAIN:4 * CHAIN]
        ps = c.psum
        BANKC = 4
        fills = [range(g, min(g + BANKC, CH)) for g in range(0, CH, BANKC)]
        PARTS = 4
        PW = FLAT // PARTS
        block = ctx.enter_context(nc.Block())

        @block.sync
        def _(sp):
            for h in range(H):
                sp.dma_start(targets[h * CT:(h + 1) * CT, :].rearrange("t (c e) -> t c e", e=P),
                             d.rel[0:SLOTS, :].rearrange("(c t) e -> t c e", t=CT)).then_inc(dst_loaded, 16)
            sp.wait_ge(step, 10)
            sp.dma_start(d.ends, ends.rearrange("p v c k -> p (v c k)")).then_inc(ends_out, 16)
            sp.wait_ge(ends_out, 16)
            sp.dma_start(chain_raw, d.ends.rearrange("(h t) n -> h (t n)", h=H)).then_inc(ends_in, 16)
            sp.wait_ge(step, 17)
            sp.dma_start(d.joined.rearrange("(h t) n -> h (t n)", h=H), chain_out).then_inc(joined_out, 16)
            sp.wait_ge(joined_out, 16)
            sp.dma_start(joined.rearrange("p c k -> p (c k)"), d.joined).then_inc(joined_in, 16)
            sp.wait_ge(joined_in, 16)

        @block.gpsimd
        def _(pool):
            pool.wait_ge(by_head_made, PARTS)
            nc.gpsimd.memset(a, 0.0).then_inc(zeroed, 1)
            pool.wait_ge(shifted, len(fills))
            nc.gpsimd.memset(c.arena[:, W2_AT + FLAT:W2_AT + J * HW], 0.0).then_inc(zeroed, 1)
            pool.wait_ge(zeroed, 2)

        @block.tensor
        def _(pe):
            for g, chunks in enumerate(fills):
                pe.wait_ge(alpha_made, min(-(-(chunks[-1] + 1) * P // PW), PARTS))
                if g >= 8:
                    pe.wait_ge(taken, g - 7)
                for n, ch in enumerate(chunks):
                    last = nc.tensor.transpose(ps[:, g % 8, n * P:(n + 1) * P],
                                               s[:, ch * P:(ch + 1) * P], c.ident[:, :])
                last.then_inc(flipped, 1)
            for g, chunks in enumerate(fills):
                pe.wait_ge(exp_done, g + 1)
                if g >= 8:
                    pe.wait_ge(ex_stored, g - 7)
                for n, ch in enumerate(chunks):
                    last = nc.tensor.transpose(ps[:, g % 8, n * P:(n + 1) * P], fwd[:, ch * P:(ch + 1) * P], c.ident[:, :])
                last.then_inc(back, 1)

        @block.scalar
        def _(act):
            by_head = dict(t=CT, h=H)
            for n in range(PARTS):
                cols = slice(n * PW, (n + 1) * PW)
                nc.scalar.copy(alpha[:, cols].rearrange("p (c h t) -> p c h t", **by_head),
                               a[:, cols].rearrange("p (c t h) -> p c h t", **by_head)).then_inc(by_head_made, 1)
            for g, chunks in enumerate(fills):
                act.wait_ge(flipped, g + 1)
                nc.scalar.copy(alpha[:, chunks[0] * P:(chunks[-1] + 1) * P], ps[:, g % 8, 0:len(chunks) * P]).then_inc(taken, 1)
            for g, chunks in enumerate(fills):
                part = fwd[:, chunks[0] * P:(chunks[-1] + 1) * P]
                act.wait_ge(shifted, g + 1)
                nc.scalar.activation(part, part, ACT.Exp).then_inc(exp_done, 1)

        @block.vector
        def _(dve):
            for n in range(PARTS):
                cols = slice(n * PW, (n + 1) * PW)
                dve.wait_ge(by_head_made, n + 1)
                nc.vector.scalar_tensor_tensor(s[:, cols], alpha[:, cols], 0.2, alpha[:, cols], ALU.mult, ALU.max).then_inc(alpha_made, 1)
            dve.wait_ge(dst_loaded, 16 * H)
            nc.vector.tensor_tensor(link[:, 1:FLAT], targets[:, 1:FLAT], targets[:, 0:FLAT - 1], ALU.is_equal).then_inc(step, 1)
            nc.vector.tensor_copy(ends[:, 1, :, 0], targets[:, 0:FLAT:P]).then_inc(step, 1)
            nc.vector.tensor_copy(ends[:, 1, :, 1], targets[:, P - 1:FLAT:P]).then_inc(step, 1)
            dve.wait_ge(step, 3)
            nc.vector.tensor_scalar(link[:, 1:FLAT], link[:, 1:FLAT], -0.5, 2 * BIG, ALU.add, ALU.mult).then_inc(step, 1)
            dve.wait_ge(step, 4)
            nc.vector.memset(link[:, 0:FLAT:P], -BIG).then_inc(step, 1)
            nc.vector.memset(link[:, FLAT:FLAT + 1], -BIG).then_inc(step, 1)
            dve.wait_ge(step, 6)
            dve.wait_ge(taken, len(fills))
            nc.vector.tensor_tensor_scan(fwd, link[:, 0:FLAT], alpha, -BIG, ALU.min, ALU.max).then_inc(step, 1)
            dve.wait_ge(step, 7)
            nc.vector.tensor_tensor_scan(top[:, ::-1], link[:, 1:FLAT + 1][:, ::-1], fwd[:, ::-1], -BIG, ALU.min, ALU.max).then_inc(step, 1)
            dve.wait_ge(step, 8)
            nc.vector.tensor_copy(ends[:, 0, :, 0], top[:, 0:FLAT:P]).then_inc(step, 1)
            nc.vector.tensor_copy(ends[:, 0, :, 1], top[:, P - 1:FLAT:P]).then_inc(step, 1)
            dve.wait_ge(ends_in, 16)
            raw = chain_raw.rearrange("h (t v c k) -> h v c t k", t=CT, v=2, k=2)
            order = dict(c=CH, t=CT, k=2)
            nc.vector.tensor_copy(chain.rearrange("h (c t k) -> h c t k", **order), raw[:, 0]).then_inc(step, 1)
            nc.vector.tensor_copy(chain_dst.rearrange("h (c t k) -> h c t k", **order), raw[:, 1]).then_inc(step, 1)
            nc.vector.memset(chain_link[:, 0:CHAIN + 1:CHAIN], -BIG).then_inc(chain_cut, 1)
            dve.wait_ge(step, 12)
            nc.vector.tensor_tensor(chain_link[:, 1:CHAIN], chain_dst[:, 1:CHAIN], chain_dst[:, 0:CHAIN - 1], ALU.is_equal).then_inc(step, 1)
            dve.wait_ge(step, 13)
            nc.vector.tensor_scalar(chain_link[:, 1:CHAIN], chain_link[:, 1:CHAIN], -0.5, 2 * BIG, ALU.add, ALU.mult).then_inc(step, 1)
            dve.wait_ge(step, 14)
            dve.wait_ge(chain_cut, 1)
            nc.vector.tensor_tensor_scan(chain_fwd, chain_link[:, 0:CHAIN], chain, -BIG, ALU.min, ALU.max).then_inc(step, 1)
            dve.wait_ge(step, 15)
            nc.vector.tensor_tensor_scan(chain_top[:, ::-1], chain_link[:, 1:CHAIN + 1][:, ::-1], chain_fwd[:, ::-1], -BIG, ALU.min,
                                         ALU.max).then_inc(step, 1)
            dve.wait_ge(step, 16)
            nc.vector.tensor_copy(chain_out.rearrange("h (t c k) -> h c t k", **order),
                                  chain_top.rearrange("h (c t k) -> h c t k", **order)).then_inc(step, 1)
            dve.wait_ge(joined_in, 16)
            nc.vector.tensor_copy(top[:, 0:FLAT:P], joined[:, :, 0]).then_inc(step, 1)
            nc.vector.tensor_copy(top[:, P - 1:FLAT:P], joined[:, :, 1]).then_inc(step, 1)
            dve.wait_ge(step, 19)
            nc.vector.tensor_tensor_scan(fwd, link[:, 0:FLAT], top, -BIG, ALU.min, ALU.max).then_inc(step, 1)
            dve.wait_ge(step, 20)
            nc.vector.tensor_tensor_scan(top[:, ::-1], link[:, 1:FLAT + 1][:, ::-1], fwd[:, ::-1], -BIG, ALU.min, ALU.max).then_inc(step, 1)
            dve.wait_ge(step, 21)
            for chunks in fills:
                cols = slice(chunks[0] * P, (chunks[-1] + 1) * P)
                nc.vector.tensor_tensor(fwd[:, cols], alpha[:, cols], top[:, cols], ALU.subtract).then_inc(shifted, 1)
            for g, chunks in enumerate(fills):
                dve.wait_ge(back, g + 1)
                n = len(chunks)
                nc.vector.tensor_copy(ex[:, chunks[0] * P:(chunks[-1] + 1) * P].rearrange("p (c t h) -> p c h t", c=n, h=H),
                                      ps[:, g % 8, 0:n * P].rearrange("p (c h t) -> p c h t", c=n, h=H)).then_inc(ex_stored, 1)


def aggregate(nc, c, d):
    with ExitStack() as ctx:
        (msg_done, den_done, sum_done, acc_done, gate_done, idx_copied) = semaphores(nc, ctx, "g_msg", "g_den", "g_sum", "g_acc", "g_gate", "g_idx")
        PR = R // 2
        gathered = semaphores(nc, ctx, *[f"g_gat{k}" for k in range(2 * PR)])
        acc = c.arena[:, W2_AT:W2_AT + J * HW]
        ex = c.arena[:, EX_AT:EX_AT + SLOTS * H]
        rows = c.arena[:, B1_AT:B1_AT + 2 * R * HW].rearrange("p (b k n) -> p b k n", b=2, k=R)
        oh = c.arena[:, W2_AT + J * HW:W2_AT + J * HW + 2 * R * P].rearrange("p (b k n) -> p b k n", b=2, k=R)
        w1 = c.arena[:, W1_AT:W1_AT + W1_WORDS].rearrange("p (k e n) -> p k e n", k=KH, e=X)
        ps = c.psum
        block = ctx.enter_context(nc.Block())

        @block.sync
        def _(sp):
            for e in range(X):
                sp.wait_ge(sum_done, 2 * PR + (e + 1) * 2 * PR)
                sp.dma_start(w1[:, :, e, :], d.W1[e].rearrange("(k p) n -> p k n", p=P)).then_inc(c.w1_loaded, 16)

        @block.gpsimd
        def _(pool):
            pool.sem_inc(gate_done, 1)
            with pool.Fori(0, TURNS // 2) as i:
                for b in range(2):
                    pool.wait_ge(idx_copied, i * 2 + (b + 1))
                    pool.wait_ge(sum_done, i * (2 * PR) + (b + 1) * PR)
                    pool.wait_ge(gate_done, i * 2 + (b + 1))
                    nc.gpsimd.tensor_tensor(c.gate[:, :], c.ones[0:1, 0:1], c.ones[0:1, 0:1], ALU.add).then_inc(gate_done, 1)
                    for k in range(R):
                        pool.indirect_dma_start(rows[:, b, k, :], None, d.h_tab[:, :],
                                                bass.IndirectOffsetOnAxis(ap=c.idx[:, b, k:k + 1], axis=0)).then_inc(gathered[b * PR + k // 2], 16)

        @block.scalar
        def _(act):
            def indices(i, b):
                nc.scalar.copy(c.idx[:, b, :], c.src[:, ds(i * (2 * R) + b * R, R)]).then_inc(idx_copied, 1)

            def weights(i, n):
                b, q = divmod(n, PR)
                act.wait_ge(gathered[n], i * 32 + 32)
                nc.scalar.copy(rows[:, b, 2 * q:2 * q + 2, D:HW:D + 1],
                               ex[:, ds(i * (2 * R * H) + 2 * n * H, 2 * H)].rearrange("p (k h) -> p k h", k=2)).then_inc(den_done, 1)

            indices(0, 0)
            indices(0, 1)
            with act.Fori(0, TURNS // 2 - 1) as i:
                for b in range(2):
                    for q in range(PR):
                        weights(i, b * PR + q)
                    indices(i + 1, b)
            for n in range(2 * PR):
                weights(TURNS // 2 - 1, n)

        @block.tensor
        def _(pe):
            pe.sem_inc(sum_done, 2 * PR)
            with pe.Fori(0, TURNS // 2) as i:
                for n in range(2 * PR):
                    b, q = divmod(n, PR)
                    pe.wait_ge(den_done, i * (2 * PR) + (n + 1))
                    pe.wait_ge(msg_done, i * (2 * PR) + (n + 1))
                    pe.wait_ge(acc_done, i * (4 * PR) + (2 * n + 2))
                    for k in range(2):
                        last = nc.tensor.matmul(ps[:, 2 * q + k, 0:HW], oh[:, b, 2 * q + k, :], rows[:, b, 2 * q + k, :], start=True, stop=True)
                    last.then_inc(sum_done, 1)

        @block.vector
        def _(dve):
            dve.sem_inc(acc_done, 8)
            STEPS, PAIRS = TURNS // 2, 2 * PR

            def one_hot(i, n):
                b, q = divmod(n, PR)
                dve.wait_ge(sum_done, i * PAIRS + (n + 1))
                nc.vector.tensor_tensor(oh[:, b, 2 * q:2 * q + 2, :], c.iota_row[:, :].unsqueeze(1).to_broadcast([P, 2, P]),
                                        c.rel[:, ds(i * (2 * R) + 2 * n, 2)].unsqueeze(2).to_broadcast([P, 2, P]), ALU.is_equal)

            def message(i, n):
                b, q = divmod(n, PR)
                dve.wait_ge(gathered[n], i * 32 + 32)
                row = rows[:, b, 2 * q:2 * q + 2, :].rearrange("p k (h f) -> p (k h) f", f=D + 1)[:, :, 0:D]
                nc.vector.tensor_tensor(row, row, ex[:, ds(i * (2 * R * H) + 2 * n * H, 2 * H)].unsqueeze(2).to_broadcast([P, 2 * H, D]),
                                        ALU.mult).then_inc(msg_done, 1)

            def take(i, n, k, j):
                if k == 0:
                    dve.wait_ge(sum_done, i * PAIRS + (PAIRS + n + 1))
                dve.wait_ge(acc_done, i * (2 * PAIRS) + (8 + 2 * n + k))
                a_j = acc[:, ds(j, HW)]
                nc.vector.tensor_tensor(a_j, a_j, ps[:, 2 * (n % PR) + k, 0:HW], ALU.add).then_inc(acc_done, 1)

            def step(i, then):
                for n in range(PAIRS):
                    if n % PR == 0:
                        js = load_words(nc, c.slot_j[0:1, ds(i * (2 * R) + 2 * n, R)], mybir.EngineType.DVE)
                    ahead = (i, n + LEAD) if n + LEAD < PAIRS else (then, n + LEAD - PAIRS)
                    if ahead[0] is not None:
                        one_hot(*ahead)
                    take(i, n, 0, js[2 * (n % PR)])
                    if ahead[0] is not None:
                        message(*ahead)
                    take(i, n, 1, js[2 * (n % PR) + 1])

            LEAD = 2
            for n in range(LEAD):
                one_hot(0, n)
                message(0, n)
            with dve.Fori(0, STEPS - 1) as i:
                step(i, i + 1)
            step(STEPS - 1, None)


def attend(nc, c, d):
    with ExitStack() as ctx:
        (x_loaded, x2_made, x2_stored, stats1, merged1, var1, sd1, rs1, f_made, stats2, merged2, var2, sd2, rs2, xn_made,
         fT_made, fT_copied, logits_made, logits_copied, den_step, xn_stored) = semaphores(
            nc, ctx, "t_x", "t_x2", "t_x2st", "t_st1", "t_mg1", "t_var1", "t_sd1", "t_rs1", "t_f", "t_st2", "t_mg2", "t_var2", "t_sd2",
            "t_rs2", "t_xn", "t_fT", "t_fTc", "t_lg", "t_lgc", "t_den", "t_xnst")
        acc = c.arena[:, W2_AT:W2_AT + J * HW]
        logits = c.arena[:, LOGITS_AT:LOGITS_AT + J * X]
        GW = GT * IN
        xg = c.arena[:, EX_AT:EX_AT + GW].rearrange("p (k i) -> p k i", k=GT)
        f = c.arena[:, EX_AT + GW:EX_AT + 2 * GW].rearrange("p (k i) -> p k i", k=GT)
        att = c.arena[:, EX_AT + 2 * GW:EX_AT + 3 * GW]
        at = EX_AT + 3 * GW
        fT = c.arena[:, at:at + 3 * IN].rearrange("p (b i) -> p b i", b=3)
        assert at + 3 * IN <= LOGITS_AT
        at = W2_AT + J * HW
        den = c.arena[:, at:at + GT * H]
        st = c.arena[:, at + 64:at + 64 + GT * 6].rearrange("p (k s) -> p k s", k=GT)
        mv = c.arena[:, at + 128:at + 128 + 5 * GT].rearrange("p (s k) -> p s k", k=GT)
        mv2 = c.arena[:, at + 192:at + 192 + 5 * GT].rearrange("p (s k) -> p s k", k=GT)
        st2 = c.arena[:, at + 256:at + 256 + GT * 6].rearrange("p (k s) -> p k s", k=GT)
        sd, rs, sdb, rsb = (c.arena[:, at + 320 + 8 * n:at + 320 + 8 * n + GT] for n in range(4))
        at = W2_AT + J * HW + 384
        xn = c.arena[:, at:at + GT * IN].rearrange("p (k i) -> p k i", k=GT)
        assert at + GT * IN <= B1_AT
        ps = c.psum
        LG = 3
        bank = lambda k: 2 if k == GT - 1 else k % 2
        block = ctx.enter_context(nc.Block())

        @block.sync
        def _(sp):
            with sp.Fori(0, GROUPS) as i:
                sp.wait_ge(x2_stored, i * 16 + 16)
                sp.wait_ge(f_made, i * GT + GT)
                sp.dma_start(xg, d.x[ds(i * (GT * P), GT * P), :].rearrange("(k p) i -> p k i", p=P)).then_inc(x_loaded, 16)
                sp.wait_ge(x2_made, i + 1)
                sp.dma_start(d.out[ds(i * (GT * P), GT * P), :].rearrange("(k p) i -> p k i", p=P), xg).then_inc(x2_stored, 16)
            sp.wait_ge(x2_stored, 16 * GROUPS + 16)

        @block.scalar
        def _(act):
            act.sem_inc(xn_stored, 16)
            act.dma_start(c.arena[:, B1_AT:B1_AT + B1_WORDS], d.b1.rearrange("e n -> (e n)").partition_broadcast(P)).then_inc(c.w1_loaded, 16)
            with act.Fori(0, GROUPS) as i:
                act.wait_ge(var1, i + 1)
                nc.scalar.activation(sd, mv[:, 3, :], ACT.Sqrt, bias=c.eps[:, :], scale=1.0 / IN).then_inc(sd1, 1)
                act.wait_ge(var2, i + 1)
                nc.scalar.activation(sdb, mv2[:, 3, :], ACT.Sqrt, bias=c.eps[:, :], scale=1.0 / IN).then_inc(sd2, 1)
                for k in range(GT):
                    act.wait_ge(fT_made, i * GT + (k + 1))
                    act.wait_ge(logits_made, i * GT + (k + 1))
                    nc.scalar.copy(fT[:, bank(k), :], ps[:, bank(k), 0:IN]).then_inc(fT_copied, 1)
                act.wait_ge(xn_made, i * GT + GT)
                act.dma_start(d.xn[ds(i * (GT * P), GT * P), :].rearrange("(k p) n -> p k n", p=P),
                              xn).then_inc(xn_stored, 16)
            act.wait_ge(xn_stored, 16 * GROUPS + 16)

        @block.tensor
        def _(pe):
            pe.sem_inc(logits_made, 2)

            def turn(i, k):
                pe.wait_ge(f_made, i * GT + (GT + k + 1))
                pe.wait_ge(fT_copied, i * GT + (k + 1))
                for m in range(KH):
                    last = nc.tensor.transpose(ps[:, bank(k), m * P:(m + 1) * P], f[:, k, m * P:(m + 1) * P], c.ident[:, :])
                last.then_inc(fT_made, 1)

            with pe.Fori(0, GROUPS) as i:
                turn(i, 0)
                for k in range(GT):
                    if k + 1 < GT:
                        turn(i, k + 1)
                    pe.wait_ge(fT_copied, i * GT + (k + 3))
                    for m in range(KH):
                        last = nc.tensor.matmul(ps[:, LG, ds((i * GT + k) * X, X)], fT[:, bank(k), m * P:(m + 1) * P], c.wr[:, m, :],
                                                start=(m == 0), stop=(m == KH - 1))
                    last.then_inc(logits_made, 1)

        @block.vector
        def _(dve):
            dve.sem_inc(x2_stored, 16)
            dve.sem_inc(f_made, GT)
            dve.sem_inc(fT_copied, 2)
            with dve.Fori(0, GROUPS) as i:
                sums = acc[:, ds(i * (GT * HW), GT * HW)].rearrange("p (q f) -> p q f", f=D + 1)
                nc.vector.tensor_scalar(den, sums[:, :, D], 1e-10, None, ALU.max).then_inc(den_step, 1)
                dve.wait_ge(den_step, i * 4 + 1)
                nc.vector.reciprocal(den, den).then_inc(den_step, 1)
                dve.wait_ge(den_step, i * 4 + 2)
                nc.vector.tensor_tensor(att.rearrange("p (q f) -> p q f", f=D), sums[:, :, 0:D],
                                        den.unsqueeze(2).to_broadcast([P, GT * H, D]), ALU.mult).then_inc(den_step, 1)
                dve.wait_ge(den_step, i * 4 + 3)
                att_k = att.rearrange("p (k i) -> p k i", k=GT)
                nc.vector.tensor_tensor(att_k, att_k, c.gnn_bias[:, :].unsqueeze(1).to_broadcast([P, GT, IN]), ALU.add).then_inc(den_step, 1)
                dve.wait_ge(den_step, i * 4 + 4)
                dve.wait_ge(x_loaded, i * 16 + 16)
                nc.vector.tensor_tensor(xg, xg, att_k, ALU.add).then_inc(x2_made, 1)
                dve.wait_ge(x2_made, i + 1)
                for k in range(GT):
                    nc.vector.bn_stats(st[:, k, :], xg[:, k, :]).then_inc(stats1, 1)
                dve.wait_ge(stats1, i * GT + GT)
                merge_stats(nc, dve, st, mv, i, merged1, var1)
                dve.wait_ge(sd1, i + 1)
                nc.vector.reciprocal(rs, sd).then_inc(rs1, 1)
                dve.wait_ge(rs1, i + 1)
                dve.wait_ge(fT_copied, i * GT + 2)
                for k in range(GT):
                    nc.vector.tensor_scalar(f[:, k, :], xg[:, k, :], mv[:, 4, k:k + 1], rs[:, k:k + 1], ALU.subtract, ALU.mult).then_inc(f_made, 1)
                for k in range(GT):
                    dve.wait_ge(f_made, i * GT + (GT + k + 1))
                    nc.vector.bn_stats(st2[:, k, :], f[:, k, :]).then_inc(stats2, 1)
                dve.wait_ge(stats2, i * GT + GT)
                merge_stats(nc, dve, st2, mv2, i, merged2, var2)
                dve.wait_ge(sd2, i + 1)
                nc.vector.reciprocal(rsb, sdb).then_inc(rs2, 1)
                dve.wait_ge(rs2, i + 1)
                dve.wait_ge(xn_stored, i * 16 + 16)
                for k in range(GT):
                    nc.vector.tensor_scalar(xn[:, k, :], f[:, k, :], mv2[:, 4, k:k + 1], rsb[:, k:k + 1], ALU.subtract, ALU.mult).then_inc(xn_made, 1)
            dve.wait_ge(logits_made, J + 2)
            nc.vector.tensor_tensor(logits.rearrange("p (j e) -> p j e", e=X), ps[:, LG, 0:J * X].rearrange("p (j e) -> p j e", e=X),
                                    c.br[:, :].unsqueeze(1).to_broadcast([P, J, X]), ALU.add).then_inc(logits_copied, 1)
            dve.wait_ge(logits_copied, 1)


def route(nc, c, d):
    with ExitStack() as ctx:
        (iotas, step, p_made, ranks, gates_stored, list_step, picked, listed) = semaphores(
            nc, ctx, "r_iotas", "r_step", "r_p", "r_ranks", "r_gatesst", "r_lstep", "r_picked", "r_listed")
        logits = c.arena[:, LOGITS_AT:LOGITS_AT + J * X]
        C = J * X
        at = EX_AT

        def take(n):
            nonlocal at
            at += n
            assert at <= LOGITS_AT
            return c.arena[:, at - n:at]

        same, score_, oh1, oh2, rest, total, before, tile_of = (take(C) for _ in range(8))
        top1, pick1, top2, pick2, gap, gate_sum = (take(J) for _ in range(6))
        rev, tiles, upto, offset, count = (take(X) for _ in range(5))
        tile_start = take(J)
        tile_id = take(XS_TILES)
        many = take(XS_TILES * X)
        place = take(TOPK * J)
        jx = lambda ap: ap.rearrange("p (j e) -> p j e", e=X)
        over_x = lambda ap: ap.unsqueeze(2).to_broadcast([P, J, X])
        over_j = lambda ap: ap.unsqueeze(1).to_broadcast([P, J, X])
        gates = take(TOPK * J).rearrange("p (j k) -> p j k", k=TOPK)
        gate1, gate2 = gates[:, :, 0], gates[:, :, 1]
        RING = GT
        COLS = TOPK * J
        in_row = take(RING * P).rearrange("p (q n) -> p q n", q=RING)
        in_tile = c.rel[:, 0:RING * LIST_TILES].rearrange("p (q n) -> p q n", q=RING)
        tile_no, tile_i, row_no, value = (ap[:, 0:COLS] for ap in (same, score_, rest, total))
        unused, code, token = (ap[:, COLS:COLS + LIST_TILES] for ap in (same, score_, rest))
        token_here, pad = tile_of[:, 0:J], tile_of[:, J:J + 1]
        columns = many[:, 0:LIST_TILES]
        ps = c.psum
        block = ctx.enter_context(nc.Block())

        @block.gpsimd
        def _(pool):
            ia = dict(allow_small_or_imprecise_dtypes=True)
            pool.iota(rev, [[-1, X]], base=X, channel_multiplier=0, **ia).then_inc(iotas, 1)
            pool.iota(tile_start, [[P, J]], base=0, channel_multiplier=0, **ia).then_inc(iotas, 1)
            pool.iota(tile_id, [[1, XS_TILES]], base=0, channel_multiplier=0, **ia).then_inc(iotas, 1)
            pool.wait_ge(step, 33)
            pool.iota(columns, [[1, LIST_TILES]], base=0, channel_multiplier=0, **ia).then_inc(iotas, 1)

        @block.sync
        def _(sp):
            sp.wait_ge(step, 16)
            with nc.allow_non_contiguous_dma(reason="the two gates of a token"):
                sp.dma_start(d.gates[0:TOPK * NP, :].rearrange("(j p k) n -> p j (k n)", p=P, k=TOPK), gates).then_inc(gates_stored, 16)
            for e in range(X):
                sp.dma_start(c.arena[:, W2_AT:W2_AT + W2_WORDS].rearrange("p (h e n) -> p h e n", e=X, n=IN)[:, :, e, :],
                             d.W2[e].rearrange("(h p) n -> p h n", p=P)).then_inc(c.w2_loaded, 16)
            sp.wait_ge(gates_stored, 16)

        @block.scalar
        def _(act):
            act.wait_ge(step, 12)
            nc.scalar.activation(gap, gap, ACT.Exp).then_inc(p_made, 1)

        @block.tensor
        def _(pe):
            pe.wait_ge(step, 13)
            nc.tensor.matmul(ps[:, 0, 0:C], c.tri[:, :], total, start=True, stop=True)
            nc.tensor.matmul(ps[:, 1, 0:C], c.ones[:, :], total, start=True, stop=True).then_inc(ranks, 1)

            def collect(i, first, last):
                for q in range(RING):
                    pe.wait_ge(picked, i * RING + (q + 1))
                    nc.tensor.matmul(ps[:, 2, 0:LIST_TILES], in_row[:, q, :], in_tile[:, q, :], start=first and q == 0,
                                     stop=last and q == RING - 1).then_inc(listed, 1)

            collect(0, True, False)
            with pe.Fori(1, COLS // RING - 1) as i:
                collect(i, False, False)
            collect(COLS // RING - 1, False, True)

        @block.vector
        def _(dve):
            def choose(values, top, pick, onehot, n):
                nc.vector.tensor_reduce(top, jx(values), AX.X, ALU.max).then_inc(step, 1)
                dve.wait_ge(step, n + 1)
                nc.vector.tensor_tensor(jx(same), jx(values), over_x(top), ALU.is_equal).then_inc(step, 1)
                dve.wait_ge(step, n + 2)
                nc.vector.tensor_tensor(jx(score_), jx(same), over_j(rev), ALU.mult).then_inc(step, 1)
                dve.wait_ge(step, n + 3)
                nc.vector.tensor_reduce(pick, jx(score_), AX.X, ALU.max).then_inc(step, 1)
                dve.wait_ge(step, n + 4)
                nc.vector.tensor_tensor(jx(onehot), over_j(rev), over_x(pick), ALU.is_equal).then_inc(step, 1)
                dve.wait_ge(step, n + 5)

            dve.wait_ge(iotas, 3)
            choose(logits, top1, pick1, oh1, 0)
            nc.vector.scalar_tensor_tensor(rest, oh1, -3.0e38, logits, ALU.mult, ALU.add).then_inc(step, 1)
            dve.wait_ge(step, 6)
            choose(rest, top2, pick2, oh2, 6)
            nc.vector.tensor_tensor(gap, top2, top1, ALU.subtract).then_inc(step, 1)
            nc.vector.tensor_tensor(total, oh1, oh2, ALU.add).then_inc(step, 1)
            dve.wait_ge(p_made, 1)
            nc.vector.tensor_scalar(gate_sum, gap, 1.0, None, ALU.add).then_inc(step, 1)
            dve.wait_ge(step, 14)
            nc.vector.reciprocal(gate1, gate_sum).then_inc(step, 1)
            dve.wait_ge(step, 15)
            nc.vector.tensor_tensor(gate2, gap, gate1, ALU.mult).then_inc(step, 1)
            dve.wait_ge(ranks, 1)
            for e in range(X):
                nc.vector.tensor_tensor_scan(before[:, e:C:X], c.ones[:, 0:J], ps[:, 1, e:C:X], 0.0, ALU.mult, ALU.add).then_inc(step, 1)
            dve.wait_ge(step, 24)
            nc.vector.tensor_copy(count, before[:, (J - 1) * X:C]).then_inc(step, 1)
            dve.wait_ge(step, 25)
            nc.vector.tensor_tensor(before, before, ps[:, 1, 0:C], ALU.subtract).then_inc(step, 1)
            m = tile_of.rearrange("p (e j) -> p e j", e=X)
            nc.vector.tensor_tensor(m, count.unsqueeze(2).to_broadcast([P, X, J]), tile_start.unsqueeze(1).to_broadcast([P, X, J]),
                                    ALU.is_gt).then_inc(step, 1)
            dve.wait_ge(step, 27)
            nc.vector.tensor_reduce(tiles, m, AX.X, ALU.add).then_inc(step, 1)
            dve.wait_ge(step, 28)
            nc.vector.tensor_tensor_scan(upto, c.ones[:, 0:X], tiles, 0.0, ALU.mult, ALU.add).then_inc(step, 1)
            dve.wait_ge(step, 29)
            nc.vector.tensor_tensor(offset, upto, tiles, ALU.subtract).then_inc(step, 1)
            u = many.rearrange("p (u e) -> p u e", e=X)
            nc.vector.tensor_tensor(u, tile_id.unsqueeze(2).to_broadcast([P, XS_TILES, X]), upto.unsqueeze(1).to_broadcast([P, XS_TILES, X]),
                                    ALU.is_ge).then_inc(step, 1)
            dve.wait_ge(step, 31)
            nc.vector.tensor_scalar(offset, offset, float(P), None, ALU.mult).then_inc(step, 1)
            nc.vector.tensor_reduce(tile_id, u, AX.X, ALU.add).then_inc(step, 1)
            nc.vector.tensor_tensor(before, before, ps[:, 0, 0:C], ALU.add).then_inc(step, 1)
            dve.wait_ge(step, 34)
            nc.vector.tensor_scalar(c.tile_e[:, :], tile_id[0:1, :], float(X - 1), None, ALU.min).then_inc(step, 1)
            nc.vector.tensor_tensor(jx(before), jx(before), over_j(offset), ALU.add).then_inc(step, 1)
            dve.wait_ge(step, 36)
            nc.vector.tensor_tensor(oh1, oh1, before, ALU.mult).then_inc(step, 1)
            nc.vector.tensor_tensor(oh2, oh2, before, ALU.mult).then_inc(step, 1)
            dve.wait_ge(step, 38)
            nc.vector.tensor_reduce(place[:, 0:J], jx(oh1), AX.X, ALU.add).then_inc(step, 1)
            nc.vector.tensor_reduce(place[:, J:2 * J], jx(oh2), AX.X, ALU.add).then_inc(step, 1)
            dve.wait_ge(step, 40)
            nc.vector.tensor_copy(c.place_i[:, :], place).then_inc(list_step, 1)
            nc.vector.tensor_scalar(token_here, tile_start, c.iota_p[:, :], None, ALU.add).then_inc(list_step, 1)
            nc.vector.tensor_scalar(pad, c.iota_p[:, :], float(TOPK), float(TOPK * NP + 1), ALU.mult, ALU.add).then_inc(list_step, 1)
            dve.wait_ge(list_step, 3)
            nc.vector.tensor_scalar(tile_i.bitcast(I32), c.place_i[:, :], 7, None, ALU.logical_shift_right).then_inc(list_step, 1)
            for k in range(TOPK):
                nc.vector.tensor_scalar(value[:, k * J:(k + 1) * J], token_here, float(TOPK), float(k + 1), ALU.mult, ALU.add).then_inc(list_step, 1)
            dve.wait_ge(list_step, 6)
            nc.vector.tensor_copy(tile_no, tile_i.bitcast(I32)).then_inc(list_step, 1)
            dve.wait_ge(list_step, 7)
            nc.vector.scalar_tensor_tensor(row_no, tile_no, -float(P), place, ALU.mult, ALU.add).then_inc(list_step, 1)
            dve.wait_ge(list_step, 8)
            dve.wait_ge(iotas, 4)
            dve.sem_inc(listed, RING)
            with dve.Fori(0, COLS // RING) as i:
                for part in (range(RING // 2 + 1), range(RING // 2 + 1, RING)):
                    q0, n = part[0], len(part)
                    dve.wait_ge(listed, i * RING + (q0 + n))
                    nc.vector.tensor_tensor(in_row[:, q0:q0 + n, :], c.iota_row[:, :].unsqueeze(1).to_broadcast([P, n, P]),
                                            row_no[:, ds(i * RING + q0, n)].unsqueeze(2).to_broadcast([P, n, P]), ALU.is_equal)
                    for q in part:
                        nc.vector.tensor_scalar(in_tile[:, q, :], columns, tile_no[:, ds(i * RING + q, 1)], value[:, ds(i * RING + q, 1)],
                                                ALU.is_equal, ALU.mult).then_inc(picked, 1)
            dve.wait_ge(listed, RING + COLS)
            nc.vector.tensor_scalar(unused, ps[:, 2, 0:LIST_TILES], 0.0, pad, ALU.is_equal, ALU.mult).then_inc(list_step, 1)
            dve.wait_ge(list_step, 9)
            nc.vector.scalar_tensor_tensor(code.bitcast(I32), unused, -1.0, ps[:, 2, 0:LIST_TILES], ALU.add, ALU.add).then_inc(list_step, 1)
            dve.wait_ge(list_step, 10)
            nc.vector.tensor_scalar(token.bitcast(I32), code.bitcast(I32), 1, None, ALU.logical_shift_right).then_inc(list_step, 1)
            dve.wait_ge(list_step, 11)
            nc.vector.tensor_copy(c.first_rows, token[:, 0:AHEAD].bitcast(I32)).then_inc(list_step, 1)
            for n, (ap, on) in enumerate(((token, AHEAD), (token, 0), (code, 0))):
                nc.vector.tensor_copy(c.lists[:, :, n], ap[:, on:on + MOE_TILES].bitcast(I32)).then_inc(list_step, 1)
            dve.wait_ge(list_step, 15)


def experts_of(nc, row, engine):
    _, values = nc.values_load_multi_w_load_instructions(
        row, engines=(engine,), min_val=0, max_val=X - 1, skip_runtime_bounds_check_because="route caps the table at X - 1")
    return values


def experts(nc, c, d):
    with ExitStack() as ctx:
        (x_loaded0, x_loaded1, b2_loaded, xT_made, xT_copied, up_done, pre_made, preT_made, gelu_done, down_done, sum_made, y_made, gate_done, idx_copied) = semaphores(
            nc, ctx, "e_x0", "e_x1", "e_b2", "e_xT", "e_xTc", "e_up", "e_pre", "e_preT", "e_gelu", "e_down", "e_sum", "e_y", "e_gate", "e_idx")
        gate_loaded, y_stored = semaphores(nc, ctx, "e_gat0", "e_gat1"), semaphores(nc, ctx, "e_yst0", "e_yst1")
        x_loaded = (x_loaded0, x_loaded1)
        w1 = c.arena[:, W1_AT:W1_AT + W1_WORDS]
        w2 = c.arena[:, W2_AT:W2_AT + W2_WORDS]
        b1 = c.arena[:, B1_AT:B1_AT + B1_WORDS]
        HC = HID // P
        at = EX_AT

        def take(n):
            nonlocal at
            at += n
            assert at <= EX_AT + EX_WORDS
            return c.arena[:, at - n:at]

        pre = take(HID)
        hT = take(HID)
        b2 = take(X * IN)
        xt = take(2 * IN).rearrange("p (b i) -> p b i", b=2)
        gate = take(2)
        xT = take(2 * IN).rearrange("p (b i) -> p b i", b=2)
        y = take(2 * IN).rearrange("p (b i) -> p b i", b=2)
        ps = c.psum
        UP, PRET, DOWN, XT = 0, 2, 4, 6
        PAIRS = MOE_TILES // 2
        lists = c.lists.rearrange("p u n -> p (u n)")
        block = ctx.enter_context(nc.Block())

        @block.sync
        def _(sp):
            sp.dma_start(b2, d.b2.rearrange("e n -> (e n)").partition_broadcast(P)).then_inc(b2_loaded, 16)

        @block.gpsimd
        def _(pool):
            pool.sem_inc(gate_done, 1)

            def rows_of(index, b):
                pool.indirect_dma_start(xt[:, b, :], None, d.xn[:, :], bass.IndirectOffsetOnAxis(ap=index, axis=0)).then_inc(x_loaded[b], 16)

            def pass_gate():
                nc.gpsimd.tensor_tensor(c.gate[:, :], c.ones[0:1, 0:1], c.ones[0:1, 0:1], ALU.add).then_inc(gate_done, 1)

            def turn(i, b):
                pool.wait_ge(idx_copied, i * 2 + (b + 1))
                pool.wait_ge(xT_made, i * 2 + (b + 2))
                pool.wait_ge(gate_done, i * 4 + (2 * b + 1))
                pass_gate()
                rows_of(c.idx[:, b, 0:1], 1 - b)
                pool.indirect_dma_start(gate[:, b:b + 1], None, d.gates[:, :], bass.IndirectOffsetOnAxis(ap=c.idx[:, b, 2:3], axis=0)
                                        ).then_inc(gate_loaded[b], 16)
                pool.wait_ge(y_made, i * 2 + (b + 1))
                if b:
                    pool.wait_ge(y_stored[0], i * 16 + 16)
                elif not isinstance(i, int):
                    pool.wait_ge(y_stored[1], i * 16)
                pool.wait_ge(gate_done, i * 4 + (2 * b + 2))
                pass_gate()
                pool.indirect_dma_start(d.out[:, :], bass.IndirectOffsetOnAxis(ap=c.idx[:, b, 1:2], axis=0), y[:, b, :], None,
                                        compute_op=ALU.add).then_inc(y_stored[b], 16)

            rows_of(c.first_rows[:, 0:1], 0)
            rows_of(c.first_rows[:, 1:2], 1)
            pool.wait_ge(xT_made, 1)
            rows_of(c.first_rows[:, 2:3], 0)
            turn(0, 0)
            turn(0, 1)
            with pool.Fori(1, PAIRS) as i:
                for b in range(2):
                    turn(i, b)
            for b in range(2):
                pool.wait_ge(y_stored[b], 16 * PAIRS)
                pool.wait_ge(x_loaded[b], 16 * ((MOE_TILES + AHEAD + 1 - b) // 2))

        @block.tensor
        def _(pe):
            def turn_rows(n, b):
                for m in range(KH):
                    last = nc.tensor.transpose(ps[:, XT + b, m * P:(m + 1) * P], xt[:, b, m * P:(m + 1) * P], c.ident[:, :])
                last.then_inc(xT_made, 1)

            def up(e, b):
                for n in range(HID // 512):
                    for m in range(KH):
                        last = nc.tensor.matmul(ps[:, UP + n, :], xT[:, b, m * P:(m + 1) * P], w1[:, ds(e * HID + (m * X * HID + n * 512), 512)],
                                                start=(m == 0), stop=(m == KH - 1))
                last.then_inc(up_done, 1)

            pe.wait_ge(x_loaded[0], 16)
            turn_rows(0, 0)
            pe.wait_ge(x_loaded[1], 16)
            turn_rows(1, 1)
            pe.wait_ge(c.w1_loaded, 16 * (X + 1))
            pe.wait_ge(xT_copied, 1)
            up(pe.value_load(c.tile_e[0:1, 0:1], min_val=0, max_val=X - 1), 0)
            pe.wait_ge(c.w2_loaded, 16 * X)
            with pe.Fori(0, PAIRS) as i:
                for b in range(2):
                    e_now, e_next = experts_of(nc, c.tile_e[0:1, ds(i * 2 + b, 2)], mybir.EngineType.PE)
                    pe.wait_ge(pre_made, i * 2 + (b + 1))
                    for h in range(HC):
                        last = nc.tensor.transpose(ps[:, PRET + h // 4, h % 4 * P:(h % 4 + 1) * P], pre[:, h * P:(h + 1) * P], c.ident[:, :])
                        if h % 4 == 3:
                            last.then_inc(preT_made, 1)
                    pe.wait_ge(xT_copied, i * 2 + (b + 2))
                    up(e_next, 1 - b)
                    pe.wait_ge(x_loaded[b], i * 16 + 32)
                    pe.wait_ge(xT_copied, i * 2 + (b + 1))
                    turn_rows(0, b)
                    pe.wait_ge(gelu_done, i * 4 + (2 * b + 2))
                    pe.wait_ge(y_made, i * 2 + (b + 1) - 1) if b else None
                    for h in range(HC):
                        last = nc.tensor.matmul(ps[:, DOWN + b, 0:IN], hT[:, h * P:(h + 1) * P], w2[:, ds(e_now * IN + h * X * IN, IN)],
                                                start=(h == 0), stop=(h == HC - 1))
                    last.then_inc(down_done, 1)

        @block.scalar
        def _(act):
            with act.Fori(0, PAIRS) as i:
                for b in range(2):
                    for n in range(2):
                        act.wait_ge(preT_made, i * 4 + (2 * b + n + 1))
                        nc.scalar.activation(hT[:, n * 512:(n + 1) * 512], ps[:, PRET + n, :], ACT.Gelu).then_inc(gelu_done, 1)

        @block.vector
        def _(dve):
            def bias(n, e):
                for q in range(2):
                    part = slice(q * 512, (q + 1) * 512)
                    last = nc.vector.tensor_tensor(pre[:, part], ps[:, UP + q, :], b1[:, ds(e * HID + q * 512, 512)], ALU.add)
                last.then_inc(pre_made, 1)

            def scale(b, e):
                for m in range(KH):
                    last = nc.vector.tensor_scalar(xT[:, b, m * P:(m + 1) * P], ps[:, XT + b, m * P:(m + 1) * P], c.ln_g[:, m, ds(e, 1)],
                                                   c.ln_b[:, m, ds(e, 1)], ALU.mult, ALU.add)
                last.then_inc(xT_copied, 1)

            for b in range(2):
                dve.wait_ge(xT_made, b + 1)
                scale(b, dve.value_load(c.tile_e[0:1, b:b + 1], min_val=0, max_val=X - 1))
            dve.wait_ge(b2_loaded, 16)
            dve.wait_ge(up_done, 1)
            bias(0, dve.value_load(c.tile_e[0:1, 0:1], min_val=0, max_val=X - 1))
            with dve.Fori(0, PAIRS) as i:
                for b in range(2):
                    dve.wait_ge(gate_done, i * 4 + (2 * b + 1))
                    dve.wait_ge(xT_made, i * 2 + (b + 2))
                    nc.vector.tensor_copy(c.idx[:, b, 0:3], lists[:, ds((i * 2 + b) * 3, 3)]).then_inc(idx_copied, 1)
                    e_now, e_next, e_after = experts_of(nc, c.tile_e[0:1, ds(i * 2 + b, 3)], mybir.EngineType.DVE)
                    dve.wait_ge(up_done, i * 2 + (b + 2))
                    bias(0, e_next)
                    dve.wait_ge(xT_made, i * 2 + (b + 3))
                    scale(b, e_after)
                    dve.wait_ge(down_done, i * 2 + (b + 1))
                    dve.wait_ge(gate_loaded[b], i * 16 + 16)
                    nc.vector.tensor_tensor(y[:, b, :], ps[:, DOWN + b, 0:IN], b2[:, ds(e_now * IN, IN)], ALU.add).then_inc(sum_made, 1)
                    dve.wait_ge(sum_made, i * 2 + (b + 1))
                    nc.vector.tensor_scalar(y[:, b, :], y[:, b, :], gate[:, b:b + 1], None, ALU.mult).then_inc(y_made, 1)


STAGES = [prepare, score, softmax, aggregate, attend, route, experts]


def program(nc, d):
    c = Chip()
    with ExitStack() as ctx:
        def sb(name, shape, dt=F32):
            return ctx.enter_context(nc.sbuf_tensor(name, shape, dt))

        c.arena = sb("arena", [P, ARENA])
        c.psum = ctx.enter_context(nc.psum_tensor("psum", [P, 8, 512], F32))
        c.iota_row = sb("iota_row", [P, P])
        c.iota_p = sb("iota_p", [P, 1])
        c.ident = sb("ident", [P, P])
        c.tri = sb("tri", [P, P])
        c.ones = sb("ones", [P, P])
        c.eps = sb("eps", [P, 1])
        c.ew = sb("ew", [P, HW])
        c.src = sb("src", [P, SLOTS], I32)
        c.rel = sb("rel", [P, SLOTS])
        c.src_tiles = c.arena[:, SRC_TILES_AT:SRC_TILES_AT + T + R].bitcast(I32)
        c.slot_t = c.arena[0:1, SLOT_T_AT:SLOT_T_AT + SLOTS].bitcast(I32)
        c.slot_j = sb("slot_j", [1, SG * P], I32)
        c.gnn_bias = sb("gnn_bias", [P, HD])
        c.wr = sb("wr", [P, KH, X])
        c.br = sb("br", [P, X])
        c.ln_g = sb("ln_g", [P, KH, X])
        c.ln_b = sb("ln_b", [P, KH, X])
        c.idx = sb("idx", [P, 2, R], I32)
        c.gate = sb("gate", [1, 1])
        c.place_i = sb("place_i", [P, TOPK * J], I32)
        c.lists = c.src[:, 0:3 * MOE_TILES].rearrange("p (u n) -> p u n", n=3)
        c.first_rows = c.src[:, 3 * MOE_TILES:3 * MOE_TILES + AHEAD]
        c.tile_e = sb("tile_e", [1, XS_TILES], I32)
        (c.consts_ready, c.w1_loaded, c.w2_loaded) = semaphores(nc, ctx, "consts_ready", "w1_loaded", "w2_loaded")
        d.h_tab = nc.dram_tensor("h_tab", [NP, HW], F32)
        d.s_tab = nc.dram_tensor("s_tab", [NP, H], F32)
        d.slot_t = nc.dram_tensor("slot_t_list", [SG * P], I32)
        d.slot_j = nc.dram_tensor("slot_j_list", [SG * P], I32)
        d.rel = nc.dram_tensor("rel_list", [SG * P, P], F32)
        d.ea_slots = nc.dram_tensor("ea_slots", [EF + 1, SG * P, P], F32)
        d.xn = nc.dram_tensor("xn", [NP + P, IN], F32)
        d.gates = nc.dram_tensor("gates", [TOPK * (NP + P), 1], F32)
        d.ends = nc.dram_tensor("ends", [P, CH * 4], F32).ap()
        d.joined = nc.dram_tensor("joined", [P, CH * 2], F32).ap()
        for stage in STAGES:
            stage(nc, c, d)


def kernel(**inputs):
    import numpy as np
    import concourse.bacc as bacc
    from concourse.bass_utils import run_bass_kernel_spmd as run

    f = np.float32
    x = np.concatenate([np.asarray(inputs["x"]), np.zeros((NP - N, IN), f)])
    src = np.concatenate([np.asarray(inputs["src"]), np.zeros(EP - E, np.int32)])
    dst = np.concatenate([np.asarray(inputs["dst"]), np.full(EP - E, NP - 1, np.int32)])
    ea = np.zeros((EF + 1, EP), f)
    ea[:EF, :E] = np.asarray(inputs["edge_attr_3"]).T
    ea[EF] = 1.0
    W = np.ascontiguousarray(inputs["L0_gnn_W"])
    a_bd = np.zeros((H, D, 2, H), f)
    for h in range(H):
        a_bd[h, :, 0, h] = inputs["L0_gnn_a_src"][h]
        a_bd[h, :, 1, h] = inputs["L0_gnn_a_dst"][h]
    ew = np.zeros((EF + 1, H, D + 1), f)
    ew[:EF, :, :D] = np.asarray(inputs["L0_gnn_edge_W"]).T.reshape(EF, H, D)
    ew[EF, :, :D] = np.asarray(inputs["L0_gnn_edge_b"]).reshape(H, D)
    ew[EF, :, D] = 1.0
    arrays = {
        "x": x, "src_rows": src.reshape(T, P), "src_cols": np.concatenate([src.reshape(T, P).T, np.zeros((P, R), np.int32)], axis=1), "dst_rows": dst.reshape(T, P),
        "ea_rows": ea.reshape(EF + 1, T, P).swapaxes(0, 1).reshape(T, (EF + 1) * P), "W": W, "WT": W.T, "a_bd": a_bd.reshape(HD, 2 * H), "ew": ew.reshape(EF + 1, HW),
        "gnn_bias": inputs["L0_gnn_bias"], "Wr": inputs["L0_ffn_Wr"], "br": inputs["L0_ffn_br"],
        "ln_gT": np.asarray(inputs["L0_ffn_ln_g"]).T, "ln_bT": np.asarray(inputs["L0_ffn_ln_b"]).T,
        "W1": inputs["L0_ffn_W1"], "b1": inputs["L0_ffn_b1"], "W2": inputs["L0_ffn_W2"], "b2": inputs["L0_ffn_b2"],
    }
    arrays = {k: np.ascontiguousarray(v) for k, v in arrays.items()}

    class Dram:
        pass

    nc = bacc.Bacc("TRN2", target_bir_lowering=False, num_devices=1)
    d = Dram()
    for name, a in arrays.items():
        d.__dict__[name] = nc.dram_tensor(f"in_{name}", a.shape, mybir.dt.from_np(a.dtype), kind="ExternalInput").ap()
    d.out = nc.dram_tensor("out_rows", (NP + P, IN), F32, kind="ExternalOutput").ap()
    program(nc, d)
    r = run(nc, [{f"in_{k}": v for k, v in arrays.items()}], core_ids=[0])
    return r.results[0]["out_rows"][:N]
```
